# Optimizing a Trainium2 kernel written in Bass

```python
import numpy as np
import jax
import jax.numpy as jnp

def _softmax(x, axis=-1):
    return jax.nn.softmax(x, axis=axis)

def _gelu(x):
    return jax.nn.gelu(x, approximate=True)

def _silu(x):
    return jax.nn.silu(x)

def _sigmoid(x):
    return jax.nn.sigmoid(x)

def _layernorm(x, axis=-1, eps=1e-05):
    m = jnp.mean(x, axis=axis, keepdims=True)
    v = jnp.var(x, axis=axis, keepdims=True)
    return (x - m) / jnp.sqrt(v + eps)

def _scatter_add(tgt, idx, src, axis=0):
    return tgt.at[idx].add(src)

def _segment_sum(src, seg, n):
    return jax.ops.segment_sum(src, seg, n)
kernel_name = 'mk_adaln_d2_jaxref_r8_8f2392'

def setup_inputs(seed: int=0):
    np.random.seed(seed)
    _w = jnp.asarray

    def _L0_attn_setup():
        import math
        import jax, jax.numpy as jnp
        import numpy as np
        EMBED = 128
        HEADS = 16
        FACTOR = 3
        key = jax.random.key(seed)
        ks = jax.random.split(key, 9)
        B, T, E = (8, 512, EMBED)
        s = 1.0 / np.sqrt(E)
        inp = {'hidden_states': jax.random.normal(ks[0], (B, T, E), jnp.float32)}
        for i, n in enumerate(['q', 'k', 'v', 'o']):
            inp[f'W{n}'] = jax.random.normal(ks[1 + i], (E, E), jnp.float32) * s
            inp[f'b{n}'] = jax.random.normal(ks[5 + i], (E,), jnp.float32) * 0.01
        return inp
    _L0_attn_in = _L0_attn_setup()

    def _L0_ffn_setup():
        import jax, jax.numpy as jnp
        import numpy as np
        B, T, D, H, E = (4, 256, 128, 512, 8)
        key = jax.random.key(seed)
        ks = jax.random.split(key, 7)
        x = jax.random.normal(ks[0], (B, T, D), dtype=jnp.float32)
        Wg = jax.random.normal(ks[1], (D, E), dtype=jnp.float32) / np.sqrt(D)
        bg = jax.random.normal(ks[2], (E,), dtype=jnp.float32) * 0.01
        W1 = jax.random.normal(ks[3], (E, D, H), dtype=jnp.float32) / np.sqrt(D)
        b1 = jax.random.normal(ks[4], (E, H), dtype=jnp.float32) * 0.01
        W2 = jax.random.normal(ks[5], (E, H, D), dtype=jnp.float32) / np.sqrt(H)
        b2 = jax.random.normal(ks[6], (E, D), dtype=jnp.float32) * 0.01
        return {'x': x, 'Wg': Wg, 'bg': bg, 'W1': W1, 'b1': b1, 'W2': W2, 'b2': b2}
    _L0_ffn_in = _L0_ffn_setup()
    _L0_c = _w((lambda *s: np.random.randn(*s).astype(np.float32) * 0.05)(1, 128))
    _L0_wmod = _w((lambda *s: np.random.randn(*s).astype(np.float32) * 0.05)(128, 6 * 128) * 128 ** (-0.5))

    def _L1_attn_setup():
        import jax, jax.numpy as jnp
        import numpy as np
        N_EMBD = 128
        N_HEAD = 8
        HEAD_DIM = N_EMBD // N_HEAD
        EPS = 1e-06

        def _lrpe(xh, theta, n):
            idx = jnp.arange(n, dtype=xh.dtype).reshape(1, n, 1)
            th = theta * idx
            th = th[None]
            return jnp.concatenate([xh * jnp.cos(th), xh * jnp.sin(th)], axis=-1)

        def _srmsnorm(y):
            ms = jnp.mean(jnp.square(y), axis=-1, keepdims=True)
            return y * jax.lax.rsqrt(ms + EPS)
        key = jax.random.key(seed)
        ks = jax.random.split(key, 8)
        b, n = (2, 256)
        x = jax.random.normal(ks[0], (b, n, N_EMBD), dtype=jnp.float32)
        slope_rate = -jax.random.uniform(ks[1], (N_HEAD, 1, 1), dtype=jnp.float32)
        s = 0.02
        qkvu_w = jax.random.normal(ks[2], (4 * N_EMBD, N_EMBD), dtype=jnp.float32) * s
        qkvu_b = jnp.zeros((4 * N_EMBD,), dtype=jnp.float32)
        out_w = jax.random.normal(ks[3], (N_EMBD, N_EMBD), dtype=jnp.float32) * s
        out_b = jnp.zeros((N_EMBD,), dtype=jnp.float32)
        d = N_EMBD
        theta = (10000.0 ** (-2.0 / d * jnp.arange(d, dtype=jnp.float32))).reshape(N_HEAD, 1, HEAD_DIM)
        return {'x': x, 'slope_rate': slope_rate, 'qkvu_w': qkvu_w, 'qkvu_b': qkvu_b, 'out_w': out_w, 'out_b': out_b, 'theta': theta}
    _L1_attn_in = _L1_attn_setup()

    def _L1_ffn_setup():
        import jax, jax.numpy as jnp
        import numpy as np
        B, L, D = (2, 256, 128)
        E = 15
        H = D * 1
        K = 3
        T = 1.0
        key = jax.random.key(seed)
        ks = jax.random.split(key, 12)
        s = 0.02
        return {'x': jax.random.normal(ks[0], (B, L, D), dtype=jnp.float32), 'router_W': jax.random.normal(ks[1], (D, E), dtype=jnp.float32) * s, 'router_b': jnp.zeros((E,), dtype=jnp.float32), 'sW1': jax.random.normal(ks[2], (D, H), dtype=jnp.float32) * s, 'sb1': jnp.zeros((H,), dtype=jnp.float32), 'sW2': jax.random.normal(ks[3], (H, D), dtype=jnp.float32) * s, 'sb2': jnp.zeros((D,), dtype=jnp.float32), 'eW1': jax.random.normal(ks[4], (E, D, H), dtype=jnp.float32) * s, 'eb1': jnp.zeros((E, H), dtype=jnp.float32), 'eW2': jax.random.normal(ks[5], (E, H, D), dtype=jnp.float32) * s, 'eb2': jnp.zeros((E, D), dtype=jnp.float32)}
    _L1_ffn_in = _L1_ffn_setup()
    _L1_c = _w((lambda *s: np.random.randn(*s).astype(np.float32) * 0.05)(1, 128))
    _L1_wmod = _w((lambda *s: np.random.randn(*s).astype(np.float32) * 0.05)(128, 6 * 128) * 128 ** (-0.5))
    _d = {'L0_attn_hidden_states': _L0_attn_in['hidden_states'], 'L0_attn_Wq': _L0_attn_in['Wq'], 'L0_attn_bq': _L0_attn_in['bq'], 'L0_attn_Wk': _L0_attn_in['Wk'], 'L0_attn_bk': _L0_attn_in['bk'], 'L0_attn_Wv': _L0_attn_in['Wv'], 'L0_attn_bv': _L0_attn_in['bv'], 'L0_attn_Wo': _L0_attn_in['Wo'], 'L0_attn_bo': _L0_attn_in['bo'], 'L0_ffn_Wg': _L0_ffn_in['Wg'], 'L0_ffn_bg': _L0_ffn_in['bg'], 'L0_ffn_W1': _L0_ffn_in['W1'], 'L0_ffn_b1': _L0_ffn_in['b1'], 'L0_ffn_W2': _L0_ffn_in['W2'], 'L0_ffn_b2': _L0_ffn_in['b2'], 'L0_c': _L0_c, 'L0_wmod': _L0_wmod, 'L1_attn_slope_rate': _L1_attn_in['slope_rate'], 'L1_attn_qkvu_w': _L1_attn_in['qkvu_w'], 'L1_attn_qkvu_b': _L1_attn_in['qkvu_b'], 'L1_attn_out_w': _L1_attn_in['out_w'], 'L1_attn_out_b': _L1_attn_in['out_b'], 'L1_attn_theta': _L1_attn_in['theta'], 'L1_ffn_router_W': _L1_ffn_in['router_W'], 'L1_ffn_router_b': _L1_ffn_in['router_b'], 'L1_ffn_sW1': _L1_ffn_in['sW1'], 'L1_ffn_sb1': _L1_ffn_in['sb1'], 'L1_ffn_sW2': _L1_ffn_in['sW2'], 'L1_ffn_sb2': _L1_ffn_in['sb2'], 'L1_ffn_eW1': _L1_ffn_in['eW1'], 'L1_ffn_eb1': _L1_ffn_in['eb1'], 'L1_ffn_eW2': _L1_ffn_in['eW2'], 'L1_ffn_eb2': _L1_ffn_in['eb2'], 'L1_c': _L1_c, 'L1_wmod': _L1_wmod}
    _x0 = _d['L0_attn_hidden_states']
    _d['L0_attn_hidden_states'] = jax.random.normal(jax.random.fold_in(jax.random.key(seed), 1), (1, 2048, 128), dtype=_x0.dtype)
    del _x0
    return _d

def reference(L0_attn_hidden_states, L0_attn_Wq, L0_attn_bq, L0_attn_Wk, L0_attn_bk, L0_attn_Wv, L0_attn_bv, L0_attn_Wo, L0_attn_bo, L0_ffn_Wg, L0_ffn_bg, L0_ffn_W1, L0_ffn_b1, L0_ffn_W2, L0_ffn_b2, L0_c, L0_wmod, L1_attn_slope_rate, L1_attn_qkvu_w, L1_attn_qkvu_b, L1_attn_out_w, L1_attn_out_b, L1_attn_theta, L1_ffn_router_W, L1_ffn_router_b, L1_ffn_sW1, L1_ffn_sb1, L1_ffn_sW2, L1_ffn_sb2, L1_ffn_eW1, L1_ffn_eb1, L1_ffn_eW2, L1_ffn_eb2, L1_c, L1_wmod):

    def _L0_attn_ref(hidden_states, Wq, bq, Wk, bk, Wv, bv, Wo, bo):
        import math
        import jax, jax.numpy as jnp
        import numpy as np
        EMBED = 128
        HEADS = 16
        FACTOR = 3
        B, T, E = hidden_states.shape
        H = HEADS
        D = E // H

        def shape(x):
            return x.reshape(B, T, H, D).transpose(0, 2, 1, 3).reshape(B * H, T, D)
        q = shape(hidden_states @ Wq + bq)
        k = shape(hidden_states @ Wk + bk)
        v = shape(hidden_states @ Wv + bv)
        qf = jnp.fft.rfft(q, axis=1)
        kf = jnp.fft.rfft(k, axis=1)
        attn_weights = jnp.fft.irfft(qf * jnp.conj(kf), n=T, axis=1)
        mean_ac = attn_weights.reshape(B, H, T, D).mean(axis=(1, 3))
        top_k = int(FACTOR * math.log(T))
        top_vals, top_idx = jax.lax.top_k(mean_ac, top_k)
        BN = B * H
        bidx = jnp.arange(BN) % B
        w_flat = top_vals[bidx]
        d_flat = top_idx[bidx]
        t = jnp.arange(T)

        def body(acc, kd):
            d_k, w_k = kd
            idx = (t[None, :] + d_k[:, None]) % T
            rolled = jnp.take_along_axis(v, idx[:, :, None], axis=1)
            return (acc + w_k[:, None, None] * rolled, None)
        agg, _ = jax.lax.scan(body, jnp.zeros_like(v), (d_flat.T, w_flat.T))
        out = agg.reshape(B, H, T, D).transpose(0, 2, 1, 3).reshape(B, T, E)
        return out @ Wo + bo

    def _L0_ffn_ref(x, Wg, bg, W1, b1, W2, b2):
        import jax, jax.numpy as jnp
        import numpy as np
        B, T, D, H, E = (4, 256, 128, 512, 8)
        gate_scores = x @ Wg + bg
        top1 = jnp.argmax(gate_scores, axis=-1)
        onehot = jax.nn.one_hot(top1, Wg.shape[-1], dtype=x.dtype)
        h = jax.nn.relu(jnp.einsum('btd,edh->beth', x, W1) + b1[None, :, None, :])
        y = jnp.einsum('beth,ehd->betd', h, W2) + b2[None, :, None, :]
        out = jnp.einsum('betd,bte->btd', y, onehot)
        return out

    def _L1_attn_ref(x, slope_rate, qkvu_w, qkvu_b, out_w, out_b, theta):
        import jax, jax.numpy as jnp
        import numpy as np
        N_EMBD = 128
        N_HEAD = 8
        HEAD_DIM = N_EMBD // N_HEAD
        EPS = 1e-06

        def _lrpe(xh, theta, n):
            idx = jnp.arange(n, dtype=xh.dtype).reshape(1, n, 1)
            th = theta * idx
            th = th[None]
            return jnp.concatenate([xh * jnp.cos(th), xh * jnp.sin(th)], axis=-1)

        def _srmsnorm(y):
            ms = jnp.mean(jnp.square(y), axis=-1, keepdims=True)
            return y * jax.lax.rsqrt(ms + EPS)
        b, n, hd = x.shape
        h = N_HEAD
        qkvu = x @ qkvu_w.T + qkvu_b
        q, k, v, u = jnp.split(qkvu, 4, axis=-1)

        def to_heads(t):
            return t.reshape(b, n, h, hd // h).transpose(0, 2, 1, 3)
        q, k, v = (to_heads(q), to_heads(k), to_heads(v))
        q = jax.nn.silu(q)
        k = jax.nn.silu(k)
        q = _lrpe(q, theta, n)
        k = _lrpe(k, theta, n)
        tril = jnp.tril(jnp.ones((n, n), dtype=x.dtype))
        mask = jnp.exp(slope_rate * tril)
        energy = jnp.einsum('bhne,bhme->bhnm', q, k) * mask[None]
        out = jnp.einsum('bhnm,bhmd->bhnd', energy, v)
        out = out.transpose(0, 2, 1, 3).reshape(b, n, hd)
        out = _srmsnorm(out)
        out = u * out
        out = out @ out_w.T + out_b
        return out

    def _L1_ffn_ref(x, router_W, router_b, sW1, sb1, sW2, sb2, eW1, eb1, eW2, eb2):
        import jax, jax.numpy as jnp
        import numpy as np
        B, L, D = (2, 256, 128)
        E = 15
        H = D * 1
        K = 3
        T = 1.0
        b, l, d = x.shape
        n = b * l
        xt = x.reshape(n, d)
        shared = jax.nn.relu(xt @ sW1 + sb1) @ sW2 + sb2
        logits = xt @ router_W + router_b
        probs = jax.nn.softmax(logits / T, axis=-1)
        top_p, top_i = jax.lax.top_k(probs, K)
        cw = jnp.zeros((n, E), dtype=probs.dtype)
        cw = cw.at[jnp.arange(n)[:, None], top_i].set(top_p)
        h = jax.nn.relu(jnp.einsum('nd,edh->neh', xt, eW1) + eb1)
        ye = jnp.einsum('neh,ehd->ned', h, eW2) + eb2
        routed = jnp.einsum('ned,ne->nd', ye, cw)
        return (shared + routed).reshape(b, l, d)
    x = L0_attn_hidden_states
    mod = (_silu(L0_c) @ L0_wmod).reshape(L0_c.shape[0], 6, 1, -1)
    sa, ca, ga, sb, cb, gb = (mod[:, 0], mod[:, 1], mod[:, 2], mod[:, 3], mod[:, 4], mod[:, 5])
    ga = (2 * (ga >= 0) - 1) * jnp.maximum(jnp.abs(ga), 0.25)
    gb = (2 * (gb >= 0) - 1) * jnp.maximum(jnp.abs(gb), 0.25)
    h = _layernorm(x, axis=-1) * (1 + ca) + sa
    x = x + ga * _L0_attn_ref(h, L0_attn_Wq, L0_attn_bq, L0_attn_Wk, L0_attn_bk, L0_attn_Wv, L0_attn_bv, L0_attn_Wo, L0_attn_bo)
    h = _layernorm(x, axis=-1) * (1 + cb) + sb
    x = x + gb * _L0_ffn_ref(h, L0_ffn_Wg, L0_ffn_bg, L0_ffn_W1, L0_ffn_b1, L0_ffn_W2, L0_ffn_b2)
    mod = (_silu(L1_c) @ L1_wmod).reshape(L1_c.shape[0], 6, 1, -1)
    sa, ca, ga, sb, cb, gb = (mod[:, 0], mod[:, 1], mod[:, 2], mod[:, 3], mod[:, 4], mod[:, 5])
    ga = (2 * (ga >= 0) - 1) * jnp.maximum(jnp.abs(ga), 0.25)
    gb = (2 * (gb >= 0) - 1) * jnp.maximum(jnp.abs(gb), 0.25)
    h = _layernorm(x, axis=-1) * (1 + ca) + sa
    x = x + ga * _L1_attn_ref(h, L1_attn_slope_rate, L1_attn_qkvu_w, L1_attn_qkvu_b, L1_attn_out_w, L1_attn_out_b, L1_attn_theta)
    h = _layernorm(x, axis=-1) * (1 + cb) + sb
    x = x + gb * _L1_ffn_ref(h, L1_ffn_router_W, L1_ffn_router_b, L1_ffn_sW1, L1_ffn_sb1, L1_ffn_sW2, L1_ffn_sb2, L1_ffn_eW1, L1_ffn_eb1, L1_ffn_eW2, L1_ffn_eb2)
    return x

_drawn_inputs = setup_inputs


def setup_inputs(seed=0):
    import zlib

    import numpy as np

    out = dict(_drawn_inputs(seed))
    spreads = {'L1_attn_qkvu_b': (0.0, 0.8),
     'L1_attn_out_b': (0.0, 2.0),
     'L1_ffn_router_b': (0.0, 2.0),
     'L1_ffn_sb1': (0.0, 2.0),
     'L1_ffn_sb2': (0.0, 2.0),
     'L1_ffn_eb1': (0.0, 2.0),
     'L1_ffn_eb2': (0.0, 2.0)}
    factors = {'L0_attn_bq': 8.0,
     'L0_attn_bk': 8.0,
     'L0_attn_bo': 29.479,
     'L0_ffn_Wg': 4.344,
     'L0_ffn_bg': 8.0,
     'L0_ffn_W1': 4.941,
     'L0_ffn_b1': 64.0,
     'L0_ffn_W2': 4.085,
     'L0_ffn_b2': 200.0,
     'L1_attn_slope_rate': 8.0,
     'L1_attn_qkvu_w': 8.0,
     'L1_attn_out_w': 8.0,
     'L1_attn_theta': 8.0,
     'L1_ffn_router_W': 8.0,
     'L1_ffn_sW1': 8.0,
     'L1_ffn_sW2': 8.0,
     'L1_ffn_eW1': 8.0,
     'L1_ffn_eW2': 8.0,
     'L1_c': 8.0,
     'L1_wmod': 8.0}
    for name, (base, spread) in spreads.items():
        noise = np.random.default_rng([zlib.crc32(name.encode()), seed]).standard_normal(out[name].shape)
        drawn = base * np.exp(spread * noise) if base else spread * noise
        out[name] = jnp.asarray(drawn.astype(out[name].dtype))
    for name, factor in factors.items():
        out[name] = (out[name] * factor).astype(out[name].dtype)
    return out
```

```python
from contextlib import ExitStack

import numpy as np
import concourse.bass as bass
from concourse import mybir

F32 = mybir.dt.float32
I32 = mybir.dt.int32
ALU = mybir.AluOpType
ACT = mybir.ActivationFunctionType
AX = mybir.AxisListType

P = 128
C = 128
T = 2048
J = T // P
NS = P // 2
NG = NS // 4
TOPK = int(3 * np.log(T))
EPS_LN = 1e-5
NEG = -3.0e38
E0, H0 = 8, 512
HC = H0 // P
NB0 = T // P + E0 - 1
HEADS, HD = 8, 16
E1, TOP1 = 15, 3
EPS_RMS = 1e-6
TWO_PI = [6.28125, float(np.float32(np.round((2 * np.pi - 6.28125) * 2**20) / 2**20))]
TWO_PI.append(float(np.float32(2 * np.pi - TWO_PI[0] - TWO_PI[1])))
INV_2PI = float(np.float32(0.5 / np.pi))
ROUND = 1.5 * 2.0**23
PI_IN = 3.1415925


class Chain:

    def __init__(self, eng, sem):
        self.eng, self.sem, self.n = eng, sem, 0

    def __call__(self, ins):
        self.n += 1
        ins.then_inc(self.sem, 1)
        self.eng.wait_ge(self.sem, self.n)


def shape_constants():
    p, b = np.arange(P), np.arange(NS)
    ang = 2 * np.pi * np.outer(p, b) / P
    nyq = np.cos(np.pi * p)
    dft = np.zeros((P, NS, 2))
    dft[:, :, 0], dft[:, :, 1] = np.cos(ang), -np.sin(ang)
    dft[:, 0, 1] = nyq
    idft = np.zeros((NS, 2, P))
    idft[:, 0], idft[:, 1] = 2 * np.cos(ang.T) / P, -2 * np.sin(ang.T) / P
    idft[0, 0], idft[0, 1] = 1 / P, nyq / P
    diag = np.zeros((4, 2, J, 2, 4, 3, 32))
    toep = np.zeros((3, 32, 2, 4, 4, 2, J))
    for a in range(J):
        for c in range(J):
            for r1, r2, kind, v in ((0, 0, 0, 1), (1, 1, 1, 1), (1, 0, 2, 1), (0, 1, 2, -1)):
                diag[c % 4, r1, a, r2, c // 4, kind, a - c + 16] = v
                toep[kind, a - c + 16, r2, c // 4, c % 4, r1, a] = 1 if kind < 2 else -v
    corr = np.zeros((NS, 2, 3, P))
    for half, d in ((0, p + 1), (1, p)):
        a2 = 2 * np.pi * np.outer(b, d) / P
        corr[:, half, 0] = corr[:, half, 1] = 2 * np.cos(a2)
        corr[:, half, 2] = -2 * np.sin(a2)
        corr[0, half, 0], corr[0, half, 1], corr[0, half, 2] = 1, np.cos(np.pi * d), 0
    corr /= P * C
    gdft = np.zeros((P, 3, NS))
    gdft[:, 0] = gdft[:, 1] = np.cos(ang)
    gdft[:, 2] = np.sin(ang)
    gdft[:, 1, 0] = nyq
    ident = np.eye(P)
    before = np.triu(np.ones((P, P)), 1)
    prev = np.roll(np.eye(P), 1, axis=1)
    last1 = np.tile(float(E1) - np.arange(E1), (P, 1))
    blk16 = np.repeat(np.eye(J), 24, axis=1)
    causal = np.triu(np.ones((P, P)))
    head = np.repeat(np.repeat(np.eye(4), 32, axis=0), HD, axis=1)
    headcol = np.repeat(np.eye(4), 32, axis=0)
    phase = np.tile(np.repeat([[np.pi / 2, 0.25], [0, 0]], HD, axis=0), (4, 1))
    last = np.tile(8.0 - np.arange(8), (P, 1))
    steps = np.tile(128.0 * np.arange(J), (P, 1))
    pidx = np.arange(P, dtype=float)[:, None]
    eidx = np.tile(np.arange(E0, dtype=float), (P, 1))
    parts = dict(ident=ident, dft=dft.reshape(P, P), idft=idft.reshape(P, P), corr=corr.reshape(NS, -1),
                 diag=diag.reshape(P, -1), before=before, prev=prev, blk16=blk16, gdft=gdft.reshape(P, -1),
                 toep=toep.reshape(96, -1), causal=causal, head=head, headcol=headcol, phase=phase,
                 last=last, last1=last1, steps=steps, pidx=pidx, eidx=eidx)
    first = ("ident", "dft")
    cols, at = {}, 0
    for n in (*first, *(k for k in parts if k not in first)):
        cols[n] = (at, parts[n].shape)
        at += parts[n].shape[1]
    table = np.zeros((P, at), np.float32)
    for n, (a, (r, w)) in cols.items():
        table[:r, a:a + w] = parts[n]
    return table, cols


TABLE, COLS = shape_constants()
NFIRST = COLS["dft"][0] + P

ROW_C0, ROW_C1, ROW_EB1, ROW_SB1 = 0, 1, 2, 2 + E1
ROW_QB = ROW_SB1 + 1
ROW_KB = ROW_QB + 2
ROW_TH = ROW_KB + 2
NROWS = ROW_TH + 2


def build(nc, a, out):
    ctx = ExitStack()
    with ctx:
        def sb(name, shape, dt=F32):
            return ctx.enter_context(nc.sbuf_tensor(name, shape, dt))

        def sem(name):
            return ctx.enter_context(nc.semaphore(name))

        tab = sb("tab", [P, TABLE.shape[1]])

        def tb(name):
            at, (r, w) = COLS[name]
            return tab[0:r, at:at + w]

        ident, dft, idft, before, prev = (tb(n) for n in ("ident", "dft", "idft", "before", "prev"))
        rows = sb("rows", [NROWS, C])
        cols = sb("cols", [P, NROWS])
        wmod = sb("wmod", [P, 2, 6 * C])
        silu_c = sb("silu_c", [P, 2])
        silu_cb = sb("silu_cb", [P, 2, P])
        ones = sb("ones", [P, P])
        modc = sb("modc", [P, 2, 4])
        gate = sb("gate", [P, 2, 2, C])
        space_d = sb("space_d", [P, T])
        gsign, gneg, gmag = (space_d[:, 512 * k:512 * k + 512].rearrange("p (l k c) -> p l k c", l=2, k=2) for k in range(3))
        x = sb("x", [P, J, C])
        z = sb("z", [P, J, C])
        stats = sb("stats", [P, J, 6])
        mv = sb("mv", [P, J, 2])
        var_eps = sb("var_eps", [P, J])
        std = sb("std", [P, J])
        rstd = sb("rstd", [P, J])
        hT = sb("hT", [P, P, J])
        hTf = hT[:, :, :].rearrange("c m j -> c (m j)")
        wqkvo = sb("wqkvo", [P, 4, C])
        brow = sb("brow", [1, 3, C])
        bo_b = sb("bo_b", [P, C])
        ind = sb("ind", [1, P])
        sa128 = sb("sa128", [P, 1])
        space_a = sb("space_a", [P, 4 * T])
        qT = space_a[:, 0:T]
        kT = space_a[:, T:2 * T]
        v0 = space_a[:, 2 * T:3 * T].rearrange("p (g c) -> p g c", c=C)
        prod = sb("prod", [P, 8, NS])
        lag_f = sb("lag_f", [NS, 96])
        lag = sb("lag", [P, J])
        lagT = sb("lagT", [J, P])
        lagW = sb("lagW", [J, P])
        lagX = sb("lagX", [J, P])
        cand = sb("cand", [J, 24])
        cand_d = sb("cand_d", [J, J, 24])
        space_c = sb("space_c", [P, 17 * 2 * C])
        call, callW, callX = (space_c[:, k * J * 24:(k + 1) * J * 24] for k in range(3))
        best = sb("best", [P, 24])
        above = sb("above", [P, J])
        equal = sb("equal", [P, J])
        n_above = sb("n_above", [P, 1])
        eq_run = sb("eq_run", [P, J])
        n_before = sb("n_before", [P, 1])
        keep = sb("keep", [P, J])
        keep2 = sb("keep2", [P, J])
        keep3 = sb("keep3", [P, J])
        gx = sb("gx", [P, 2 * J])
        gh = sb("gh", [96, NS])
        gb = space_a[:, 3 * T:4 * T].rearrange("p (g m) -> p g m", m=P)
        space_b = sb("space_b", [P, 2 * T])
        aT = space_b[:, 0:T].rearrange("p (m j) -> p m j", j=J)
        aTf = space_b[:, 0:T]
        wo_g = sb("wo_g", [P, C])
        bo_g = sb("bo_g", [P, C])
        oh = space_b[:, T:2 * T].rearrange("p (j c) -> p j c", c=C)


        h2T = hTf
        wg = sb("wg", [P, E0])
        bg_b = sb("bg_b", [P, E0])
        b1rows = sb("b1rows", [E0, H0])
        score = sb("score", [P, J, E0])
        smax = sb("smax", [P, J])
        hit = sb("hit", [P, J, E0])
        rank = sb("rank", [P, J, E0])
        rmax = sb("rmax", [P, J])
        choice = sb("choice", [P, E0, J])
        total = sb("total", [P, E0 * J])
        run_in = sb("run_in", [P, E0 * J])
        run_ex = sb("run_ex", [P, E0 * J])
        count = sb("count", [P, E0])
        over = sb("over", [P, E0, J])
        nblk = sb("nblk", [P, E0])
        bend = sb("bend", [P, E0])
        bstart = sb("bstart", [P, E0])
        shift = sb("shift", [P, E0])
        place = sb("place", [P, E0, J])
        place2 = sb("place2", [P, E0, J])
        place3 = sb("place3", [P, E0, J])
        slot_f = sb("slot_f", [P, J])
        slot = sb("slot", [P, J], I32)
        past = sb("past", [P, E0])
        bexp = sb("bexp", [P, 1])
        bexp_c = sb("bexp_c", [P, 1])
        bhot = sb("bhot", [P, E0])
        bhotT = sb("bhotT", [E0, P])
        bexpT = sb("bexpT", [1, P], I32)
        b1all = sb("b1all", [P, P, HC])
        zero = sb("zero", [P, C])
        w1b = space_c[:, 0:4 * H0].rearrange("p (s n) -> p s n", s=4)
        w2b = space_c[:, 4 * H0:8 * H0].rearrange("p (s k n) -> p s k n", s=4, k=HC)
        b2b = sb("b2b", [1, 4, C])
        xb = sb("xb", [P, 4, C])
        xTb = sb("xTb", [P, 2, P])
        b1b = sb("b1b", [P, 2, HC])
        hb = space_d[:, 0:2 * H0].rearrange("p (u n) -> p u n", u=2)
        yb = sb("yb", [P, 4, C])
        yg = z
        xsort = nc.dram_tensor("xsort", (NB0 * P, C), F32).ap()
        ysort = nc.dram_tensor("ysort", (NB0 * P, C), F32).ap()

        def block_of(it, v, back):
            c = 3 + v - back
            return 4 * it + c, c % 4, it + c // 4

        def wait_if(eng, s, value):
            if not isinstance(value, int) or value > 0:
                eng.wait_ge(s, value)


        wrow = sb("wrow", [P, 5, C])
        wqe = sb("wqe", [P, 2, 2, 4, 2, HD])
        wvu = sb("wvu", [P, 2 * C])
        vu_b = sb("vu_b", [P, 2 * C])
        ob_b = sb("ob_b", [P, C])
        ob_g = sb("ob_g", [P, C])
        wo1_g = sb("wo1_g", [P, C])
        slope = sb("slope", [P, HEADS])
        decay = sb("decay", [P, HEADS])
        decay_v = sb("decay_v", [P, HEADS, HD])
        space_e = sb("space_e", [P, 2 * T])
        trig = space_e[:, :].rearrange("p (g t) -> p g t", g=2)
        pos_i = sb("pos_i", [P, 2 * C], I32)
        pos = sb("pos", [P, 2 * C])
        qk = space_a[:, :].rearrange("p (w g t) -> p w g t", w=2, g=2)
        hT3 = hT
        act4 = space_d[:, :].rearrange("p (n c) -> p n c", n=4)
        vt = space_e[:, :].rearrange("p (m g k c) -> p m g k c", m=J, g=2, k=2)
        ut = z
        kt = space_b[:, :].rearrange("p (m g c) -> p m g c", m=J, g=2)
        run = space_c[:, :].rearrange("p (m g c) -> p m g c", m=17, g=2)
        state = sb("state", [P, J, 2, C // 2])
        space_q = sb("space_q", [P, T])
        qd = space_q[:, :].rearrange("p (u g h n) -> p u g h n", u=2, g=2, h=4)
        sc = space_d[:, :].rearrange("p (u g h n) -> p u g h n", u=2, g=2, h=4)
        square = sb("square", [P, 2, C])
        ssq = sb("ssq", [P, J])
        msq = sb("msq", [P, J])
        rms = sb("rms", [P, J])
        irms = sb("irms", [P, J])
        ytok = sb("ytok", [P, 2, C])
        yT, yTf = hT, hTf
        ang = space_d[:, :]
        turns = state[:, :, :, :].rearrange("p m g c -> p (m g c)")
        part = space_q[:, :]

        h4T = hTf
        rw = sb("rw", [P, E1])
        rb_b = sb("rb_b", [P, E1])
        b2r = sb("b2r", [E1 + 1, C])
        b2g = sb("b2g", [E1 + 1, C])
        by_expert = lambda k: space_c[:, T + k * J * E1:T + (k + 1) * J * E1].rearrange("p (j e) -> p j e", e=E1)
        logit = by_expert(0)
        lmax = sb("lmax", [P, J])
        ldiff = by_expert(1)
        lexp = by_expert(2)
        lsum = sb("lsum", [P, J])
        lrec = sb("lrec", [P, J])
        prob = by_expert(3)
        left = by_expert(4)
        pmax = sb("pmax", [P, J])
        phit = by_expert(5)
        prank = by_expert(6)
        prmax = sb("prmax", [P, J])
        pick = by_expert(7)
        cw = sb("cw", [P, J, E1 + 1])
        cwT = space_c[0:E1 + 1, 0:T].rearrange("e (j p) -> e j p", p=P)
        ew1 = sb("ew1", [P, 2, C])
        ew2 = sb("ew2", [P, 2, C])
        ew2g = sb("ew2g", [P, 2, C])
        ebs = sb("ebs", [P, 2])
        hid = space_b[:, :].rearrange("p (u t) -> p u t", u=2)

        def expert_of(it, v, back):
            c = 1 + v - back
            return 2 * it + c, c % 2, it + c // 2

        ps = ctx.enter_context(nc.psum_tensor("ps", [P, 8, 512], F32))

        (ld_x, ld_tab, ld_tab2, ld_rows, ld_mod, ld_att, fill_ok, dve_seq, act_seq, pool_seq, cols_up, cols_ok,
         silu_ok, silub_ok, modc_up, gate_up, modc_ok, gate_ok, var_ok, std_ok, z_ok, hT_up, hT_ok, hT_all, q_up,
         q_ok, k_up, k_ok, prod_up, prod_ok, v0_up, v0_ok, lagf_up, lagf_ok, lag_up, lag_ok, lagT_up,
         candd_ok, call_up, cnt_ok, cnt_up, g_ok, gprev_up, gx_ok, gh_up, gh_ok, toep_up, gb_ok, aT_up, aT_ok,
         oh_up, oh_ok, attn_up, x1_ok, wo_ok, xb_ok, st_out) = (sem(n) for n in """ld_x ld_tab ld_tab2 ld_rows
         ld_mod ld_att fill_ok dve_seq act_seq pool_seq cols_up cols_ok silu_ok silub_ok modc_up gate_up modc_ok
         gate_ok var_ok std_ok z_ok hT_up hT_ok hT_all q_up q_ok k_up k_ok prod_up prod_ok v0_up v0_ok lagf_up
         lagf_ok lag_up lag_ok lagT_up candd_ok call_up cnt_ok cnt_up g_ok gprev_up gx_ok gh_up gh_ok toep_up
         gb_ok aT_up aT_ok oh_up oh_ok attn_up x1_ok wo_ok xb_ok st_out""".split())

        (ld_moe, pool_zero, h2T_up, h2T_ok, score_up, choice_ok, count_up, slot_ok, bexp_ok, bexp_up,
         bhotT_ok, b1all_up, b1all_ok, zfill, scattered, xT_up, xT_ok, b1_ok, h_up, hA_ok, hV_ok, y_up,
         y_ok, gathered, x2_ok, ld_w1_0, ld_w1_1, ld_w1_2, ld_w1_3, ld_w2_0, ld_w2_1, ld_w2_2, ld_w2_3, ld_xb_0, ld_xb_1, ld_xb_2, ld_xb_3,
         st_y_0, st_y_1, st_y_2, st_y_3) = (sem(n) for n in """
         ld_moe pool_zero h2T_up h2T_ok score_up choice_ok count_up slot_ok bexp_ok bexp_up bhotT_ok
         b1all_up b1all_ok zfill scattered xT_up xT_ok b1_ok h_up hA_ok hV_ok y_up y_ok gathered x2_ok
         ld_w1_0 ld_w1_1 ld_w1_2 ld_w1_3 ld_w2_0 ld_w2_1 ld_w2_2 ld_w2_3 ld_xb_0 ld_xb_1 ld_xb_2 ld_xb_3 st_y_0 st_y_1 st_y_2 st_y_3""".split())

        (ld_l1w, ld_l1b, ld_rows2, ld_r, wT_up, wT_ok, wo1_ok, pos_ok, ang_ok, trig_ok, decay_ok0,
         decay_ok, h3T_up, h3T_ok, qk_up, act4_ok, qk_ok, vu_up, vt_ok, ut_ok, vd_ok, kt_up, kt_ok, st_up,
         run_ok, state_ok, qd_ok, sc_up, sc_ok, o_up, ssq_ok, msq_ok, rms_ok, ytok_ok, yT_up, yT_ok,
         fin_up, xb3_ok, x3_ok, h4T_up, h4T_ok, logit_up, ldiff_ok, lexp_ok, cw_ok, cwT_up, cwT_ok,
         b2g_ok, base_up, eu_up, hid_ok, edb_up, accb_ok, ew2g_ok, ebs_ok, ld_e_0, ld_e_1, ld_e2_0, ld_e2_1) = (sem(n) for n in """
         ld_l1w ld_l1b ld_rows2 ld_r wT_up wT_ok wo1_ok pos_ok ang_ok trig_ok decay_ok0 decay_ok h3T_up
         h3T_ok qk_up act4_ok qk_ok vu_up vt_ok ut_ok vd_ok kt_up kt_ok st_up run_ok state_ok qd_ok sc_up
         sc_ok o_up ssq_ok msq_ok rms_ok ytok_ok yT_up yT_ok fin_up xb3_ok x3_ok h4T_up h4T_ok logit_up
         ldiff_ok lexp_ok cw_ok cwT_up cwT_ok b2g_ok base_up eu_up hid_ok edb_up accb_ok ew2g_ok ebs_ok
         ld_e_0 ld_e_1 ld_e2_0 ld_e2_1""".split())

        block = ctx.enter_context(nc.Block())

        ld_e, ld_e2 = (ld_e_0, ld_e_1), (ld_e2_0, ld_e2_1)
        ld_w1, ld_w2 = (ld_w1_0, ld_w1_1, ld_w1_2, ld_w1_3), (ld_w2_0, ld_w2_1, ld_w2_2, ld_w2_3)
        ld_xb, st_y = (ld_xb_0, ld_xb_1, ld_xb_2, ld_xb_3), (st_y_0, st_y_1, st_y_2, st_y_3)

        psq = ps[:, 0:4, :].rearrange("p b (g m) -> p m (b g)", m=P)
        pst = ps[:, 3, :].rearrange("p (m b) -> p m b", m=8)

        def take_prod(copy, i, q):
            return copy(prod[32 * q:32 * q + 32, :, i::4], psq[32 * i:32 * i + 32, 32 * i + q:32 * i + 32:4, :])

        gbv = gb[:, :, :].rearrange("p g (i m q) -> p i q m g", i=4, q=4)

        def take_toep(copy, i, q):
            return copy(gbv[32 * i:32 * i + 32, i, q, :, :], pst[32 * q:32 * q + 32, :, i::4])

        @block.sync
        def _(eng):
            eng.dma_start(x[:, :, :], a["L0_attn_hidden_states"][0].rearrange("(p j) c -> p j c", j=J)).then_inc(ld_x, 16)
            for k, n in enumerate(("Wq", "Wk", "Wv", "Wo")):
                eng.dma_start(wqkvo[:, k, :], a["L0_attn_" + n]).then_inc(ld_att, 16)
            for k, n in enumerate(("bq", "bk", "bv")):
                eng.dma_start(brow[0:1, k, :], a["L0_attn_" + n].rearrange("(a c) -> a c", a=1)).then_inc(ld_att, 16)
            eng.dma_start(bo_b[:, :], a["L0_attn_bo"].partition_broadcast(P)).then_inc(ld_att, 16)
            eng.dma_start(tab[:, NFIRST:], a["table"][:, NFIRST:]).then_inc(ld_tab2, 16)
            eng.dma_start(wg[:, :], a["L0_ffn_Wg"]).then_inc(ld_moe, 16)
            eng.dma_start(bg_b[:, :], a["L0_ffn_bg"].partition_broadcast(P)).then_inc(ld_moe, 16)
            eng.dma_start(b1rows[:, :], a["L0_ffn_b1"]).then_inc(ld_moe, 16)
            eng.wait_ge(pool_zero, 1)
            eng.dma_start(xsort.rearrange("(b p) c -> p b c", p=P), zero[:, None, :].to_broadcast([P, NB0, C])).then_inc(zfill, 16)
            eng.dma_start(wrow[:, 0:4, :], a["L1_attn_qkvu_w"].rearrange("(s p) c -> p s c", p=P)).then_inc(ld_l1w, 16)
            eng.dma_start(wrow[:, 4, :], a["L1_attn_out_w"]).then_inc(ld_l1w, 16)
            eng.dma_start(vu_b[:, :], a["L1_attn_qkvu_b"][2 * C:4 * C].partition_broadcast(P)).then_inc(ld_l1b, 16)
            eng.dma_start(ob_b[:, :], a["L1_attn_out_b"].partition_broadcast(P)).then_inc(ld_l1b, 16)
            eng.dma_start(slope[:, :], a["L1_attn_slope_rate"].rearrange("h a b -> (h a b)").partition_broadcast(P)).then_inc(ld_l1b, 16)
            eng.dma_start(rw[:, :], a["L1_ffn_router_W"]).then_inc(ld_r, 16)
            eng.dma_start(rb_b[:, :], a["L1_ffn_router_b"].partition_broadcast(P)).then_inc(ld_r, 16)
            eng.dma_start(b2r[0:E1, :], a["L1_ffn_eb2"]).then_inc(ld_r, 16)
            eng.dma_start(b2r[E1:E1 + 1, :], a["L1_ffn_sb2"].rearrange("(a c) -> a c", a=1)).then_inc(ld_r, 16)

            def expert_id(b):
                return eng.value_load(bexpT[0:1, bass.ds(b, 1)], min_val=0, max_val=E0 - 1)

            def load_w1(b, slot_, rnd):
                e = expert_id(b)
                wait_if(eng, h_up, b - 3)
                eng.dma_start(w1b[:, slot_, :], a["L0_ffn_W1"][bass.ds(e, 1)].rearrange("e p n -> (e p) n")).then_inc(ld_w1[slot_], 16)
                return e

            def load_w2(b, slot_, rnd, e):
                wait_if(eng, y_up, b - 3)
                eng.dma_start(w2b[:, slot_, :, :], a["L0_ffn_W2"][bass.ds(e, 1)].rearrange("e (k p) n -> p (e k) n", p=P)).then_inc(ld_w2[slot_], 16)
                eng.dma_start(b2b[0:1, slot_, :], a["L0_ffn_b2"][bass.ds(e, 1)]).then_inc(ld_w2[slot_], 16)

            def step(it, v, e, last=False):
                if e is None:
                    e = expert_id(block_of(it, v, -1)[0])
                e2 = None
                if not last or v < 2:
                    e2 = load_w1(*block_of(it, v, -2))
                if not last or v < 3:
                    load_w2(*block_of(it, v, -1), e)
                return e2

            def round_of(it, last=False):
                e = None
                for v in range(4):
                    e = step(it, v, e, last)

            eng.wait_ge(bexp_ok, 2)
            for b in range(4):
                e = load_w1(*block_of(0, b - 3, 0))
                load_w2(*block_of(0, b - 3, 0), e)
            load_w1(*block_of(0, 1, 0))
            round_of(0)
            with eng.Fori(1, (NB0 - 3) // 4 - 1) as it:
                round_of(it)
            round_of((NB0 - 3) // 4 - 1, last=True)
            def load_e(e, u, rnd):
                shared = isinstance(e, int) and e == E1
                wait_if(eng, ew2g_ok, e - 1)
                eng.dma_start(ew2[:, u, :], a["L1_ffn_sW2"] if shared else
                              a["L1_ffn_eW2"][bass.ds(e, 1)].rearrange("e p n -> (e p) n")).then_inc(ld_e2[u], 16)
                wait_if(eng, eu_up, 4 * e - 4)
                eng.dma_start(ew1[:, u, :], a["L1_ffn_sW1"] if shared else
                              a["L1_ffn_eW1"][bass.ds(e, 1)].rearrange("e p n -> (e p) n")).then_inc(ld_e[u], 16)

            load_e(*expert_of(0, -1, 0))
            for v in range(2):
                load_e(*expert_of(0, v, 0))
            with eng.Fori(1, (E1 - 1) // 2) as it:
                for v in range(2):
                    load_e(*expert_of(it, v, 0))
            load_e(*expert_of(0, E1 - 1, 0))
            eng.wait_ge(accb_ok, 4 * (E1 + 2))
            eng.dma_start(out[0].rearrange("(p j) c -> p j c", j=J), x[:, :, :]).then_inc(st_out, 16)
            eng.wait_ge(st_out, 16)

        @block.scalar
        def _(eng):
            eng.dma_start(tab[:, 0:NFIRST], a["table"][:, 0:NFIRST]).then_inc(ld_tab, 16)
            for at, src in ((ROW_C0, a["L0_c"]), (ROW_C1, a["L1_c"])):
                eng.dma_start(rows[at:at + 1, :], src).then_inc(ld_rows, 16)
            for l in range(2):
                eng.dma_start(wmod[:, l, :], a[f"L{l}_wmod"]).then_inc(ld_mod, 16)
            eng.dma_start(rows[ROW_EB1:ROW_EB1 + E1, :], a["L1_ffn_eb1"]).then_inc(ld_rows2, 16)
            eng.dma_start(rows[ROW_SB1:ROW_SB1 + 1, :], a["L1_ffn_sb1"].rearrange("(a c) -> a c", a=1)).then_inc(ld_rows2, 16)
            for at, src in ((ROW_QB, a["L1_attn_qkvu_b"][0:C]), (ROW_KB, a["L1_attn_qkvu_b"][C:2 * C]),
                            (ROW_TH, a["L1_attn_theta"].rearrange("h a d -> (h a d)"))):
                s3 = src.rearrange("(g h d) -> g h d", g=2, h=4)
                for half in range(2):
                    dst = rows[at:at + 2, :].rearrange("g (h s d) -> g h s d", h=4, s=2)[:, :, half, :]
                    eng.dma_start(dst, s3).then_inc(ld_rows2, 16)

            eng.wait_ge(cols_ok, 1)
            eng.activation(silu_c[:, :], cols[:, 0:2], ACT.Silu).then_inc(silu_ok, 1)

            def ln_std():
                eng.activation(std[:, :], var_eps[:, :], ACT.Sqrt).then_inc(std_ok, 1)

            def sines(g):
                eng.wait_ge(ang_ok, g + 1)
                eng.activation(trig[:, g, :], ang, ACT.Sin).then_inc(trig_ok, 1)

            eng.wait_ge(var_ok, 1)
            ln_std()
            eng.wait_ge(wT_up, 1)
            for w in range(2):
                for half in range(2):
                    for g in range(2):
                        eng.activation(wqe[:, w, g, :, half, :], ps[:, 3, w * C + 64 * g:w * C + 64 * g + 64].rearrange("c (h d) -> c h d", h=4),
                                       ACT.Copy).then_inc(wT_ok, 1)
            eng.activation(wvu[:, :], ps[:, 3, 2 * C:4 * C], ACT.Copy).then_inc(wT_ok, 1)
            eng.wait_ge(modc_ok, 1)
            for b in range(0, 4, 2):
                eng.wait_ge(hT_up, b + 1)
                eng.activation(hT[:, :, 4 * b:4 * b + 4], ps[:, b, :].rearrange("c (j m) -> c m j", m=P), ACT.Copy,
                               scale=modc[:, 0, 1:2]).then_inc(hT_ok, 1)
            for b in range(4):
                eng.wait_ge(q_up, b + 1)
                eng.activation(qT[:, 512 * b:512 * b + 512], ps[:, b, :], ACT.Copy).then_inc(q_ok, 1)
            copy = lambda o, i: eng.activation(o, i, ACT.Copy)
            eng.wait_ge(prod_up, 1)
            for i in range(2):
                for q in range(4):
                    take_prod(copy, i, q).then_inc(prod_ok, 1)
            for b in range(4):
                eng.wait_ge(v0_up, b + 1)
                eng.activation(v0[:, 4 * b:4 * b + 4, :], ps[:, 4 + b, :], ACT.Copy).then_inc(v0_ok, 1)
            eng.wait_ge(toep_up, 1)
            eng.wait_ge(fill_ok, 3)
            for i in range(4):
                for q in range(2):
                    take_toep(copy, i, q).then_inc(gb_ok, 1)
            for b in range(0, 4, 2):
                eng.wait_ge(aT_up, b + 1)
                eng.activation(aTf[:, 512 * b:512 * b + 512], ps[:, 4 + b, :], ACT.Copy).then_inc(aT_ok, 1)
            for b in range(0, 4, 2):
                eng.wait_ge(oh_up, b + 1)
                eng.activation(oh[:, 4 * b:4 * b + 4, :], ps[:, b, :], ACT.Copy).then_inc(oh_ok, 1)
            eng.wait_ge(var_ok, 2)
            ln_std()
            for b in range(0, 4, 2):
                eng.wait_ge(h2T_up, b + 1)
                eng.activation(h2T[:, 512 * b:512 * b + 512], ps[:, b, :], ACT.Identity, bias=modc[:, 0, 2:3],
                               scale=modc[:, 0, 3:4]).then_inc(h2T_ok, 1)

            sines(0)

            def relu_a(b, slot_, rnd):
                u = slot_ % 2
                wait_if(eng, h_up, b + 1)
                wait_if(eng, b1_ok, b + 1)
                wait_if(eng, y_up, b - 1)
                for k in range(2):
                    r = eng.activation(hb[:, u, k * P:k * P + P], ps[:, 2 + u, k * P:k * P + P], ACT.Relu, bias=b1b[:, u, k:k + 1])
                r.then_inc(hA_ok, 1)

            def load_x(b, slot_, rnd):
                wait_if(eng, xT_up, b - 3)
                eng.dma_start(xb[:, slot_, :], xsort.rearrange("(b p) c -> b p c", p=P)[bass.ds(b, 1)].rearrange("b p c -> (b p) c")).then_inc(ld_xb[slot_], 16)

            def store_y(b, slot_, rnd):
                wait_if(eng, y_ok, b + 1)
                eng.dma_start(ysort.rearrange("(b p) c -> b p c", p=P)[bass.ds(b, 1)].rearrange("b p c -> (b p) c"), yb[:, slot_, :]).then_inc(st_y[slot_], 16)

            eng.wait_ge(scattered, J * 16)
            for b in range(4):
                load_x(*block_of(0, b - 3, 0))
            for v in range(-2, 0):
                relu_a(*block_of(0, v, 1))
            load_x(*block_of(0, 1, 0))

            def round_of(it, last=False):
                for v in range(4):
                    store_y(*block_of(it, v, 3))
                    if not last or v < 2:
                        load_x(*block_of(it, v, -2))
                    relu_a(*block_of(it, v, 1))

            round_of(0)
            with eng.Fori(1, (NB0 - 3) // 4 - 1) as it:
                round_of(it)
            round_of((NB0 - 3) // 4 - 1, last=True)
            relu_a(*block_of(0, NB0 - 3, 1))
            for b in range(NB0 - 3, NB0):
                store_y(*block_of(0, b - 3, 0))
            sines(1)
            eng.wait_ge(ld_l1b, 48)
            eng.activation(decay[:, :], slope[:, :], ACT.Exp).then_inc(decay_ok0, 1)
            eng.wait_ge(var_ok, 3)
            ln_std()
            for b in range(0, 4, 2):
                eng.wait_ge(h3T_up, b + 1)
                eng.activation(hT3[:, :, 4 * b:4 * b + 4], ps[:, b, :].rearrange("c (j p) -> c p j", p=P), ACT.Identity,
                               bias=modc[:, 1, 0:1], scale=modc[:, 1, 1:2]).then_inc(h3T_ok, 1)
            for n in range(16):
                w, g, b = n // 8, n // 4 % 2, n % 4
                col = (ROW_QB, ROW_KB)[w] + g
                eng.wait_ge(qk_up, n + 1)
                if n >= 4:
                    eng.wait_ge(qk_ok, n - 3)
                eng.activation(act4[:, n % 4, :], ps[:, n % 8, :], ACT.Silu, bias=cols[:, col:col + 1]).then_inc(act4_ok, 1)
            for n in range(8):
                eng.wait_ge(kt_up, n + 1)
                eng.activation(kt[:, 2 * n:2 * n + 2, :, :], ps[:, n % 4, :], ACT.Copy).then_inc(kt_ok, 1)
            for m in range(J + 1):
                if m < J:
                    eng.wait_ge(o_up, m + 1)
                    eng.activation(square[:, m % 2, :], ps[:, 4 + m % 2, 0:C], ACT.Square, accum_out=ssq[:, m:m + 1]).then_inc(ssq_ok, 1)
                    eng.wait_ge(msq_ok, m + 1)
                    eng.activation(rms[:, m:m + 1], msq[:, m:m + 1], ACT.Sqrt).then_inc(rms_ok, 1)
                if m >= 1:
                    eng.wait_ge(yT_up, m)
                    eng.activation(yTf[:, (m - 1) * P:m * P], ps[:, 6 + (m - 1) % 2, 0:P], ACT.Copy).then_inc(yT_ok, 1)
            eng.wait_ge(var_ok, 4)
            ln_std()
            for b in range(0, 4, 2):
                eng.wait_ge(h4T_up, b + 1)
                eng.activation(h4T[:, 512 * b:512 * b + 512], ps[:, b, :], ACT.Identity, bias=modc[:, 1, 2:3],
                               scale=modc[:, 1, 3:4]).then_inc(h4T_ok, 1)
            eng.wait_ge(ldiff_ok, 1)
            eng.activation(lexp[:, :, :], ldiff[:, :, :], ACT.Exp).then_inc(lexp_ok, 1)

            def relu_e(e, u, rnd):
                if isinstance(e, int):
                    eng.activation(ebs[:, u:u + 1], cols[:, ROW_EB1 + e:ROW_EB1 + e + 1], ACT.Copy).then_inc(ebs_ok, 1)
                else:
                    eng.activation(ebs[:, u:u + 1], cols[:, bass.ds(e + ROW_EB1, 1)], ACT.Copy).then_inc(ebs_ok, 1)
                eng.wait_ge(ebs_ok, e + 1)
                for b in range(4):
                    eng.wait_ge(eu_up, 4 * e + b + 1)
                    if b == 0:
                        wait_if(eng, edb_up, 4 * e - 4)
                    eng.activation(hid[:, u, 512 * b:512 * b + 512], ps[:, b, :], ACT.Relu, bias=ebs[:, u:u + 1]).then_inc(hid_ok, 1)

            relu_e(*expert_of(0, -1, 0))
            for v in range(2):
                relu_e(*expert_of(0, v, 0))
            with eng.Fori(1, (E1 - 1) // 2) as it:
                for v in range(2):
                    relu_e(*expert_of(it, v, 0))
            relu_e(*expert_of(0, E1 - 1, 0))

        @block.gpsimd
        def _(eng):
            eng.memset(ones[:, :], 1.0).then_inc(fill_ok, 1)
            eng.memset(zero[:, :], 0.0).then_inc(pool_zero, 1)
            eng.memset(ind[:, :], 0.0).then_inc(fill_ok, 1)
            eng.memset(gb[:, :, :], 0.0).then_inc(fill_ok, 1)
            eng.wait_ge(fill_ok, 3)
            eng.memset(ind[:, 0:J], float(P)).then_inc(fill_ok, 1)
            eng.wait_ge(gate_ok, 1)
            eng.wait_ge(ld_att, 8 * 16)
            eng.tensor_tensor(wo_g[:, :], wqkvo[:, 3, :], gate[:, 0, 0, :], ALU.mult).then_inc(wo_ok, 1)
            eng.tensor_tensor(bo_g[:, :], bo_b[:, :], gate[:, 0, 0, :], ALU.mult).then_inc(pool_seq, 1)
            eng.wait_ge(pool_seq, 1)
            eng.wait_ge(z_ok, J)
            eng.tensor_tensor(x[:, :, :], x[:, :, :], bo_g[:, None, :].to_broadcast([P, J, C]), ALU.add).then_inc(xb_ok, 1)
            eng.iota(pos_i[:, :], pattern=[[1, 2 * C]], base=0, channel_multiplier=0).then_inc(pool_seq, 1)
            eng.wait_ge(pool_seq, 2)
            eng.tensor_copy(pos[:, :], pos_i[:, :]).then_inc(pos_ok, 1)
            eng.wait_ge(slot_ok, 1)
            eng.wait_ge(zfill, 16)
            for j in range(J):
                eng.indirect_dma_start(out=xsort, out_offset=bass.IndirectOffsetOnAxis(ap=slot[:, j:j + 1], axis=0),
                                       in_=z[:, j, :], in_offset=None).then_inc(scattered, 16)
            for k in range(4):
                eng.wait_ge(st_y[k], 16 * ((NB0 - 1 - k) // 4 + 1))
            for j in range(J):
                eng.indirect_dma_start(out=yg[:, j, :], out_offset=None, in_=ysort,
                                       in_offset=bass.IndirectOffsetOnAxis(ap=slot[:, j:j + 1], axis=0)).then_inc(gathered, 16)
            eng.tensor_tensor(ob_g[:, :], ob_b[:, :], gate[:, 1, 0, :], ALU.mult).then_inc(pool_seq, 1)
            eng.wait_ge(pool_seq, 3)
            eng.wait_ge(z_ok, 3 * J)
            eng.tensor_tensor(x[:, :, :], x[:, :, :], ob_g[:, None, :].to_broadcast([P, J, C]), ALU.add).then_inc(xb3_ok, 1)
            eng.wait_ge(decay_ok, 1)
            dv = decay_v[:, :, :].rearrange("p (g h) d -> p g (h d)", g=2)
            for m in range(J):
                eng.wait_ge(vt_ok, m + 1)
                eng.tensor_tensor(vt[:, m, :, 1, :], vt[:, m, :, 0, :], dv, ALU.mult).then_inc(vd_ok, 1)
            hc = tb("headcol")
            for m in range(J):
                eng.wait_ge(qk_ok, 16)
                if m >= 2:
                    eng.wait_ge(sc_up, m - 1)
                for g in range(2):
                    eng.tensor_tensor(qd[:, m % 2, g, :, :], qk[:, 0, g, None, m * P:m * P + P].to_broadcast([P, 4, P]),
                                      hc[:, :, None].to_broadcast([P, 4, P]), ALU.mult).then_inc(qd_ok, 1)
            eng.wait_ge(ld_r, 64)
            eng.tensor_tensor(b2g[:, :], b2r[:, :], gate[0:E1 + 1, 1, 1, :], ALU.mult).then_inc(b2g_ok, 1)

            def gate_w(e, u, rnd):
                wait_if(eng, ld_e2[u], 16 * (rnd + 1))
                wait_if(eng, edb_up, 4 * e - 4)
                eng.tensor_tensor(ew2g[:, u, :], ew2[:, u, :], gate[:, 1, 1, :], ALU.mult).then_inc(ew2g_ok, 1)

            for v in range(-1, E1):
                gate_w(*expert_of(0, v, 0))

        @block.tensor
        def _(eng):
            eng.wait_ge(ld_tab, 16)
            eng.wait_ge(ld_rows, 2 * 16)
            eng.transpose(ps[:, 0, 0:2], rows[0:2, :], ident[0:2, 0:2]).then_inc(cols_up, 1)
            eng.wait_ge(silu_ok, 1)
            eng.wait_ge(ld_mod, 32)
            for l in range(2):
                for k, part in enumerate((0, 1, 3, 4)):
                    mm = eng.matmul(ps[:, 1, 4 * l + k:4 * l + k + 1], wmod[:, l, part * C:part * C + C],
                                    silu_c[:, l:l + 1], start=True, stop=True)
            mm.then_inc(modc_up, 1)
            eng.wait_ge(ld_l1w, 32)
            for k in range(4):
                eng.transpose(ps[:, 3, k * C:k * C + C], wrow[:, k, :], ident)
            eng.transpose(ps[:, 4, 0:C], wrow[:, 4, :], ident).then_inc(wT_up, 1)
            eng.wait_ge(silub_ok, 2)
            for l in range(2):
                for k, part in enumerate((2, 5)):
                    mm = eng.matmul(ps[:, 2, (2 * l + k) * C:(2 * l + k + 1) * C], silu_cb[:, l, :],
                                    wmod[:, l, part * C:part * C + C], start=True, stop=True)
            mm.then_inc(gate_up, 1)

            eng.wait_ge(ld_rows2, 8 * 16)
            eng.transpose(ps[:, 5, 0:NROWS], rows[:, :], ident[0:NROWS, 0:NROWS]).then_inc(cols_up, 1)

            eng.wait_ge(modc_ok, 1)
            eng.wait_ge(gate_ok, 1)
            eng.wait_ge(wT_ok, 9)
            eng.wait_ge(wo1_ok, 1)
            for j in range(J):
                eng.wait_ge(z_ok, j + 1)
                mm = eng.matmul(ps[:, j // 4, (j % 4) * P:(j % 4 + 1) * P], z[:, j, :], dft, start=True, stop=True)
                if j % 4 == 3:
                    mm.then_inc(hT_up, 1)
            eng.wait_ge(hT_all, 1)
            eng.wait_ge(ld_att, 8 * 16)
            eng.wait_ge(fill_ok, 4)
            eng.wait_ge(cols_ok, 2)
            for w, first, up in ((0, 0, q_up), (1, 4, k_up)):
                for b in range(4):
                    mm = eng.matmul(ps[:, first + b, :], wqkvo[:, w, :], hTf[:, 512 * b:512 * b + 512], start=True, stop=b > 0)
                    if b == 0:
                        mm = eng.matmul(ps[:, first, 0:J], brow[0:1, w, :], ind[0:1, 0:J], start=False, stop=True)
                    mm.then_inc(up, 1)
            for g in range(NG):
                if g % 4 == 0:
                    eng.wait_ge(q_ok, g // 4 + 1)
                    eng.wait_ge(k_ok, g // 4 + 1)
                mm = eng.matmul(ps[:, g // 4, (g % 4) * P:(g % 4 + 1) * P], qT[:, g * P:g * P + P], kT[:, g * P:g * P + P],
                                start=True, stop=True)
            mm.then_inc(prod_up, 1)
            for g in range(NG):
                mm = eng.matmul(ps[:, 4 + g // 4, (g % 4) * P:(g % 4 + 1) * P], hTf[:, g * P:g * P + P], wqkvo[:, 2, :],
                                start=True, stop=g > 0)
                if g == 0:
                    eng.matmul(ps[:, 4, 0:C], ind[0:1, :], brow[0:1, 2, :], start=False, stop=True)
                if g % 4 == 3:
                    mm.then_inc(v0_up, 1)
            eng.wait_ge(ld_tab2, 16)
            eng.wait_ge(prod_ok, 16)
            diag = tb("diag")
            for n in range(8):
                mm = eng.matmul(ps[0:NS, 0, 0:96], prod[:, n, :], diag[:, 96 * n:96 * n + 96], start=n == 0, stop=n == 7)
            mm.then_inc(lagf_up, 1)
            eng.wait_ge(lagf_ok, 1)
            corr = tb("corr")
            for k in range(6):
                half, kind = divmod(k, 3)
                mm = eng.matmul(ps[:, 1, 0:J], corr[:, k * P:k * P + P], lag_f[:, 32 * kind + 16 * half:32 * kind + 16 * half + 16],
                                start=k == 0, stop=k == 5)
            mm.then_inc(lag_up, 1)
            eng.wait_ge(lag_ok, 1)
            eng.transpose(ps[0:J, 2, 0:P], lag[:, :], ident).then_inc(lagT_up, 1)
            eng.wait_ge(candd_ok, 1)
            eng.matmul(ps[:, 3, 0:J * 24], ones[0:J, :], cand_d[:, :, :].rearrange("a b c -> a (b c)"), start=True, stop=True).then_inc(call_up, 1)
            eng.wait_ge(cnt_ok, 1)
            eng.matmul(ps[:, 0, 0:1], ones[:, :], n_above[:, :], start=True, stop=False)
            eng.matmul(ps[:, 0, 0:1], before, eq_run[:, J - 1:J], start=False, stop=True).then_inc(cnt_up, 1)
            eng.wait_ge(g_ok, 1)
            eng.matmul(ps[:, 1, 0:J], prev, gx[:, J:2 * J], start=True, stop=True).then_inc(gprev_up, 1)
            eng.wait_ge(gx_ok, 1)
            gdft, toep = tb("gdft"), tb("toep")
            for k in range(3):
                mm = eng.matmul(ps[32 * k:32 * k + 32, 2, 0:NS], gx[:, :], gdft[:, NS * k:NS * k + NS], start=True, stop=True)
            mm.then_inc(gh_up, 1)
            eng.wait_ge(gh_ok, 1)
            for m in range(8):
                mm = eng.matmul(ps[:, 3, m * NS:m * NS + NS], toep[:, m * P:m * P + P], gh[:, :], start=True, stop=True)
            mm.then_inc(toep_up, 1)
            eng.wait_ge(gb_ok, 16)
            eng.wait_ge(v0_ok, 4)
            for g in range(NG):
                mm = eng.matmul(ps[:, 4 + g // 4, (g % 4) * P:(g % 4 + 1) * P], v0[:, g, :], gb[:, g, :], start=True, stop=True)
                if g % 4 == 3:
                    mm.then_inc(aT_up, 1)
            eng.wait_ge(aT_ok, 4)
            eng.wait_ge(wo_ok, 1)
            for j in range(J):
                mm = eng.matmul(ps[:, j // 4, (j % 4) * P:(j % 4 + 1) * P], aT[:, :, j], wo_g[:, :], start=True, stop=True)
                if j % 4 == 3:
                    mm.then_inc(oh_up, 1)
            eng.wait_ge(oh_ok, 4)
            for b in range(4):
                eng.matmul(ps[:, 4 + b, :], idft, oh[:, 4 * b:4 * b + 4, :], start=True, stop=True).then_inc(attn_up, 1)
            for j in range(J):
                eng.wait_ge(z_ok, J + j + 1)
                mm = eng.transpose(ps[:, j // 4, (j % 4) * P:(j % 4 + 1) * P], z[:, j, :], ident)
                if j % 4 == 3:
                    mm.then_inc(h2T_up, 1)
            eng.wait_ge(ld_moe, 48)
            eng.wait_ge(h2T_ok, 4)
            eng.wait_ge(x1_ok, 4)
            for j in range(J):
                mm = eng.matmul(ps[:, 4, j * E0:j * E0 + E0], h2T[:, j * P:j * P + P], wg[:, :], start=True, stop=True)
            mm.then_inc(score_up, 1)
            eng.wait_ge(choice_ok, 1)
            ch = choice[:, :, :].rearrange("p e j -> p (e j)")
            eng.matmul(ps[:, 5, 0:P], before, ch, start=True, stop=True)
            eng.matmul(ps[:, 6, 0:P], ones[:, :], ch, start=True, stop=True).then_inc(count_up, 1)
            eng.wait_ge(bexp_ok, 1)
            eng.transpose(ps[0:1, 0, 0:P], bexp_c[:, :], ident)
            eng.transpose(ps[0:E0, 1, 0:P], bhot[:, :], ident).then_inc(bexp_up, 1)
            eng.wait_ge(bhotT_ok, 1)
            for k in range(HC):
                mm = eng.matmul(ps[:, 7, k * P:k * P + P], b1rows[:, k * P:k * P + P], bhotT[:, :], start=True, stop=True)
            mm.then_inc(b1all_up, 1)

            def turn(b, slot_, rnd):
                u = slot_ % 2
                wait_if(eng, ld_xb[slot_], 16 * (rnd + 1))
                wait_if(eng, xT_ok, b - 1)
                eng.transpose(ps[:, u, 0:P], xb[:, slot_, :], ident).then_inc(xT_up, 1)

            def up(b, slot_, rnd):
                u = slot_ % 2
                wait_if(eng, xT_ok, b + 1)
                wait_if(eng, hA_ok, b - 1)
                wait_if(eng, hV_ok, b - 1)
                wait_if(eng, ld_w1[slot_], 16 * (rnd + 1))
                for k in range(HC):
                    mm = eng.matmul(ps[:, (2 if k < 2 else 6) + u, k * P:k * P + P], w1b[:, slot_, k * P:k * P + P], xTb[:, u, :], start=True, stop=True)
                mm.then_inc(h_up, 1)

            def down(b, slot_, rnd):
                u = slot_ % 2
                wait_if(eng, hA_ok, b + 1)
                wait_if(eng, hV_ok, b + 1)
                wait_if(eng, y_ok, b - 1)
                wait_if(eng, ld_w2[slot_], 32 * (rnd + 1))
                for k in range(HC):
                    eng.matmul(ps[:, 4 + u, 0:C], hb[:, u, k * P:k * P + P], w2b[:, slot_, k, :], start=k == 0, stop=False)
                eng.matmul(ps[:, 4 + u, 0:C], ones[0:1, :], b2b[0:1, slot_, :], start=False, stop=True).then_inc(y_up, 1)

            eng.wait_ge(b1all_ok, 1)
            turn(*block_of(0, -3, 0))
            turn(*block_of(0, -2, 0))
            up(*block_of(0, -2, 1))
            for v in (-1,):
                turn(*block_of(0, v, 0))
                up(*block_of(0, v, 1))
                down(*block_of(0, v, 2))
            for v in range(4):
                turn(*block_of(0, v, 0))
                up(*block_of(0, v, 1))
                down(*block_of(0, v, 2))
            with eng.Fori(1, (NB0 - 3) // 4) as it:
                for v in range(4):
                    turn(*block_of(it, v, 0))
                    up(*block_of(it, v, 1))
                    down(*block_of(it, v, 2))
            up(*block_of(0, NB0 - 3, 1))
            down(*block_of(0, NB0 - 3, 2))
            down(*block_of(0, NB0 - 2, 2))
            eng.wait_ge(y_ok, NB0)
            for j in range(J):
                eng.wait_ge(z_ok, 2 * J + j + 1)
                mm = eng.transpose(ps[:, j // 4, (j % 4) * P:(j % 4 + 1) * P], z[:, j, :], ident)
                if j % 4 == 3:
                    mm.then_inc(h3T_up, 1)
            eng.wait_ge(h3T_ok, 4)
            for n in range(16):
                w, g, b = n // 8, n // 4 % 2, n % 4
                if n >= 8:
                    eng.wait_ge(act4_ok, n - 7)
                eng.matmul(ps[:, n % 8, :], wqe[:, w, g, :, :, :].rearrange("c h s d -> c (h s d)"), hTf[:, 512 * b:512 * b + 512],
                           start=True, stop=True).then_inc(qk_up, 1)
            for m in range(J):
                if m < 8:
                    eng.wait_ge(act4_ok, 9 + m)
                else:
                    eng.wait_ge(ut_ok, m - 7)
                eng.matmul(ps[:, m % 8, 0:2 * C], hTf[:, m * P:m * P + P], wvu[:, :], start=True, stop=True).then_inc(vu_up, 1)
            eng.wait_ge(qk_ok, 16)
            for n in range(8):
                if n < 4:
                    eng.wait_ge(ut_ok, 9 + n)
                else:
                    eng.wait_ge(kt_ok, n - 3)
                for i in range(4):
                    m, g = 2 * n + i // 2, i % 2
                    mm = eng.transpose(ps[:, n % 4, i * P:i * P + P], qk[:, 1, g, m * P:m * P + P], ident)
                mm.then_inc(kt_up, 1)
            for m in range(J):
                eng.wait_ge(kt_ok, m // 2 + 1)
                eng.wait_ge(vd_ok, m + 1)
                if m < 4:
                    eng.wait_ge(ut_ok, 13 + m)
                else:
                    eng.wait_ge(run_ok, m - 3)
                for g in range(2):
                    mm = eng.matmul(ps[:, 4 + m % 4, g * C:g * C + C], kt[:, m, g, :], vt[:, m, g, :, :].rearrange("p k c -> p (k c)"),
                                    start=True, stop=True)
                mm.then_inc(st_up, 1)

            def scores(m):
                eng.wait_ge(qd_ok, 2 * m + 2)
                if m >= 2:
                    eng.wait_ge(sc_ok, 2 * m - 2)
                for g in range(2):
                    mm = eng.matmul(ps[:, 2 * (m % 2) + g, :], qk[:, 1, g, m * P:m * P + P], qd[:, m % 2, g, :, :].rearrange("p h n -> p (h n)"),
                                    start=True, stop=True)
                mm.then_inc(sc_up, 1)

            def outputs(m):
                eng.wait_ge(state_ok, 1)
                if m >= 2:
                    eng.wait_ge(ytok_ok, m - 1)
                o = ps[:, 4 + m % 2, 0:C]
                for g in range(2):
                    eng.matmul(o[:, 64 * g:64 * g + 64], qk[:, 0, g, m * P:m * P + P], state[:, m, g, :], start=g == 0, stop=False,
                               skip_group_check=True)
                for g in range(2):
                    eng.wait_ge(sc_ok, 2 * m + g + 1)
                    for h in range(4):
                        c = 64 * g + HD * h
                        mm = eng.matmul(o[:, c:c + HD], sc[:, m % 2, g, h, :], vt[:, m, g, 1, HD * h:HD * h + HD], start=False,
                                        stop=g == 1 and h == 3, skip_group_check=True)
                mm.then_inc(o_up, 1)

            def turn_y(m):
                eng.wait_ge(ytok_ok, m + 1)
                if m >= 2:
                    eng.wait_ge(yT_ok, m - 1)
                eng.transpose(ps[:, 6 + m % 2, 0:P], ytok[:, m % 2, :], ident).then_inc(yT_up, 1)

            eng.wait_ge(kt_ok, 8)
            eng.wait_ge(run_ok, J)
            for m in range(J + 2):
                if m < J:
                    scores(m)
                if 1 <= m <= J:
                    outputs(m - 1)
                if m >= 2:
                    turn_y(m - 2)
            eng.wait_ge(yT_ok, J)
            eng.wait_ge(sc_ok, 2 * J)
            for j in range(J):
                mm = eng.matmul(ps[:, j // 4, (j % 4) * P:(j % 4 + 1) * P], yT[:, :, j], wo1_g[:, :], start=True, stop=True)
                if j % 4 == 3:
                    mm.then_inc(fin_up, 1)

            eng.wait_ge(x3_ok, 4)
            for j in range(J):
                eng.wait_ge(z_ok, 3 * J + j + 1)
                mm = eng.transpose(ps[:, j // 4, (j % 4) * P:(j % 4 + 1) * P], z[:, j, :], ident)
                if j % 4 == 3:
                    mm.then_inc(h4T_up, 1)
            eng.wait_ge(h4T_ok, 4)
            eng.wait_ge(ld_r, 64)
            for j in range(J):
                mm = eng.matmul(ps[:, 4, j * E1:j * E1 + E1], h4T[:, j * P:j * P + P], rw[:, :], start=True, stop=True)
            mm.then_inc(logit_up, 1)

            def up_e(e, u, rnd):
                wait_if(eng, ld_e[u], 16 * (rnd + 1))
                for b in range(4):
                    wait_if(eng, hid_ok, 4 * e - 3 + b)
                    eng.matmul(ps[:, b, :], ew1[:, u, :], h4T[:, 512 * b:512 * b + 512], start=True, stop=True).then_inc(eu_up, 1)

            def down_e(e, u, rnd):
                eng.wait_ge(ew2g_ok, e + 1)
                for b in range(4):
                    eng.wait_ge(hid_ok, 4 * e + b + 1)
                    eng.wait_ge(accb_ok, 4 * e + 1 + b)
                    for j in range(4 * b, 4 * b + 4):
                        mm = eng.matmul(ps[:, 4 + b, (j % 4) * P:(j % 4 + 1) * P], hid[:, u, j * P:j * P + P], ew2g[:, u, :], start=True, stop=True)
                    mm.then_inc(edb_up, 1)

            up_e(*expert_of(0, -1, 0))
            eng.wait_ge(cw_ok, 1)
            for j in range(J):
                mm = eng.transpose(ps[0:E1 + 1, 4 + j // 4, (j % 4) * P:(j % 4 + 1) * P], cw[:, j, :], ident)
            mm.then_inc(cwT_up, 1)
            eng.wait_ge(cwT_ok, 4)
            eng.wait_ge(b2g_ok, 1)
            for j in range(J):
                mm = eng.matmul(ps[:, 4 + j // 4, (j % 4) * P:(j % 4 + 1) * P], cwT[:, j, :], b2g[:, :], start=True, stop=True)
            mm.then_inc(base_up, 1)
            eng.wait_ge(accb_ok, 4)
            for v in range(2):
                up_e(*expert_of(0, v, 0))
                down_e(*expert_of(0, v, 1))
            with eng.Fori(1, (E1 - 1) // 2) as it:
                for v in range(2):
                    up_e(*expert_of(it, v, 0))
                    down_e(*expert_of(it, v, 1))
            up_e(*expert_of(0, E1 - 1, 0))
            down_e(*expert_of(0, E1 - 1, 1))
            down_e(*expert_of(0, E1, 1))

        @block.vector
        def _(eng):
            seq = Chain(eng, dve_seq)

            def stats_of():
                for j in range(J):
                    ins = eng.bn_stats(stats[:, j, :], x[:, j, :])
                seq(ins)
                for j in range(J):
                    ins = eng.bn_aggr(mv[:, j, :], stats[:, j, :])
                seq(ins)
                eng.tensor_scalar(var_eps[:, :], mv[:, :, 1], EPS_LN, None, ALU.add).then_inc(var_ok, 1)

            def normalise(n_std):
                eng.wait_ge(std_ok, n_std)
                seq(eng.reciprocal(rstd[:, :], std[:, :]))
                for j in range(J):
                    eng.tensor_scalar(z[:, j, :], x[:, j, :], mv[:, j, 0:1], rstd[:, j:j + 1], ALU.subtract, ALU.mult).then_inc(z_ok, 1)

            eng.wait_ge(ld_x, 16)
            stats_of()
            eng.wait_ge(cols_up, 1)
            eng.tensor_copy(cols[:, 0:2], ps[:, 0, 0:2]).then_inc(cols_ok, 1)
            eng.wait_ge(silu_ok, 1)
            eng.wait_ge(fill_ok, 1)
            for l in range(2):
                eng.tensor_scalar(silu_cb[:, l, :], ones[:, :], silu_c[:, l:l + 1], None, ALU.mult).then_inc(silub_ok, 1)
            normalise(1)
            eng.wait_ge(modc_up, 1)
            mc = modc[:, :, :].rearrange("p l k -> p (l k)")
            seq(eng.tensor_copy(mc, ps[:, 1, 0:8]))
            seq(eng.tensor_scalar(mc[:, 1::2], mc[:, 1::2], 1.0, None, ALU.add))
            eng.tensor_scalar(sa128[:, :], modc[:, 0, 0:1], float(P), None, ALU.mult).then_inc(modc_ok, 1)
            eng.wait_ge(gate_up, 1)
            g4 = lambda t: t[:, :, :, :].rearrange("p l k c -> p (l k c)")
            seq(eng.tensor_scalar(g4(gsign), ps[:, 2, :], 0.0, 2.0, ALU.is_ge, ALU.mult))
            seq(eng.tensor_scalar(g4(gneg), ps[:, 2, :], -1.0, 0.25, ALU.mult, ALU.max))
            seq(eng.tensor_tensor(g4(gmag), ps[:, 2, :], g4(gneg), ALU.max))
            eng.scalar_tensor_tensor(out=g4(gate), in0=g4(gsign), scalar=-1.0, in1=g4(gmag), op0=ALU.add, op1=ALU.mult).then_inc(gate_ok, 1)
            eng.wait_ge(gate_ok, 1)
            eng.wait_ge(wT_up, 1)
            eng.tensor_tensor(wo1_g[:, :], ps[:, 4, 0:C], gate[:, 1, 0, :], ALU.mult).then_inc(wo1_ok, 1)
            eng.wait_ge(cols_up, 2)
            eng.tensor_copy(cols[:, 2:NROWS], ps[:, 5, 2:NROWS]).then_inc(cols_ok, 1)
            for b in range(1, 4, 2):
                eng.wait_ge(hT_up, b + 1)
                eng.tensor_scalar(hT[:, :, 4 * b:4 * b + 4], ps[:, b, :].rearrange("c (j m) -> c m j", m=P), modc[:, 0, 1:2],
                                  None, ALU.mult).then_inc(hT_ok, 1)
            eng.wait_ge(hT_ok, 4)
            eng.wait_ge(modc_ok, 1)
            eng.tensor_scalar(hTf[:, 0:J], hTf[:, 0:J], sa128[:, 0:1], None, ALU.add).then_inc(hT_all, 1)
            for b in range(4):
                eng.wait_ge(k_up, b + 1)
                eng.tensor_copy(kT[:, 512 * b:512 * b + 512], ps[:, 4 + b, :]).then_inc(k_ok, 1)
            copy = lambda o, i: eng.tensor_copy(o, i)
            eng.wait_ge(prod_up, 1)
            for i in range(2, 4):
                for q in range(4):
                    take_prod(copy, i, q).then_inc(prod_ok, 1)
            eng.wait_ge(lagf_up, 1)
            eng.tensor_copy(lag_f[:, :], ps[0:NS, 0, 0:96]).then_inc(lagf_ok, 1)
            eng.wait_ge(lag_up, 1)
            eng.tensor_copy(lag[:, :], ps[:, 1, 0:J]).then_inc(lag_ok, 1)
            eng.wait_ge(lagT_up, 1)
            seq(eng.tensor_copy(lagT[:, :], ps[0:J, 2, 0:P]))

            def largest(dst, src, w1, w2):
                seq(eng.max(dst[:, 0:8], src))
                seq(eng.match_replace(w1, dst[:, 0:8], src, NEG))
                seq(eng.max(dst[:, 8:16], w1))
                seq(eng.match_replace(w2, dst[:, 8:16], w1, NEG))
                seq(eng.max(dst[:, 16:24], w2))

            largest(cand, lagT[:, :], lagW[:, :], lagX[:, :])
            eng.tensor_tensor(cand_d[:, :, :], tb("blk16").rearrange("a (b c) -> a b c", c=24),
                              cand[:, None, :].to_broadcast([J, J, 24]), ALU.mult).then_inc(candd_ok, 1)
            eng.wait_ge(call_up, 1)
            seq(eng.tensor_copy(call[:, :], ps[:, 3, 0:J * 24]))
            largest(best, call[:, :], callW[:, :], callX[:, :])
            thr = best[:, TOPK - 1:TOPK]
            seq(eng.tensor_scalar(above[:, :], lag[:, :], thr, None, ALU.is_gt))
            seq(eng.tensor_scalar(equal[:, :], lag[:, :], thr, None, ALU.is_equal))
            seq(eng.tensor_reduce(n_above[:, :], above[:, :], AX.X, ALU.add))
            eng.tensor_tensor_scan(eq_run[:, :], ones[:, 0:J], equal[:, :], 0.0, ALU.mult, ALU.add).then_inc(cnt_ok, 1)
            eng.wait_ge(cnt_ok, 1)
            eng.wait_ge(cnt_up, 1)
            seq(eng.tensor_copy(n_before[:, :], ps[:, 0, 0:1]))
            seq(eng.tensor_scalar(keep[:, :], eq_run[:, :], n_before[:, 0:1], TOPK + 0.5, ALU.add, ALU.is_le))
            seq(eng.tensor_tensor(keep2[:, :], keep[:, :], equal[:, :], ALU.mult))
            seq(eng.tensor_tensor(keep3[:, :], keep2[:, :], above[:, :], ALU.add))
            eng.tensor_tensor(gx[:, J:2 * J], keep3[:, :], lag[:, :], ALU.mult).then_inc(g_ok, 1)
            eng.wait_ge(gprev_up, 1)
            eng.tensor_copy(gx[:, 0:J], ps[:, 1, 0:J]).then_inc(gx_ok, 1)
            eng.wait_ge(gh_up, 1)
            eng.tensor_copy(gh[:, :], ps[0:96, 2, 0:NS]).then_inc(gh_ok, 1)
            eng.wait_ge(toep_up, 1)
            eng.wait_ge(fill_ok, 3)
            for i in range(4):
                for q in range(2, 4):
                    take_toep(copy, i, q).then_inc(gb_ok, 1)
            for b in range(1, 4, 2):
                eng.wait_ge(aT_up, b + 1)
                eng.tensor_copy(aTf[:, 512 * b:512 * b + 512], ps[:, 4 + b, :]).then_inc(aT_ok, 1)
            for b in range(1, 4, 2):
                eng.wait_ge(oh_up, b + 1)
                eng.tensor_copy(oh[:, 4 * b:4 * b + 4, :], ps[:, b, :]).then_inc(oh_ok, 1)
            eng.wait_ge(xb_ok, 1)
            for b in range(4):
                eng.wait_ge(attn_up, b + 1)
                eng.tensor_tensor(x[:, 4 * b:4 * b + 4, :], ps[:, 4 + b, :], x[:, 4 * b:4 * b + 4, :], ALU.add).then_inc(x1_ok, 1)
            eng.wait_ge(x1_ok, 4)
            stats_of()
            normalise(2)
            for b in range(1, 4, 2):
                eng.wait_ge(h2T_up, b + 1)
                eng.tensor_scalar(h2T[:, 512 * b:512 * b + 512], ps[:, b, :], modc[:, 0, 3:4], modc[:, 0, 2:3], ALU.mult,
                                  ALU.add).then_inc(h2T_ok, 1)
            eng.wait_ge(score_up, 1)
            seq(eng.tensor_tensor(score[:, :, :], ps[:, 4, 0:J * E0].rearrange("p (j e) -> p j e", e=E0),
                                  bg_b[:, None, :].to_broadcast([P, J, E0]), ALU.add))
            seq(eng.tensor_reduce(smax[:, :], score[:, :, :], AX.X, ALU.max))
            seq(eng.tensor_tensor(hit[:, :, :], score[:, :, :], smax[:, :, None].to_broadcast([P, J, E0]), ALU.is_equal))
            seq(eng.tensor_tensor(rank[:, :, :], hit[:, :, :], tb("last")[:, None, :].to_broadcast([P, J, E0]), ALU.mult))
            seq(eng.tensor_reduce(rmax[:, :], rank[:, :, :], AX.X, ALU.max))
            eng.tensor_tensor(choice[:, :, :].rearrange("p e j -> p j e"), rank[:, :, :],
                              rmax[:, :, None].to_broadcast([P, J, E0]), ALU.is_equal).then_inc(choice_ok, 1)
            eng.wait_ge(count_up, 1)
            seq(eng.tensor_copy(total[:, :], ps[:, 6, 0:P]))
            seq(eng.tensor_tensor_scan(run_in[:, :], ones[:, 0:E0 * J], total[:, :], 0.0, ALU.mult, ALU.add))
            seq(eng.tensor_tensor(run_ex[:, :], run_in[:, :], total[:, :], ALU.subtract))
            seq(eng.tensor_tensor(count[:, :], run_in[:, J - 1::J], run_ex[:, 0::J], ALU.subtract))
            seq(eng.tensor_tensor(over[:, :, :], count[:, :, None].to_broadcast([P, E0, J]),
                                  tb("steps")[:, None, :].to_broadcast([P, E0, J]), ALU.is_gt))
            seq(eng.tensor_reduce(nblk[:, :], over[:, :, :], AX.X, ALU.add))
            seq(eng.tensor_tensor_scan(bend[:, :], ones[:, 0:E0], nblk[:, :], 0.0, ALU.mult, ALU.add))
            seq(eng.tensor_tensor(bstart[:, :], bend[:, :], nblk[:, :], ALU.subtract))
            seq(eng.scalar_tensor_tensor(out=shift[:, :], in0=bstart[:, :], scalar=float(P), in1=run_ex[:, 0::J],
                                         op0=ALU.mult, op1=ALU.subtract))
            flat = lambda t: t[:, :, :].rearrange("p e j -> p (e j)")
            seq(eng.tensor_tensor(flat(place), ps[:, 5, 0:P], run_ex[:, :], ALU.add))
            seq(eng.tensor_tensor(place2[:, :, :], place[:, :, :], shift[:, :, None].to_broadcast([P, E0, J]), ALU.add))
            seq(eng.tensor_tensor(place3[:, :, :], place2[:, :, :], choice[:, :, :], ALU.mult))
            seq(eng.tensor_reduce(slot_f[:, :], place3[:, :, :].rearrange("p e j -> p j e"), AX.X, ALU.add))
            eng.tensor_copy(slot[:, :], slot_f[:, :]).then_inc(slot_ok, 1)
            seq(eng.tensor_scalar(past[:, :], bend[:, :], tb("pidx")[:, 0:1], None, ALU.is_le))
            seq(eng.tensor_reduce(bexp[:, :], past[:, :], AX.X, ALU.add))
            seq(eng.tensor_scalar(bexp_c[:, :], bexp[:, :], E0 - 1.0, None, ALU.min))
            eng.tensor_scalar(bhot[:, :], tb("eidx"), bexp_c[:, 0:1], None, ALU.is_equal).then_inc(bexp_ok, 1)
            eng.wait_ge(bexp_up, 1)
            eng.tensor_copy(bexpT[:, :], ps[0:1, 0, 0:P]).then_inc(bexp_ok, 1)
            eng.tensor_copy(bhotT[:, :], ps[0:E0, 1, 0:P]).then_inc(bhotT_ok, 1)
            eng.wait_ge(b1all_up, 1)
            eng.tensor_copy(b1all[:, :, :].rearrange("p b k -> p k b"), ps[:, 7, :].rearrange("p (k b) -> p k b", k=HC)).then_inc(b1all_ok, 1)

            phase = tb("phase")

            def angles(g):
                for k in range(T // (2 * C)):
                    cut = slice(k * 2 * C, (k + 1) * 2 * C)
                    ins = eng.tensor_scalar(ang[:, cut], pos[:, :], float(k * 2 * C), cols[:, ROW_TH + g:ROW_TH + g + 1], ALU.add, ALU.mult)
                seq(ins)
                seq(eng.tensor_scalar(part, ang, INV_2PI, phase[:, 1:2], ALU.mult, ALU.add))
                seq(eng.tensor_scalar(turns, part, ROUND, ROUND, ALU.add, ALU.subtract))
                for piece in TWO_PI:
                    seq(eng.scalar_tensor_tensor(out=ang, in0=turns, scalar=-piece, in1=ang, op0=ALU.mult, op1=ALU.add))
                seq(eng.tensor_scalar(ang, ang, phase[:, 0:1], PI_IN, ALU.add, ALU.min))
                eng.tensor_scalar(ang, ang, -PI_IN, None, ALU.max).then_inc(ang_ok, 1)

            eng.wait_ge(pos_ok, 1)
            angles(0)
            eng.wait_ge(trig_ok, 1)

            def scale_x(b, slot_, rnd):
                u = slot_ % 2
                wait_if(eng, xT_up, b + 1)
                wait_if(eng, h_up, b - 1)
                eng.tensor_scalar(xTb[:, u, :], ps[:, u, 0:P], modc[:, 0, 3:4], modc[:, 0, 2:3], ALU.mult, ALU.add).then_inc(xT_ok, 1)
                wait_if(eng, hA_ok, b - 1)
                wait_if(eng, hV_ok, b - 1)
                eng.tensor_copy(b1b[:, u, :], b1all[:, bass.ds(b, 1), :].rearrange("p b k -> p (b k)")).then_inc(b1_ok, 1)

            def relu_v(b, slot_, rnd):
                u = slot_ % 2
                wait_if(eng, h_up, b + 1)
                wait_if(eng, b1_ok, b + 1)
                wait_if(eng, y_up, b - 1)
                for k in range(2, HC):
                    r = eng.tensor_scalar(hb[:, u, k * P:k * P + P], ps[:, 6 + u, k * P:k * P + P], b1b[:, u, k:k + 1], 0.0, ALU.add, ALU.max)
                r.then_inc(hV_ok, 1)

            def gate_y(b, slot_, rnd):
                u = slot_ % 2
                wait_if(eng, y_up, b + 1)
                wait_if(eng, st_y[slot_], 16 * rnd)
                eng.tensor_tensor(yb[:, slot_, :], ps[:, 4 + u, 0:C], gate[:, 0, 1, :], ALU.mult).then_inc(y_ok, 1)

            eng.wait_ge(b1all_ok, 1)
            scale_x(*block_of(0, -3, 0))
            scale_x(*block_of(0, -2, 0))
            relu_v(*block_of(0, -2, 1))
            for v in (-1,):
                scale_x(*block_of(0, v, 0))
                relu_v(*block_of(0, v, 1))
                gate_y(*block_of(0, v, 2))
            for v in range(4):
                scale_x(*block_of(0, v, 0))
                relu_v(*block_of(0, v, 1))
                gate_y(*block_of(0, v, 2))
            with eng.Fori(1, (NB0 - 3) // 4) as it:
                for v in range(4):
                    scale_x(*block_of(it, v, 0))
                    relu_v(*block_of(it, v, 1))
                    gate_y(*block_of(it, v, 2))
            relu_v(*block_of(0, NB0 - 3, 1))
            gate_y(*block_of(0, NB0 - 3, 2))
            gate_y(*block_of(0, NB0 - 2, 2))
            angles(1)
            for j in range(J):
                eng.wait_ge(gathered, J * 16)
                eng.tensor_tensor(x[:, j, :], x[:, j, :], yg[:, j, :], ALU.add).then_inc(x2_ok, 1)
            for g in range(2):
                eng.wait_ge(decay_ok0, 1)
            eng.tensor_scalar(decay_v[:, :, :], decay[:, :, None].to_broadcast([P, HEADS, HD]), -1.0, None, ALU.add).then_inc(decay_ok, 1)
            eng.wait_ge(x2_ok, J)
            stats_of()
            normalise(3)
            for b in range(1, 4, 2):
                eng.wait_ge(h3T_up, b + 1)
                eng.tensor_scalar(hT3[:, :, 4 * b:4 * b + 4], ps[:, b, :].rearrange("c (j p) -> c p j", p=P), modc[:, 1, 1:2],
                                  modc[:, 1, 0:1], ALU.mult, ALU.add).then_inc(h3T_ok, 1)
            eng.wait_ge(trig_ok, 2)
            for n in range(16):
                w, g, b = n // 8, n // 4 % 2, n % 4
                eng.wait_ge(act4_ok, n + 1)
                eng.tensor_tensor(qk[:, w, g, 512 * b:512 * b + 512], act4[:, n % 4, :], trig[:, g, 512 * b:512 * b + 512], ALU.mult).then_inc(qk_ok, 1)
            for m in range(J):
                eng.wait_ge(vu_up, m + 1)
                eng.tensor_tensor(vt[:, m, :, 0, :], ps[:, m % 8, 0:C].rearrange("p (g c) -> p g c", g=2),
                                  vu_b[:, 0:C].rearrange("p (g c) -> p g c", g=2), ALU.add).then_inc(vt_ok, 1)
                eng.tensor_tensor(ut[:, m, :], ps[:, m % 8, C:2 * C], vu_b[:, C:2 * C], ALU.add).then_inc(ut_ok, 1)
            seq(eng.memset(run[:, 0, :, :], 0.0))
            for m in range(J):
                eng.wait_ge(st_up, m + 1)
                if m:
                    eng.wait_ge(run_ok, m)
                eng.tensor_tensor(run[:, m + 1, :, :], ps[:, 4 + m % 4, 0:2 * C].rearrange("p (g c) -> p g c", g=2), run[:, m, :, :], ALU.add).then_inc(run_ok, 1)
            eng.wait_ge(run_ok, J)
            hm = tb("head")
            for g in range(2):
                seq(eng.tensor_tensor(state[:, :, g, :], run[:, 0:J, g, 64:128], run[:, J, g, None, 0:64].to_broadcast([P, J, 64]), ALU.add))
            eng.tensor_tensor(state[:, :, :, :].rearrange("p m g c -> p (m g) c"), state[:, :, :, :].rearrange("p m g c -> p (m g) c"),
                              hm[:, None, :].to_broadcast([P, 2 * J, 64]), ALU.mult).then_inc(state_ok, 1)
            cm = tb("causal")

            def mask(m):
                eng.wait_ge(sc_up, m + 1)
                if m >= 2:
                    eng.wait_ge(o_up, m - 1)
                for g in range(2):
                    eng.tensor_tensor(sc[:, m % 2, g, :, :], ps[:, 2 * (m % 2) + g, :].rearrange("p (h n) -> p h n", h=4),
                                      cm[:, None, :].to_broadcast([P, 4, P]), ALU.mult).then_inc(sc_ok, 1)

            def gate_u(m):
                eng.wait_ge(ssq_ok, m + 1)
                eng.tensor_scalar(msq[:, m:m + 1], ssq[:, m:m + 1], 1.0 / C, EPS_RMS, ALU.mult, ALU.add).then_inc(msq_ok, 1)
                eng.wait_ge(rms_ok, m + 1)
                seq(eng.reciprocal(irms[:, m:m + 1], rms[:, m:m + 1]))
                if m >= 2:
                    eng.wait_ge(yT_up, m - 1)
                eng.scalar_tensor_tensor(out=ytok[:, m % 2, :], in0=ps[:, 4 + m % 2, 0:C], scalar=irms[:, m:m + 1], in1=ut[:, m, :],
                                         op0=ALU.mult, op1=ALU.mult).then_inc(ytok_ok, 1)

            for m in range(J + 1):
                if m < J:
                    mask(m)
                if m >= 1:
                    gate_u(m - 1)
            eng.wait_ge(xb3_ok, 1)
            for b in range(4):
                eng.wait_ge(fin_up, b + 1)
                eng.tensor_tensor(x[:, 4 * b:4 * b + 4, :], ps[:, b, :], x[:, 4 * b:4 * b + 4, :], ALU.add).then_inc(x3_ok, 1)

            eng.wait_ge(x3_ok, 4)
            stats_of()
            normalise(4)
            for b in range(1, 4, 2):
                eng.wait_ge(h4T_up, b + 1)
                eng.tensor_scalar(h4T[:, 512 * b:512 * b + 512], ps[:, b, :], modc[:, 1, 3:4], modc[:, 1, 2:3], ALU.mult, ALU.add).then_inc(h4T_ok, 1)
            eng.wait_ge(logit_up, 1)
            seq(eng.memset(cw[:, :, E1:E1 + 1], 1.0))
            wide = [P, J, E1]
            seq(eng.tensor_tensor(logit[:, :, :], ps[:, 4, 0:J * E1].rearrange("p (j e) -> p j e", e=E1), rb_b[:, None, :].to_broadcast(wide), ALU.add))
            seq(eng.tensor_reduce(lmax[:, :], logit[:, :, :], AX.X, ALU.max))
            eng.tensor_tensor(ldiff[:, :, :], logit[:, :, :], lmax[:, :, None].to_broadcast(wide), ALU.subtract).then_inc(ldiff_ok, 1)
            eng.wait_ge(lexp_ok, 1)
            seq(eng.tensor_reduce(lsum[:, :], lexp[:, :, :], AX.X, ALU.add))
            seq(eng.reciprocal(lrec[:, :], lsum[:, :]))
            seq(eng.tensor_tensor(prob[:, :, :], lexp[:, :, :], lrec[:, :, None].to_broadcast(wide), ALU.mult))
            src = prob
            for n in range(TOP1):
                seq(eng.tensor_reduce(pmax[:, :], src[:, :, :], AX.X, ALU.max))
                seq(eng.tensor_tensor(phit[:, :, :], src[:, :, :], pmax[:, :, None].to_broadcast(wide), ALU.is_equal))
                seq(eng.tensor_tensor(prank[:, :, :], phit[:, :, :], tb("last1")[:, None, :].to_broadcast(wide), ALU.mult))
                seq(eng.tensor_reduce(prmax[:, :], prank[:, :, :], AX.X, ALU.max))
                seq(eng.tensor_tensor(pick[:, :, :], prank[:, :, :], prmax[:, :, None].to_broadcast(wide), ALU.is_equal))
                seq(eng.scalar_tensor_tensor(out=left[:, :, :], in0=pick[:, :, :], scalar=-2.0, in1=src[:, :, :], op0=ALU.mult, op1=ALU.add))
                src = left
            eng.scalar_tensor_tensor(out=cw[:, :, 0:E1], in0=left[:, :, :], scalar=0.0, in1=prob[:, :, :], op0=ALU.is_lt, op1=ALU.mult).then_inc(cw_ok, 1)
            eng.wait_ge(cwT_up, 1)
            for b in range(4):
                eng.tensor_copy(cwT[:, 4 * b:4 * b + 4, :], ps[0:E1 + 1, 4 + b, :].rearrange("e (j p) -> e j p", p=P)).then_inc(cwT_ok, 1)
            eng.wait_ge(base_up, 1)
            for b in range(4):
                eng.tensor_tensor(x[:, 4 * b:4 * b + 4, :], ps[:, 4 + b, :], x[:, 4 * b:4 * b + 4, :], ALU.add).then_inc(accb_ok, 1)

            def add_e(e, u, rnd):
                for b in range(4):
                    eng.wait_ge(edb_up, 4 * e + b + 1)
                    for j in range(4 * b, 4 * b + 4):
                        col = e if isinstance(e, int) else None
                        w = cw[:, j, e:e + 1] if isinstance(e, int) else cw[:, j, bass.ds(e, 1)]
                        r = eng.scalar_tensor_tensor(out=x[:, j, :], in0=ps[:, 4 + b, (j % 4) * P:(j % 4 + 1) * P], scalar=w, in1=x[:, j, :],
                                                     op0=ALU.mult, op1=ALU.add)
                    r.then_inc(accb_ok, 1)
                eng.wait_ge(accb_ok, 4 * e + 8)

            eng.wait_ge(accb_ok, 4)
            for v in range(2):
                add_e(*expert_of(0, v, 1))
            with eng.Fori(1, (E1 - 1) // 2) as it:
                for v in range(2):
                    add_e(*expert_of(it, v, 1))
            add_e(*expert_of(0, E1 - 1, 1))
            add_e(*expert_of(0, E1, 1))


OUT = (1, T, C)


def kernel(**inputs):
    import concourse.bacc as bacc
    from concourse.bass_utils import run_bass_kernel_spmd

    nc = bacc.Bacc("TRN2", target_bir_lowering=False, num_devices=1)
    arrays, aps = {}, {}
    for name, v in (*inputs.items(), ("table", TABLE)):
        v = np.ascontiguousarray(v)
        arrays[name] = v
        aps[name] = nc.dram_tensor(name, v.shape, mybir.dt.from_np(v.dtype), kind="ExternalInput").ap()
    out = nc.dram_tensor("out", OUT, F32, kind="ExternalOutput").ap()
    build(nc, aps, out)
    got = run_bass_kernel_spmd(nc, [arrays], core_ids=[0])
    return got.results[0]["out"]
```

```python
from contextlib import ExitStack

import numpy as np
import concourse.bass as bass
from concourse import mybir

F32 = mybir.dt.float32
I32 = mybir.dt.int32
ALU = mybir.AluOpType
ACT = mybir.ActivationFunctionType
AX = mybir.AxisListType

P = 128
C = 128
T = 2048
J = T // P
NS = P // 2
NG = NS // 4
TOPK = int(3 * np.log(T))
EPS_LN = 1e-5
NEG = -3.0e38
E0, H0 = 8, 512
HC = H0 // P
NB0 = T // P + E0 - 1
HEADS, HD = 8, 16
E1, TOP1 = 15, 3
EPS_RMS = 1e-6
TWO_PI = [6.28125, float(np.float32(np.round((2 * np.pi - 6.28125) * 2**20) / 2**20))]
TWO_PI.append(float(np.float32(2 * np.pi - TWO_PI[0] - TWO_PI[1])))
INV_2PI = float(np.float32(0.5 / np.pi))
ROUND = 1.5 * 2.0**23
PI_IN = 3.1415925


class Chain:

    def __init__(self, eng, sem):
        self.eng, self.sem, self.n = eng, sem, 0

    def __call__(self, ins):
        self.n += 1
        ins.then_inc(self.sem, 1)
        self.eng.wait_ge(self.sem, self.n)


def shape_constants():
    p, b = np.arange(P), np.arange(NS)
    ang = 2 * np.pi * np.outer(p, b) / P
    nyq = np.cos(np.pi * p)
    dft = np.zeros((P, NS, 2))
    dft[:, :, 0], dft[:, :, 1] = np.cos(ang), -np.sin(ang)
    dft[:, 0, 1] = nyq
    idft = np.zeros((NS, 2, P))
    idft[:, 0], idft[:, 1] = 2 * np.cos(ang.T) / P, -2 * np.sin(ang.T) / P
    idft[0, 0], idft[0, 1] = 1 / P, nyq / P
    diag = np.zeros((4, 2, J, 2, 4, 3, 32))
    toep = np.zeros((3, 32, 2, 4, 4, 2, J))
    for a in range(J):
        for c in range(J):
            for r1, r2, kind, v in ((0, 0, 0, 1), (1, 1, 1, 1), (1, 0, 2, 1), (0, 1, 2, -1)):
                diag[c % 4, r1, a, r2, c // 4, kind, a - c + 16] = v
                toep[kind, a - c + 16, r2, c // 4, c % 4, r1, a] = 1 if kind < 2 else -v
    corr = np.zeros((NS, 2, 3, P))
    for half, d in ((0, p + 1), (1, p)):
        a2 = 2 * np.pi * np.outer(b, d) / P
        corr[:, half, 0] = corr[:, half, 1] = 2 * np.cos(a2)
        corr[:, half, 2] = -2 * np.sin(a2)
        corr[0, half, 0], corr[0, half, 1], corr[0, half, 2] = 1, np.cos(np.pi * d), 0
    corr /= P * C
    gdft = np.zeros((P, 3, NS))
    gdft[:, 0] = gdft[:, 1] = np.cos(ang)
    gdft[:, 2] = np.sin(ang)
    gdft[:, 1, 0] = nyq
    ident = np.eye(P)
    before = np.triu(np.ones((P, P)), 1)
    prev = np.roll(np.eye(P), 1, axis=1)
    last1 = np.tile(float(E1) - np.arange(E1), (P, 1))
    blk16 = np.repeat(np.eye(J), 24, axis=1)
    causal = np.triu(np.ones((P, P)))
    head = np.repeat(np.repeat(np.eye(4), 32, axis=0), HD, axis=1)
    phase = np.tile(np.repeat([[np.pi / 2, 0.25], [0, 0]], HD, axis=0), (4, 1))
    last = np.tile(8.0 - np.arange(8), (P, 1))
    steps = np.tile(128.0 * np.arange(J), (P, 1))
    pidx = np.arange(P, dtype=float)[:, None]
    eidx = np.tile(np.arange(E0, dtype=float), (P, 1))
    parts = dict(ident=ident, dft=dft.reshape(P, P), idft=idft.reshape(P, P), corr=corr.reshape(NS, -1),
                 diag=diag.reshape(P, -1), before=before, prev=prev, blk16=blk16, gdft=gdft.reshape(P, -1),
                 toep=toep.reshape(96, -1), causal=causal, head=head, phase=phase,
                 last=last, last1=last1, steps=steps, pidx=pidx, eidx=eidx)
    first = ("ident", "dft")
    cols, at = {}, 0
    for n in (*first, *(k for k in parts if k not in first)):
        cols[n] = (at, parts[n].shape)
        at += parts[n].shape[1]
    table = np.zeros((P, at), np.float32)
    for n, (a, (r, w)) in cols.items():
        table[:r, a:a + w] = parts[n]
    return table, cols


TABLE, COLS = shape_constants()
NFIRST = COLS["dft"][0] + P

ROW_C0, ROW_C1, ROW_EB1, ROW_SB1 = 0, 1, 2, 2 + E1
ROW_QB = ROW_SB1 + 1
ROW_KB = ROW_QB + 2
ROW_TH = ROW_KB + 2
ROW_UB = ROW_TH + 2
NROWS = ROW_UB + 1


def build(nc, a, out):
    ctx = ExitStack()
    with ctx:
        def sb(name, shape, dt=F32):
            return ctx.enter_context(nc.sbuf_tensor(name, shape, dt))

        def sem(name):
            return ctx.enter_context(nc.semaphore(name))

        tab = sb("tab", [P, TABLE.shape[1]])

        def tb(name):
            at, (r, w) = COLS[name]
            return tab[0:r, at:at + w]

        ident, dft, idft, before, prev = (tb(n) for n in ("ident", "dft", "idft", "before", "prev"))
        rows = sb("rows", [NROWS, C])
        cols = sb("cols", [P, NROWS])
        wmod = sb("wmod", [P, 2, 6 * C])
        silu_c = sb("silu_c", [P, 2])
        silu_cb = sb("silu_cb", [P, 2, P])
        ones = sb("ones", [P, P])
        modc = sb("modc", [P, 2, 4])
        gate = sb("gate", [P, 2, 2, C])
        space_d = sb("space_d", [P, T])
        gsign, gneg, gmag = (space_d[:, 512 * k:512 * k + 512].rearrange("p (l k c) -> p l k c", l=2, k=2) for k in range(3))
        x = sb("x", [P, J, C])
        z = sb("z", [P, J, C])
        stats = sb("stats", [P, J, 6])
        mv = sb("mv", [P, J, 2])
        var_eps = sb("var_eps", [P, J])
        std = sb("std", [P, J])
        rstd = sb("rstd", [P, J])
        nmr = sb("nmr", [P, J])
        hT = sb("hT", [P, P, J])
        hTf = hT[:, :, :].rearrange("c m j -> c (m j)")
        wqkvo = sb("wqkvo", [P, 4, C])
        brow = sb("brow", [1, 3, C])
        bo_b = sb("bo_b", [P, C])
        ind = sb("ind", [1, P])
        sa128 = sb("sa128", [P, 1])
        space_a = sb("space_a", [P, 4 * T])
        qT = space_a[:, 0:T]
        kT = space_a[:, T:2 * T]
        v0 = space_a[:, 2 * T:3 * T].rearrange("p (g c) -> p g c", c=C)
        prod = sb("prod", [P, 8, NS])
        lag_f = sb("lag_f", [NS, 96])
        lag = sb("lag", [P, J])
        lagT = sb("lagT", [J, P])
        lagW = sb("lagW", [J, P])
        lagX = sb("lagX", [J, P])
        cand = sb("cand", [J, 24])
        cand_d = sb("cand_d", [J, J, 24])
        space_c = sb("space_c", [P, 17 * 2 * C])
        call, callW, callX = (space_c[:, k * J * 24:(k + 1) * J * 24] for k in range(3))
        best = sb("best", [P, 24])
        above = sb("above", [P, J])
        equal = sb("equal", [P, J])
        n_above = sb("n_above", [P, 1])
        eq_run = sb("eq_run", [P, J])
        n_before = sb("n_before", [P, 1])
        keep = sb("keep", [P, J])
        keep2 = sb("keep2", [P, J])
        keep3 = sb("keep3", [P, J])
        gx = sb("gx", [P, 2 * J])
        gh = sb("gh", [96, NS])
        gb = space_a[:, 3 * T:4 * T].rearrange("p (g m) -> p g m", m=P)
        space_b = sb("space_b", [P, 2 * T])
        aT = space_b[:, 0:T].rearrange("p (m j) -> p m j", j=J)
        aTf = space_b[:, 0:T]
        wo_g = sb("wo_g", [P, C])
        bo_g = sb("bo_g", [P, C])
        oh = space_b[:, T:2 * T].rearrange("p (j c) -> p j c", c=C)


        h2T = hTf
        wg = sb("wg", [P, E0])
        bg_b = sb("bg_b", [P, E0])
        b1rows = sb("b1rows", [E0, H0])
        score = sb("score", [P, J, E0])
        smax = sb("smax", [P, J])
        hit = sb("hit", [P, J, E0])
        rank = sb("rank", [P, J, E0])
        rmax = sb("rmax", [P, J])
        choice = sb("choice", [P, E0, J])
        total = sb("total", [P, E0 * J])
        run_in = sb("run_in", [P, E0 * J])
        run_ex = sb("run_ex", [P, E0 * J])
        count = sb("count", [P, E0])
        over = sb("over", [P, E0, J])
        nblk = sb("nblk", [P, E0])
        bend = sb("bend", [P, E0])
        bstart = sb("bstart", [P, E0])
        shift = sb("shift", [P, E0])
        place = sb("place", [P, E0, J])
        place2 = sb("place2", [P, E0, J])
        place3 = sb("place3", [P, E0, J])
        slot_f = sb("slot_f", [P, J])
        slot = sb("slot", [P, J], I32)
        past = sb("past", [P, E0])
        bexp = sb("bexp", [P, 1])
        bexp_c = sb("bexp_c", [P, 1])
        bhot = sb("bhot", [P, E0])
        bhotT = sb("bhotT", [E0, P])
        bexpT = sb("bexpT", [1, P], I32)
        b1all = sb("b1all", [P, P, HC])
        zero = sb("zero", [P, C])
        w1b = space_c[:, 0:4 * H0].rearrange("p (s n) -> p s n", s=4)
        w2b = space_c[:, 4 * H0:8 * H0].rearrange("p (s k n) -> p s k n", s=4, k=HC)
        b2b = sb("b2b", [1, 4, C])
        xb = sb("xb", [P, 4, C])
        xTb = sb("xTb", [P, 2, P])
        b1b = sb("b1b", [P, 2, HC])
        hb = space_d[:, 0:2 * H0].rearrange("p (u n) -> p u n", u=2)
        yb = sb("yb", [P, 4, C])
        yg = z
        xsort = nc.dram_tensor("xsort", (NB0 * P, C), F32).ap()
        ysort = nc.dram_tensor("ysort", (NB0 * P, C), F32).ap()

        def block_of(it, v, back):
            c = 3 + v - back
            return 4 * it + c, c % 4, it + c // 4

        def wait_if(eng, s, value):
            if not isinstance(value, int) or value > 0:
                eng.wait_ge(s, value)


        wrow = sb("wrow", [P, 5, C])
        wqe = sb("wqe", [P, 2, 2, 4, 2, HD])
        wvu = sb("wvu", [P, 2 * C])
        v_b = sb("v_b", [P, C])
        ob_b = sb("ob_b", [P, C])
        ob_g = sb("ob_g", [P, C])
        wo1_g = sb("wo1_g", [P, C])
        slope = sb("slope", [P, HEADS])
        decay = sb("decay", [P, HEADS])
        decay_v = sb("decay_v", [P, HEADS, HD])
        decay_h = sb("decay_h", [P, 2, C // 2])
        total_s = sb("total_s", [P, 2, C // 2])
        cmask = wmod[:, :, :].rearrange("p l n -> p (l n)")[:, 0:HEADS * P].rearrange("p (h n) -> p h n", h=HEADS)
        space_e = sb("space_e", [P, 2 * T])
        trig = space_e[:, :].rearrange("p (g t) -> p g t", g=2)
        pos_i = sb("pos_i", [P, 2 * C], I32)
        pos = sb("pos", [P, 2 * C])
        qk = space_a[:, :].rearrange("p (w g t) -> p w g t", w=2, g=2)
        hT3 = hT
        act4 = space_d[:, :].rearrange("p (n c) -> p n c", n=4)
        vpad = space_e[:, 0:J * 4 * 3 * HD].rearrange("p (m q a d) -> p m q a d", m=J, q=4, a=3)
        kt = space_b[:, :].rearrange("p (m g c) -> p m g c", m=J, g=2)
        run = space_c[:, 0:(J + 1) * C].rearrange("p (m g c) -> p m g c", m=J + 1, g=2)
        state = sb("state", [P, J, 2, C // 2])
        space_q = sb("space_q", [P, T])
        qd = space_q[:, :].rearrange("p (u g h n) -> p u g h n", u=2, g=2, h=4)
        sc = space_d[:, :].rearrange("p (u g h n) -> p u g h n", u=2, g=2, h=4)
        msq = sb("msq", [P, J])
        rms = sb("rms", [P, J])
        irms = sb("irms", [P, J])
        uT = z[:, :, :].rearrange("p j c -> p (j c)")
        oT = hTf
        oT2 = space_b[:, 0:T].rearrange("c (p j) -> c p j", j=J)
        yT = space_b[:, T:2 * T].rearrange("c (p j) -> c p j", j=J)
        ang = space_d[:, :]
        turns = state[:, :, :, :].rearrange("p m g c -> p (m g c)")
        part = space_q[:, :]

        h4T = hTf
        rw = sb("rw", [P, E1])
        rb_b = sb("rb_b", [P, E1])
        b2r = sb("b2r", [E1 + 1, C])
        b2g = sb("b2g", [E1 + 1, C])
        by_expert = lambda k: space_c[:, T + k * J * E1:T + (k + 1) * J * E1].rearrange("p (j e) -> p j e", e=E1)
        logit = by_expert(0)
        lmax = sb("lmax", [P, J])
        ldiff = by_expert(1)
        lexp = by_expert(2)
        lsum = sb("lsum", [P, J])
        lrec = sb("lrec", [P, J])
        prob = by_expert(3)
        left = by_expert(4)
        pmax = sb("pmax", [P, J])
        phit = by_expert(5)
        prank = by_expert(6)
        prmax = sb("prmax", [P, J])
        pick = by_expert(7)
        cw = sb("cw", [P, J, E1 + 1])
        cwT = space_c[0:E1 + 1, 0:T].rearrange("e (j p) -> e j p", p=P)
        ew1 = sb("ew1", [P, 2, C])
        ew2 = sb("ew2", [P, 2, C])
        ew2g = sb("ew2g", [P, 2, C])
        ebs = sb("ebs", [P, 2])
        hid = space_b[:, :].rearrange("p (u t) -> p u t", u=2)

        def expert_of(it, v, back):
            c = 1 + v - back
            return 2 * it + c, c % 2, it + c // 2

        ps = ctx.enter_context(nc.psum_tensor("ps", [P, 8, 512], F32))

        (ld_x_0, ld_x_1, got_0, got_1, got_2, got_3, ld_tab, ld_tab2, ld_rows, ld_mod, ld_att, fill_ok, dve_seq, pool_seq, cols_up, cols_ok,
         silu_ok, silub_ok, mod_up, modc_ok, gate_ok, var_ok, std_ok, nmr_ok, zV_ok, zA_ok, hT_up, hT_ok, hT_all,
         q_ok, k_ok, prod_up, prod_ok, v0_up, v0_ok, lagf_up, lagf_ok, lag_up, lag_ok,
         candd_ok, call_up, cnt_ok, cnt_up, g_ok, gprev_up, gx_ok, gh_up, gh_ok, toep_up, gb_ok, aT_up, aT_ok,
         oh_up, oh_ok, attn_up, x_ok, wo_ok, xb_ok, st_out) = (sem(n) for n in """ld_x_0 ld_x_1 got_0 got_1 got_2 got_3 ld_tab ld_tab2 ld_rows
         ld_mod ld_att fill_ok dve_seq pool_seq cols_up cols_ok silu_ok silub_ok mod_up modc_ok
         gate_ok var_ok std_ok nmr_ok zV_ok zA_ok hT_up hT_ok hT_all q_ok k_ok prod_up prod_ok v0_up v0_ok lagf_up
         lagf_ok lag_up lag_ok candd_ok call_up cnt_ok cnt_up g_ok gprev_up gx_ok gh_up gh_ok toep_up
         gb_ok aT_up aT_ok oh_up oh_ok attn_up x_ok wo_ok xb_ok st_out""".split())

        (ld_moe, pool_zero, score_up, choice_ok, count_up, slot_ok, bexp_ok, bexp_up,
         bhotT_ok, b1all_up, b1all_ok, zfill, scattered, xT_up, xT_ok, b1_ok, h_up, hA_ok, hV_ok, y_up,
         y_ok, ld_w1_0, ld_w1_1, ld_w1_2, ld_w1_3, ld_w2_0, ld_w2_1, ld_w2_2, ld_w2_3, ld_xb_0, ld_xb_1, ld_xb_2, ld_xb_3,
         st_y_0, st_y_1, st_y_2, st_y_3) = (sem(n) for n in """
         ld_moe pool_zero score_up choice_ok count_up slot_ok bexp_ok bexp_up bhotT_ok
         b1all_up b1all_ok zfill scattered xT_up xT_ok b1_ok h_up hA_ok hV_ok y_up y_ok
         ld_w1_0 ld_w1_1 ld_w1_2 ld_w1_3 ld_w2_0 ld_w2_1 ld_w2_2 ld_w2_3 ld_xb_0 ld_xb_1 ld_xb_2 ld_xb_3 st_y_0 st_y_1 st_y_2 st_y_3""".split())

        (ld_l1w, ld_l1b, ld_rows2, ld_r, wT_up, wT_ok, wo1_ok, pos_ok, ang_ok, trig_ok, decay_ok0, decay_ok,
         qk_up, act4_ok, qkV_ok, qkP_ok, u_up, u_ok, v_up, v_ok, vz_ok, kt_up, ktA_ok,
         ktV_ok, st_up, run_ok, total_ok, state_ok, stateP_ok, cmask_ok, qz_ok, qdA_ok, qdP_ok, sc_up, sc_ok,
         o_up, oT_ok, oT2_ok, ssq_up, msq_ok, rms_ok, yT_ok, logit_up,
         ldiff_ok, lexp_ok, cw_ok, cwT_up, cwT_ok, b2g_ok, base_up, eu_up, hid_ok, edb_up, accb_ok, ew2g_ok,
         ebs_ok, ld_e_0, ld_e_1, ld_e2_0, ld_e2_1) = (sem(n) for n in """
         ld_l1w ld_l1b ld_rows2 ld_r wT_up wT_ok wo1_ok pos_ok ang_ok trig_ok decay_ok0 decay_ok
         qk_up act4_ok qkV_ok qkP_ok u_up u_ok v_up v_ok vz_ok kt_up ktA_ok ktV_ok st_up run_ok total_ok state_ok
         stateP_ok cmask_ok qz_ok qdA_ok qdP_ok sc_up sc_ok o_up oT_ok oT2_ok ssq_up msq_ok rms_ok yT_ok
         logit_up ldiff_ok lexp_ok cw_ok cwT_up cwT_ok b2g_ok base_up eu_up hid_ok
         edb_up accb_ok ew2g_ok ebs_ok ld_e_0 ld_e_1 ld_e2_0 ld_e2_1""".split())

        block = ctx.enter_context(nc.Block())

        ld_x, got = (ld_x_0, ld_x_1), (got_0, got_1, got_2, got_3)
        ld_e, ld_e2 = (ld_e_0, ld_e_1), (ld_e2_0, ld_e2_1)
        ld_w1, ld_w2 = (ld_w1_0, ld_w1_1, ld_w1_2, ld_w1_3), (ld_w2_0, ld_w2_1, ld_w2_2, ld_w2_3)
        ld_xb, st_y = (ld_xb_0, ld_xb_1, ld_xb_2, ld_xb_3), (st_y_0, st_y_1, st_y_2, st_y_3)

        def z_ready(eng, n, b):
            eng.wait_ge(zV_ok, 8 * (n - 1) + 2 * (b + 1))
            eng.wait_ge(zA_ok, 8 * (n - 1) + 2 * (b + 1))

        psq = ps[:, 0:4, :].rearrange("p b (g m) -> p m (b g)", m=P)
        pst = ps[:, 3, :].rearrange("p (m b) -> p m b", m=8)

        def take_prod(copy, i, q):
            return copy(prod[32 * q:32 * q + 32, :, i::4], psq[32 * i:32 * i + 32, 32 * i + q:32 * i + 32:4, :])

        gbv = gb[:, :, :].rearrange("p g (i m q) -> p i q m g", i=4, q=4)

        def take_toep(copy, i, q):
            return copy(gbv[32 * i:32 * i + 32, i, q, :, :], pst[32 * q:32 * q + 32, :, i::4])

        @block.sync
        def _(eng):
            for b in range(2):
                eng.dma_start(x[:, 8 * b:8 * b + 8, :], a["L0_attn_hidden_states"][0].rearrange("(p j) c -> p j c", j=J)[:, 8 * b:8 * b + 8, :]).then_inc(ld_x[b], 16)
            for k, n in enumerate(("Wq", "Wk", "Wv", "Wo")):
                eng.dma_start(wqkvo[:, k, :], a["L0_attn_" + n]).then_inc(ld_att, 16)
            for k, n in enumerate(("bq", "bk", "bv")):
                eng.dma_start(brow[0:1, k, :], a["L0_attn_" + n].rearrange("(a c) -> a c", a=1)).then_inc(ld_att, 16)
            eng.dma_start(bo_b[:, :], a["L0_attn_bo"].partition_broadcast(P)).then_inc(ld_att, 16)
            eng.dma_start(tab[:, NFIRST:], a["table"][:, NFIRST:]).then_inc(ld_tab2, 16)
            eng.dma_start(wg[:, :], a["L0_ffn_Wg"]).then_inc(ld_moe, 16)
            eng.dma_start(bg_b[:, :], a["L0_ffn_bg"].partition_broadcast(P)).then_inc(ld_moe, 16)
            eng.dma_start(b1rows[:, :], a["L0_ffn_b1"]).then_inc(ld_moe, 16)
            eng.wait_ge(pool_zero, 1)
            eng.dma_start(xsort.rearrange("(b p) c -> p b c", p=P), zero[:, None, :].to_broadcast([P, NB0, C])).then_inc(zfill, 16)
            eng.dma_start(wrow[:, 0:4, :], a["L1_attn_qkvu_w"].rearrange("(s p) c -> p s c", p=P)).then_inc(ld_l1w, 16)
            eng.dma_start(wrow[:, 4, :], a["L1_attn_out_w"]).then_inc(ld_l1w, 16)
            eng.dma_start(v_b[:, :], a["L1_attn_qkvu_b"][2 * C:3 * C].partition_broadcast(P)).then_inc(ld_l1b, 16)
            eng.dma_start(ob_b[:, :], a["L1_attn_out_b"].partition_broadcast(P)).then_inc(ld_l1b, 16)
            eng.dma_start(slope[:, :], a["L1_attn_slope_rate"].rearrange("h a b -> (h a b)").partition_broadcast(P)).then_inc(ld_l1b, 16)
            eng.dma_start(rw[:, :], a["L1_ffn_router_W"]).then_inc(ld_r, 16)
            eng.dma_start(rb_b[:, :], a["L1_ffn_router_b"].partition_broadcast(P)).then_inc(ld_r, 16)
            eng.dma_start(b2r[0:E1, :], a["L1_ffn_eb2"]).then_inc(ld_r, 16)
            eng.dma_start(b2r[E1:E1 + 1, :], a["L1_ffn_sb2"].rearrange("(a c) -> a c", a=1)).then_inc(ld_r, 16)

            def expert_id(b):
                return eng.value_load(bexpT[0:1, bass.ds(b, 1)], min_val=0, max_val=E0 - 1)

            def load_w1(b, slot_, rnd):
                e = expert_id(b)
                wait_if(eng, h_up, b - 3)
                eng.dma_start(w1b[:, slot_, :], a["L0_ffn_W1"][bass.ds(e, 1)].rearrange("e p n -> (e p) n")).then_inc(ld_w1[slot_], 16)
                return e

            def load_w2(b, slot_, rnd, e):
                wait_if(eng, y_up, b - 3)
                eng.dma_start(w2b[:, slot_, :, :], a["L0_ffn_W2"][bass.ds(e, 1)].rearrange("e (k p) n -> p (e k) n", p=P)).then_inc(ld_w2[slot_], 16)
                eng.dma_start(b2b[0:1, slot_, :], a["L0_ffn_b2"][bass.ds(e, 1)]).then_inc(ld_w2[slot_], 16)

            def step(it, v, e, last=False):
                if e is None:
                    e = expert_id(block_of(it, v, -1)[0])
                e2 = None
                if not last or v < 2:
                    e2 = load_w1(*block_of(it, v, -2))
                if not last or v < 3:
                    load_w2(*block_of(it, v, -1), e)
                return e2

            def round_of(it, last=False):
                e = None
                for v in range(4):
                    e = step(it, v, e, last)

            eng.wait_ge(bexp_ok, 2)
            for b in range(4):
                e = load_w1(*block_of(0, b - 3, 0))
                load_w2(*block_of(0, b - 3, 0), e)
            load_w1(*block_of(0, 1, 0))
            round_of(0)
            with eng.Fori(1, (NB0 - 3) // 4 - 1) as it:
                round_of(it)
            round_of((NB0 - 3) // 4 - 1, last=True)
            def load_e(e, u, rnd):
                shared = isinstance(e, int) and e == E1
                wait_if(eng, ew2g_ok, e - 1)
                eng.dma_start(ew2[:, u, :], a["L1_ffn_sW2"] if shared else
                              a["L1_ffn_eW2"][bass.ds(e, 1)].rearrange("e p n -> (e p) n")).then_inc(ld_e2[u], 16)
                wait_if(eng, eu_up, 4 * e - 4)
                eng.dma_start(ew1[:, u, :], a["L1_ffn_sW1"] if shared else
                              a["L1_ffn_eW1"][bass.ds(e, 1)].rearrange("e p n -> (e p) n")).then_inc(ld_e[u], 16)

            load_e(*expert_of(0, -1, 0))
            for v in range(2):
                load_e(*expert_of(0, v, 0))
            with eng.Fori(1, (E1 - 1) // 2) as it:
                for v in range(2):
                    load_e(*expert_of(it, v, 0))
            load_e(*expert_of(0, E1 - 1, 0))
            for b in range(4):
                eng.wait_ge(accb_ok, 4 * (E1 + 1) + b + 1)
                eng.dma_start(out[0].rearrange("(p j) c -> p j c", j=J)[:, 4 * b:4 * b + 4, :], x[:, 4 * b:4 * b + 4, :]).then_inc(st_out, 16)
            eng.wait_ge(st_out, 4 * 16)

        @block.scalar
        def _(eng):
            eng.dma_start(tab[:, 0:NFIRST], a["table"][:, 0:NFIRST]).then_inc(ld_tab, 16)
            for at, src in ((ROW_C0, a["L0_c"]), (ROW_C1, a["L1_c"])):
                eng.dma_start(rows[at:at + 1, :], src).then_inc(ld_rows, 16)
            for l in range(2):
                eng.dma_start(wmod[:, l, :], a[f"L{l}_wmod"]).then_inc(ld_mod, 16)
            eng.dma_start(rows[ROW_EB1:ROW_EB1 + E1, :], a["L1_ffn_eb1"]).then_inc(ld_rows2, 16)
            eng.dma_start(rows[ROW_SB1:ROW_SB1 + 1, :], a["L1_ffn_sb1"].rearrange("(a c) -> a c", a=1)).then_inc(ld_rows2, 16)
            eng.dma_start(rows[ROW_UB:ROW_UB + 1, :], a["L1_attn_qkvu_b"][3 * C:4 * C].rearrange("(a c) -> a c", a=1)).then_inc(ld_rows2, 16)
            for at, src in ((ROW_QB, a["L1_attn_qkvu_b"][0:C]), (ROW_KB, a["L1_attn_qkvu_b"][C:2 * C]),
                            (ROW_TH, a["L1_attn_theta"].rearrange("h a d -> (h a d)"))):
                s3 = src.rearrange("(g h d) -> g h d", g=2, h=4)
                for half in range(2):
                    dst = rows[at:at + 2, :].rearrange("g (h s d) -> g h s d", h=4, s=2)[:, :, half, :]
                    eng.dma_start(dst, s3).then_inc(ld_rows2, 16)

            eng.wait_ge(cols_ok, 1)
            eng.activation(silu_c[:, :], cols[:, 0:2], ACT.Silu).then_inc(silu_ok, 1)

            def layer_norm(n):
                for b in range(5):
                    if b < 4:
                        eng.wait_ge(var_ok, 4 * (n - 1) + b + 1)
                        eng.activation(std[:, 4 * b:4 * b + 4], var_eps[:, 4 * b:4 * b + 4], ACT.Sqrt).then_inc(std_ok, 1)
                    if b >= 1:
                        eng.wait_ge(nmr_ok, 4 * (n - 1) + b)
                        for j in range(4 * b - 2, 4 * b):
                            eng.activation(z[:, j, :], x[:, j, :], ACT.Identity, bias=nmr[:, j:j + 1], scale=rstd[:, j:j + 1]).then_inc(zA_ok, 1)

            def sines(g):
                eng.wait_ge(ang_ok, g + 1)
                eng.activation(trig[:, g, :], ang, ACT.Sin).then_inc(trig_ok, 1)

            layer_norm(1)
            eng.wait_ge(wT_up, 1)
            for w in range(2):
                for half in range(2):
                    for g in range(2):
                        eng.activation(wqe[:, w, g, :, half, :], ps[:, 3, w * C + 64 * g:w * C + 64 * g + 64].rearrange("c (h d) -> c h d", h=4),
                                       ACT.Copy).then_inc(wT_ok, 1)
            eng.activation(wvu[:, :], ps[:, 3, 2 * C:4 * C], ACT.Copy).then_inc(wT_ok, 1)
            eng.wait_ge(modc_ok, 1)
            for b in range(0, 4, 2):
                eng.wait_ge(hT_up, b + 1)
                eng.activation(hT[:, :, 4 * b:4 * b + 4], ps[:, b, :].rearrange("c (j m) -> c m j", m=P), ACT.Copy,
                               scale=modc[:, 0, 1:2]).then_inc(hT_ok, 1)
            for b in range(4):
                eng.wait_ge(qk_up, b + 1)
                eng.activation(qT[:, 512 * b:512 * b + 512], ps[:, b, :], ACT.Copy).then_inc(q_ok, 1)
            copy = lambda o, i: eng.activation(o, i, ACT.Copy)
            eng.wait_ge(prod_up, 1)
            for i in range(2):
                for q in range(4):
                    take_prod(copy, i, q).then_inc(prod_ok, 1)
            for b in range(4):
                eng.wait_ge(v0_up, b + 1)
                eng.activation(v0[:, 4 * b:4 * b + 4, :], ps[:, 4 + b, :], ACT.Copy).then_inc(v0_ok, 1)
            eng.wait_ge(toep_up, 1)
            eng.wait_ge(fill_ok, 3)
            for i in range(4):
                for q in range(2):
                    take_toep(copy, i, q).then_inc(gb_ok, 1)
            for b in range(0, 4, 2):
                eng.wait_ge(aT_up, b + 1)
                eng.activation(aTf[:, 512 * b:512 * b + 512], ps[:, 4 + b, :], ACT.Copy).then_inc(aT_ok, 1)
            for b in range(0, 4, 2):
                eng.wait_ge(oh_up, b + 1)
                eng.activation(oh[:, 4 * b:4 * b + 4, :], ps[:, b, :], ACT.Copy).then_inc(oh_ok, 1)
            layer_norm(2)
            for b in range(0, 4, 2):
                eng.wait_ge(hT_up, 4 + b + 1)
                eng.activation(h2T[:, 512 * b:512 * b + 512], ps[:, b, :], ACT.Identity, bias=modc[:, 0, 2:3],
                               scale=modc[:, 0, 3:4]).then_inc(hT_ok, 1)

            sines(0)

            def relu_a(b, slot_, rnd):
                u = slot_ % 2
                wait_if(eng, h_up, b + 1)
                wait_if(eng, b1_ok, b + 1)
                wait_if(eng, y_up, b - 1)
                for k in range(2):
                    r = eng.activation(hb[:, u, k * P:k * P + P], ps[:, 2 + u, k * P:k * P + P], ACT.Relu, bias=b1b[:, u, k:k + 1])
                r.then_inc(hA_ok, 1)

            def load_x(b, slot_, rnd):
                wait_if(eng, xT_up, b - 3)
                eng.dma_start(xb[:, slot_, :], xsort.rearrange("(b p) c -> b p c", p=P)[bass.ds(b, 1)].rearrange("b p c -> (b p) c")).then_inc(ld_xb[slot_], 16)

            def store_y(b, slot_, rnd):
                wait_if(eng, y_ok, b + 1)
                eng.dma_start(ysort.rearrange("(b p) c -> b p c", p=P)[bass.ds(b, 1)].rearrange("b p c -> (b p) c"), yb[:, slot_, :]).then_inc(st_y[slot_], 16)

            eng.wait_ge(scattered, J * 16)
            for b in range(4):
                load_x(*block_of(0, b - 3, 0))
            for v in range(-2, 0):
                relu_a(*block_of(0, v, 1))
            load_x(*block_of(0, 1, 0))

            def round_of(it, last=False):
                for v in range(4):
                    store_y(*block_of(it, v, 3))
                    if not last or v < 2:
                        load_x(*block_of(it, v, -2))
                    relu_a(*block_of(it, v, 1))

            round_of(0)
            with eng.Fori(1, (NB0 - 3) // 4 - 1) as it:
                round_of(it)
            round_of((NB0 - 3) // 4 - 1, last=True)
            relu_a(*block_of(0, NB0 - 3, 1))
            for b in range(NB0 - 3, NB0):
                store_y(*block_of(0, b - 3, 0))
            sines(1)
            eng.wait_ge(ld_l1b, 48)
            eng.activation(decay[:, :], slope[:, :], ACT.Exp).then_inc(decay_ok0, 1)
            layer_norm(3)
            for b in range(0, 4, 2):
                eng.wait_ge(hT_up, 8 + b + 1)
                eng.activation(hT3[:, :, 4 * b:4 * b + 4], ps[:, b, :].rearrange("c (j p) -> c p j", p=P), ACT.Identity,
                               bias=modc[:, 1, 0:1], scale=modc[:, 1, 1:2]).then_inc(hT_ok, 1)
            for n in range(16):
                w, g, b = 1 - n // 8, n // 4 % 2, n % 4
                col = (ROW_QB, ROW_KB)[w] + g
                eng.wait_ge(qk_up, 8 + n + 1)
                if n >= 4 and b < 3:
                    eng.wait_ge(qkV_ok, 3 * (n // 4 - 1) + b + 1)
                elif n >= 4:
                    eng.wait_ge(qkP_ok, n // 4)
                eng.activation(act4[:, b, :], ps[:, n % 8, :], ACT.Silu, bias=cols[:, col:col + 1]).then_inc(act4_ok, 1)
            for b in range(4):
                eng.wait_ge(u_up, b + 1)
                eng.activation(uT[:, 512 * b:512 * b + 512], ps[:, b, :], ACT.Identity, bias=cols[:, ROW_UB:ROW_UB + 1]).then_inc(u_ok, 1)
            for n in range(0, 8, 2):
                eng.wait_ge(kt_up, n + 1)
                eng.activation(kt[:, 2 * n:2 * n + 2, :, :], ps[:, n % 4, :], ACT.Copy).then_inc(ktA_ok, 1)
            eng.wait_ge(qz_ok, 1)
            eng.wait_ge(qkV_ok, 12)
            eng.wait_ge(qkP_ok, 4)
            for m in range(J + 2):
                if m < J:
                    if m >= 2:
                        eng.wait_ge(sc_up, m - 1)
                    for h in range(2):
                        r = eng.activation(qd[32 * h:32 * h + 32, m % 2, :, h, :], qk[32 * h:32 * h + 32, 0, :, m * P:m * P + P], ACT.Copy)
                    r.then_inc(qdA_ok, 1)
                if m % 4 == 1 and m > 4:
                    b = m // 4 - 1
                    eng.wait_ge(o_up, 4 * b + 4)
                    eng.activation(oT[:, 512 * b:512 * b + 512], ps[:, 4 + b % 2, :], ACT.Copy).then_inc(oT_ok, 1)
                    eng.activation(oT2[:, 32 * b:32 * b + 32, :], ps[:, 4 + b % 2, :], ACT.Square).then_inc(oT2_ok, 1)
            eng.wait_ge(msq_ok, 1)
            eng.activation(rms[:, :], msq[:, :], ACT.Sqrt).then_inc(rms_ok, 1)
            layer_norm(4)
            for b in range(0, 4, 2):
                eng.wait_ge(hT_up, 12 + b + 1)
                eng.activation(h4T[:, 512 * b:512 * b + 512], ps[:, b, :], ACT.Identity, bias=modc[:, 1, 2:3],
                               scale=modc[:, 1, 3:4]).then_inc(hT_ok, 1)
            eng.wait_ge(ldiff_ok, 1)
            eng.activation(lexp[:, :, :], ldiff[:, :, :], ACT.Exp).then_inc(lexp_ok, 1)

            def relu_e(e, u, rnd):
                if isinstance(e, int):
                    eng.activation(ebs[:, u:u + 1], cols[:, ROW_EB1 + e:ROW_EB1 + e + 1], ACT.Copy).then_inc(ebs_ok, 1)
                else:
                    eng.activation(ebs[:, u:u + 1], cols[:, bass.ds(e + ROW_EB1, 1)], ACT.Copy).then_inc(ebs_ok, 1)
                eng.wait_ge(ebs_ok, e + 1)
                for b in range(4):
                    eng.wait_ge(eu_up, 4 * e + b + 1)
                    if b == 0:
                        wait_if(eng, edb_up, 4 * e - 4)
                    eng.activation(hid[:, u, 512 * b:512 * b + 512], ps[:, b, :], ACT.Relu, bias=ebs[:, u:u + 1]).then_inc(hid_ok, 1)

            relu_e(*expert_of(0, -1, 0))
            for v in range(2):
                relu_e(*expert_of(0, v, 0))
            with eng.Fori(1, (E1 - 1) // 2) as it:
                for v in range(2):
                    relu_e(*expert_of(it, v, 0))
            relu_e(*expert_of(0, E1 - 1, 0))

        @block.gpsimd
        def _(eng):
            eng.memset(ones[:, :], 1.0).then_inc(fill_ok, 1)
            eng.memset(zero[:, :], 0.0).then_inc(pool_zero, 1)
            eng.memset(ind[:, :], 0.0).then_inc(fill_ok, 1)
            eng.memset(gb[:, :, :], 0.0).then_inc(fill_ok, 1)
            eng.wait_ge(fill_ok, 3)
            eng.memset(ind[:, 0:J], float(P)).then_inc(fill_ok, 1)
            eng.wait_ge(gate_ok, 1)
            eng.wait_ge(ld_att, 8 * 16)
            eng.tensor_tensor(wo_g[:, :], wqkvo[:, 3, :], gate[:, 0, 0, :], ALU.mult).then_inc(wo_ok, 1)
            eng.tensor_tensor(bo_g[:, :], bo_b[:, :], gate[:, 0, 0, :], ALU.mult).then_inc(pool_seq, 1)
            eng.wait_ge(pool_seq, 1)
            z_ready(eng, 1, 3)
            eng.tensor_tensor(x[:, :, :], x[:, :, :], bo_g[:, None, :].to_broadcast([P, J, C]), ALU.add).then_inc(xb_ok, 1)
            eng.iota(pos_i[:, :], pattern=[[1, 2 * C]], base=0, channel_multiplier=0).then_inc(pool_seq, 1)
            eng.wait_ge(pool_seq, 2)
            eng.tensor_copy(pos[:, :], pos_i[:, :]).then_inc(pos_ok, 1)
            eng.wait_ge(slot_ok, 1)
            eng.wait_ge(zfill, 16)
            for j in range(J):
                eng.indirect_dma_start(out=xsort, out_offset=bass.IndirectOffsetOnAxis(ap=slot[:, j:j + 1], axis=0),
                                       in_=z[:, j, :], in_offset=None).then_inc(scattered, 16)
            for k in range(4):
                eng.wait_ge(st_y[k], 16 * ((NB0 - 1 - k) // 4 + 1))
            for j in range(J):
                eng.indirect_dma_start(out=yg[:, j, :], out_offset=None, in_=ysort,
                                       in_offset=bass.IndirectOffsetOnAxis(ap=slot[:, j:j + 1], axis=0)).then_inc(got[j // 4], 16)
            eng.tensor_tensor(ob_g[:, :], ob_b[:, :], gate[:, 1, 0, :], ALU.mult).then_inc(pool_seq, 1)
            eng.wait_ge(ang_ok, 2)
            eng.memset(qd[:, :, :, :, :], 0.0).then_inc(qz_ok, 1)
            eng.wait_ge(decay_ok, 1)
            eng.tensor_tensor(cmask[:, :, :], tb("causal")[:, None, :].to_broadcast([P, HEADS, P]),
                              decay_v[:, :, 0:1].to_broadcast([P, HEADS, P]), ALU.mult).then_inc(cmask_ok, 1)
            eng.wait_ge(trig_ok, 2)
            for n in range(3, 16, 4):
                w, g, b = 1 - n // 8, n // 4 % 2, n % 4
                eng.wait_ge(act4_ok, n + 1)
                eng.tensor_tensor(qk[:, w, g, 512 * b:512 * b + 512], act4[:, b, :], trig[:, g, 512 * b:512 * b + 512], ALU.mult).then_inc(qkP_ok, 1)
            eng.wait_ge(qkP_ok, 4)
            eng.wait_ge(qkV_ok, 12)
            eng.memset(vpad[:, :, :, 1, :], 0.0).then_inc(vz_ok, 1)

            def spread_q(m):
                if m >= 2:
                    eng.wait_ge(sc_up, m - 1)
                for h in range(2, 4):
                    eng.tensor_copy(qd[32 * h:32 * h + 32, m % 2, :, h, :], qk[32 * h:32 * h + 32, 0, :, m * P:m * P + P]).then_inc(qdP_ok, 1)
                    eng.wait_ge(qdP_ok, 2 * m + h - 1)

            eng.wait_ge(vz_ok, 1)
            for m in range(2):
                spread_q(m)
            eng.wait_ge(total_ok, 1)
            late = run[:, J // 2:J, :, :].rearrange("p m g c -> p m (g c)")
            eng.tensor_tensor(late, late, decay_h[:, :, :].rearrange("p g c -> p (g c)")[:, None, :].to_broadcast([P, J // 2, C]), ALU.mult).then_inc(pool_seq, 1)
            eng.wait_ge(pool_seq, 4)
            eng.tensor_tensor(state[:, J // 2:J, :, :].rearrange("p m g c -> p m (g c)"), late,
                              total_s[:, :, :].rearrange("p g c -> p (g c)")[:, None, :].to_broadcast([P, J // 2, C]), ALU.add).then_inc(stateP_ok, 1)
            eng.wait_ge(stateP_ok, 1)
            for m in range(2, J):
                spread_q(m)
            z_ready(eng, 3, 3)
            eng.tensor_tensor(x[:, :, :], x[:, :, :], ob_g[:, None, :].to_broadcast([P, J, C]), ALU.add).then_inc(xb_ok, 1)
            eng.wait_ge(ld_r, 64)
            eng.tensor_tensor(b2g[:, :], b2r[:, :], gate[0:E1 + 1, 1, 1, :], ALU.mult).then_inc(b2g_ok, 1)

            def gate_w(e, u, rnd):
                wait_if(eng, ld_e2[u], 16 * (rnd + 1))
                wait_if(eng, edb_up, 4 * e - 4)
                eng.tensor_tensor(ew2g[:, u, :], ew2[:, u, :], gate[:, 1, 1, :], ALU.mult).then_inc(ew2g_ok, 1)

            for v in range(-1, E1):
                gate_w(*expert_of(0, v, 0))

        @block.tensor
        def _(eng):
            eng.wait_ge(ld_tab, 16)
            eng.wait_ge(ld_rows, 2 * 16)
            eng.transpose(ps[:, 0, 0:2], rows[0:2, :], ident[0:2, 0:2]).then_inc(cols_up, 1)
            eng.wait_ge(silu_ok, 1)
            eng.wait_ge(ld_mod, 32)
            for l in range(2):
                for k, part in enumerate((0, 1, 3, 4)):
                    mm = eng.matmul(ps[:, 1, 4 * l + k:4 * l + k + 1], wmod[:, l, part * C:part * C + C],
                                    silu_c[:, l:l + 1], start=True, stop=True)
            mm.then_inc(mod_up, 1)
            eng.wait_ge(ld_l1w, 32)
            for k in range(4):
                eng.transpose(ps[:, 3, k * C:k * C + C], wrow[:, k, :], ident)
            eng.transpose(ps[:, 4, 0:C], wrow[:, 4, :], ident).then_inc(wT_up, 1)
            eng.wait_ge(silub_ok, 2)
            for l in range(2):
                for k, part in enumerate((2, 5)):
                    mm = eng.matmul(ps[:, 2, (2 * l + k) * C:(2 * l + k + 1) * C], silu_cb[:, l, :],
                                    wmod[:, l, part * C:part * C + C], start=True, stop=True)
            mm.then_inc(mod_up, 1)

            eng.wait_ge(ld_rows2, 9 * 16)
            eng.transpose(ps[:, 5, 0:NROWS], rows[:, :], ident[0:NROWS, 0:NROWS]).then_inc(cols_up, 1)

            eng.wait_ge(modc_ok, 1)
            eng.wait_ge(gate_ok, 1)
            eng.wait_ge(wT_ok, 9)
            eng.wait_ge(wo1_ok, 1)
            for j in range(J):
                z_ready(eng, 1, j // 4)
                mm = eng.matmul(ps[:, j // 4, (j % 4) * P:(j % 4 + 1) * P], z[:, j, :], dft, start=True, stop=True)
                if j % 4 == 3:
                    mm.then_inc(hT_up, 1)
            eng.wait_ge(hT_all, 1)
            eng.wait_ge(ld_att, 8 * 16)
            eng.wait_ge(fill_ok, 4)
            eng.wait_ge(cols_ok, 2)
            for w, first in ((0, 0), (1, 4)):
                for b in range(4):
                    mm = eng.matmul(ps[:, first + b, :], wqkvo[:, w, :], hTf[:, 512 * b:512 * b + 512], start=True, stop=b > 0)
                    if b == 0:
                        mm = eng.matmul(ps[:, first, 0:J], brow[0:1, w, :], ind[0:1, 0:J], start=False, stop=True)
                    mm.then_inc(qk_up, 1)
            for g in range(NG):
                if g % 4 == 0:
                    eng.wait_ge(q_ok, g // 4 + 1)
                    eng.wait_ge(k_ok, g // 4 + 1)
                mm = eng.matmul(ps[:, g // 4, (g % 4) * P:(g % 4 + 1) * P], qT[:, g * P:g * P + P], kT[:, g * P:g * P + P],
                                start=True, stop=True)
            mm.then_inc(prod_up, 1)
            for g in range(NG):
                mm = eng.matmul(ps[:, 4 + g // 4, (g % 4) * P:(g % 4 + 1) * P], hTf[:, g * P:g * P + P], wqkvo[:, 2, :],
                                start=True, stop=g > 0)
                if g == 0:
                    eng.matmul(ps[:, 4, 0:C], ind[0:1, :], brow[0:1, 2, :], start=False, stop=True)
                if g % 4 == 3:
                    mm.then_inc(v0_up, 1)
            eng.wait_ge(ld_tab2, 16)
            eng.wait_ge(prod_ok, 16)
            diag = tb("diag")
            for n in range(8):
                mm = eng.matmul(ps[0:NS, 0, 0:96], prod[:, n, :], diag[:, 96 * n:96 * n + 96], start=n == 0, stop=n == 7)
            mm.then_inc(lagf_up, 1)
            eng.wait_ge(lagf_ok, 1)
            corr = tb("corr")
            for k in range(6):
                half, kind = divmod(k, 3)
                mm = eng.matmul(ps[:, 1, 0:J], corr[:, k * P:k * P + P], lag_f[:, 32 * kind + 16 * half:32 * kind + 16 * half + 16],
                                start=k == 0, stop=k == 5)
            mm.then_inc(lag_up, 1)
            eng.wait_ge(lag_ok, 1)
            eng.transpose(ps[0:J, 2, 0:P], lag[:, :], ident).then_inc(lag_up, 1)
            eng.wait_ge(candd_ok, 1)
            eng.matmul(ps[:, 3, 0:J * 24], ones[0:J, :], cand_d[:, :, :].rearrange("a b c -> a (b c)"), start=True, stop=True).then_inc(call_up, 1)
            eng.wait_ge(cnt_ok, 1)
            eng.matmul(ps[:, 0, 0:1], ones[:, :], n_above[:, :], start=True, stop=False)
            eng.matmul(ps[:, 0, 0:1], before, eq_run[:, J - 1:J], start=False, stop=True).then_inc(cnt_up, 1)
            eng.wait_ge(g_ok, 1)
            eng.matmul(ps[:, 1, 0:J], prev, gx[:, J:2 * J], start=True, stop=True).then_inc(gprev_up, 1)
            eng.wait_ge(gx_ok, 1)
            gdft, toep = tb("gdft"), tb("toep")
            for k in range(3):
                mm = eng.matmul(ps[32 * k:32 * k + 32, 2, 0:NS], gx[:, :], gdft[:, NS * k:NS * k + NS], start=True, stop=True)
            mm.then_inc(gh_up, 1)
            eng.wait_ge(gh_ok, 1)
            for m in range(8):
                mm = eng.matmul(ps[:, 3, m * NS:m * NS + NS], toep[:, m * P:m * P + P], gh[:, :], start=True, stop=True)
            mm.then_inc(toep_up, 1)
            eng.wait_ge(gb_ok, 16)
            eng.wait_ge(v0_ok, 4)
            for g in range(NG):
                mm = eng.matmul(ps[:, 4 + g // 4, (g % 4) * P:(g % 4 + 1) * P], v0[:, g, :], gb[:, g, :], start=True, stop=True)
                if g % 4 == 3:
                    mm.then_inc(aT_up, 1)
            eng.wait_ge(aT_ok, 4)
            eng.wait_ge(wo_ok, 1)
            for j in range(J):
                mm = eng.matmul(ps[:, j // 4, (j % 4) * P:(j % 4 + 1) * P], aT[:, :, j], wo_g[:, :], start=True, stop=True)
                if j % 4 == 3:
                    mm.then_inc(oh_up, 1)
            eng.wait_ge(oh_ok, 4)
            for b in range(4):
                eng.matmul(ps[:, 4 + b, :], idft, oh[:, 4 * b:4 * b + 4, :], start=True, stop=True).then_inc(attn_up, 1)
            for j in range(J):
                z_ready(eng, 2, j // 4)
                mm = eng.transpose(ps[:, j // 4, (j % 4) * P:(j % 4 + 1) * P], z[:, j, :], ident)
                if j % 4 == 3:
                    mm.then_inc(hT_up, 1)
            eng.wait_ge(ld_moe, 48)
            eng.wait_ge(hT_ok, 8)
            eng.wait_ge(x_ok, 4)
            for j in range(J):
                mm = eng.matmul(ps[:, 4, j * E0:j * E0 + E0], h2T[:, j * P:j * P + P], wg[:, :], start=True, stop=True)
            mm.then_inc(score_up, 1)
            eng.wait_ge(choice_ok, 1)
            ch = choice[:, :, :].rearrange("p e j -> p (e j)")
            eng.matmul(ps[:, 5, 0:P], before, ch, start=True, stop=True)
            eng.matmul(ps[:, 6, 0:P], ones[:, :], ch, start=True, stop=True).then_inc(count_up, 1)
            eng.wait_ge(bexp_ok, 1)
            eng.transpose(ps[0:1, 0, 0:P], bexp_c[:, :], ident)
            eng.transpose(ps[0:E0, 1, 0:P], bhot[:, :], ident).then_inc(bexp_up, 1)
            eng.wait_ge(bhotT_ok, 1)
            for k in range(HC):
                mm = eng.matmul(ps[:, 7, k * P:k * P + P], b1rows[:, k * P:k * P + P], bhotT[:, :], start=True, stop=True)
            mm.then_inc(b1all_up, 1)

            def turn(b, slot_, rnd):
                u = slot_ % 2
                wait_if(eng, ld_xb[slot_], 16 * (rnd + 1))
                wait_if(eng, xT_ok, b - 1)
                eng.transpose(ps[:, u, 0:P], xb[:, slot_, :], ident).then_inc(xT_up, 1)

            def up(b, slot_, rnd):
                u = slot_ % 2
                wait_if(eng, xT_ok, b + 1)
                wait_if(eng, hA_ok, b - 1)
                wait_if(eng, hV_ok, b - 1)
                wait_if(eng, ld_w1[slot_], 16 * (rnd + 1))
                for k in range(HC):
                    mm = eng.matmul(ps[:, (2 if k < 2 else 6) + u, k * P:k * P + P], w1b[:, slot_, k * P:k * P + P], xTb[:, u, :], start=True, stop=True)
                mm.then_inc(h_up, 1)

            def down(b, slot_, rnd):
                u = slot_ % 2
                wait_if(eng, hA_ok, b + 1)
                wait_if(eng, hV_ok, b + 1)
                wait_if(eng, y_ok, b - 1)
                wait_if(eng, ld_w2[slot_], 32 * (rnd + 1))
                for k in range(HC):
                    eng.matmul(ps[:, 4 + u, 0:C], hb[:, u, k * P:k * P + P], w2b[:, slot_, k, :], start=k == 0, stop=False)
                eng.matmul(ps[:, 4 + u, 0:C], ones[0:1, :], b2b[0:1, slot_, :], start=False, stop=True).then_inc(y_up, 1)

            eng.wait_ge(b1all_ok, 1)
            turn(*block_of(0, -3, 0))
            turn(*block_of(0, -2, 0))
            up(*block_of(0, -2, 1))
            for v in (-1,):
                turn(*block_of(0, v, 0))
                up(*block_of(0, v, 1))
                down(*block_of(0, v, 2))
            for v in range(4):
                turn(*block_of(0, v, 0))
                up(*block_of(0, v, 1))
                down(*block_of(0, v, 2))
            with eng.Fori(1, (NB0 - 3) // 4) as it:
                for v in range(4):
                    turn(*block_of(it, v, 0))
                    up(*block_of(it, v, 1))
                    down(*block_of(it, v, 2))
            up(*block_of(0, NB0 - 3, 1))
            down(*block_of(0, NB0 - 3, 2))
            down(*block_of(0, NB0 - 2, 2))
            eng.wait_ge(y_ok, NB0)
            for j in range(J):
                z_ready(eng, 3, j // 4)
                mm = eng.transpose(ps[:, j // 4, (j % 4) * P:(j % 4 + 1) * P], z[:, j, :], ident)
                if j % 4 == 3:
                    mm.then_inc(hT_up, 1)
            eng.wait_ge(hT_ok, 12)
            for n in range(16):
                w, g, b = 1 - n // 8, n // 4 % 2, n % 4
                if n >= 8:
                    eng.wait_ge(act4_ok, n - 7)
                eng.matmul(ps[:, n % 8, :], wqe[:, w, g, :, :, :].rearrange("c h s d -> c (h s d)"), hTf[:, 512 * b:512 * b + 512],
                           start=True, stop=True).then_inc(qk_up, 1)
            for b in range(4):
                eng.wait_ge(act4_ok, 9 + b)
                eng.matmul(ps[:, b, :], wvu[:, C:2 * C], hTf[:, 512 * b:512 * b + 512], start=True, stop=True).then_inc(u_up, 1)
            for b in range(4):
                eng.wait_ge(act4_ok, 13 + b)
                for m in range(4 * b, 4 * b + 4):
                    mm = eng.matmul(ps[:, 4 + b, (m % 4) * C:(m % 4) * C + C], hTf[:, m * P:m * P + P], wvu[:, 0:C], start=True, stop=True)
                mm.then_inc(v_up, 1)
            eng.wait_ge(qkV_ok, 6)
            eng.wait_ge(qkP_ok, 2)
            for n in range(8):
                if n < 4:
                    eng.wait_ge(u_ok, n + 1)
                else:
                    eng.wait_ge((ktA_ok, ktV_ok)[n % 2], (n - 4) // 2 + 1)
                for i in range(4):
                    m, g = 2 * n + i // 2, i % 2
                    mm = eng.transpose(ps[:, n % 4, i * P:i * P + P], qk[:, 1, g, m * P:m * P + P], ident)
                mm.then_inc(kt_up, 1)
            eng.wait_ge(vz_ok, 1)
            for m in range(J):
                n = m // 2
                eng.wait_ge((ktA_ok, ktV_ok)[n % 2], n // 2 + 1)
                eng.wait_ge(v_ok, 8)
                if m >= 4:
                    eng.wait_ge(run_ok, m - 3)
                for g in range(2):
                    mm = eng.matmul(ps[:, 4 + m % 4, 96 * g:96 * g + 96], kt[:, m, g, :],
                                    vpad[:, m, 2 * g:2 * g + 2, :, :].rearrange("p q a d -> p (q a d)"), start=True, stop=True)
                mm.then_inc(st_up, 1)

            def scores(m):
                eng.wait_ge(qdA_ok, m + 1)
                eng.wait_ge(qdP_ok, 2 * m + 2)
                if m >= 2:
                    eng.wait_ge(sc_ok, 2 * m - 2)
                for g in range(2):
                    mm = eng.matmul(ps[:, 2 * (m % 2) + g, :], qk[:, 1, g, m * P:m * P + P], qd[:, m % 2, g, :, :].rearrange("p h n -> p (h n)"),
                                    start=True, stop=True)
                mm.then_inc(sc_up, 1)

            def outputs(m):
                eng.wait_ge(state_ok if m < J // 2 else stateP_ok, 1)
                if m >= 8 and m % 4 == 0:
                    eng.wait_ge(oT2_ok, m // 4 - 1)
                o = ps[:, 4 + m // 4 % 2, (m % 4) * P:(m % 4 + 1) * P]
                for g in range(2):
                    eng.matmul(o[64 * g:64 * g + 64, :], state[:, m, g, :], qk[:, 0, g, m * P:m * P + P], start=True, stop=False,
                               skip_group_check=True)
                for g in range(2):
                    eng.wait_ge(sc_ok, 2 * m + g + 1)
                    for h in range(4):
                        q = 2 * g + h // 2
                        if h % 2 == 0:
                            mm = eng.matmul(o[32 * q:32 * q + HD, :], vpad[:, m, q, 0, :], sc[:, m % 2, g, h, :], start=False, stop=False,
                                            skip_group_check=True)
                        else:
                            mm = eng.matmul(o[32 * q:32 * q + 2 * HD, :], vpad[:, m, q, 1:3, :].rearrange("p a d -> p (a d)"),
                                            sc[:, m % 2, g, h, :], start=False, stop=True, skip_group_check=True)
                mm.then_inc(o_up, 1)

            eng.wait_ge(ktV_ok, 4)
            eng.wait_ge(ktA_ok, 4)
            for m in range(J + 1):
                if m < J:
                    scores(m)
                if m == 1:
                    eng.wait_ge(run_ok, J)
                if m >= 1:
                    outputs(m - 1)
            eng.wait_ge(oT2_ok, 4)
            for j in range(J):
                mm = eng.matmul(ps[:, 6, j:j + 1], oT2[:, :, j], ones[:, 0:1], start=True, stop=True)
            mm.then_inc(ssq_up, 1)
            eng.wait_ge(yT_ok, 4)
            eng.wait_ge(sc_ok, 2 * J)
            for j in range(J):
                mm = eng.matmul(ps[:, j // 4, (j % 4) * P:(j % 4 + 1) * P], yT[:, :, j], wo1_g[:, :], start=True, stop=True)
                if j % 4 == 3:
                    mm.then_inc(attn_up, 1)

            eng.wait_ge(x_ok, 12)
            for j in range(J):
                z_ready(eng, 4, j // 4)
                mm = eng.transpose(ps[:, j // 4, (j % 4) * P:(j % 4 + 1) * P], z[:, j, :], ident)
                if j % 4 == 3:
                    mm.then_inc(hT_up, 1)
            eng.wait_ge(hT_ok, 16)
            eng.wait_ge(ld_r, 64)
            for j in range(J):
                mm = eng.matmul(ps[:, 4, j * E1:j * E1 + E1], h4T[:, j * P:j * P + P], rw[:, :], start=True, stop=True)
            mm.then_inc(logit_up, 1)

            def up_e(e, u, rnd):
                wait_if(eng, ld_e[u], 16 * (rnd + 1))
                for b in range(4):
                    wait_if(eng, hid_ok, 4 * e - 3 + b)
                    eng.matmul(ps[:, b, :], ew1[:, u, :], h4T[:, 512 * b:512 * b + 512], start=True, stop=True).then_inc(eu_up, 1)

            def down_e(e, u, rnd):
                eng.wait_ge(ew2g_ok, e + 1)
                for b in range(4):
                    eng.wait_ge(hid_ok, 4 * e + b + 1)
                    eng.wait_ge(accb_ok, 4 * e + 1 + b)
                    for j in range(4 * b, 4 * b + 4):
                        mm = eng.matmul(ps[:, 4 + b, (j % 4) * P:(j % 4 + 1) * P], hid[:, u, j * P:j * P + P], ew2g[:, u, :], start=True, stop=True)
                    mm.then_inc(edb_up, 1)

            up_e(*expert_of(0, -1, 0))
            eng.wait_ge(cw_ok, 1)
            for j in range(J):
                mm = eng.transpose(ps[0:E1 + 1, 4 + j // 4, (j % 4) * P:(j % 4 + 1) * P], cw[:, j, :], ident)
            mm.then_inc(cwT_up, 1)
            eng.wait_ge(cwT_ok, 4)
            eng.wait_ge(b2g_ok, 1)
            for j in range(J):
                mm = eng.matmul(ps[:, 4 + j // 4, (j % 4) * P:(j % 4 + 1) * P], cwT[:, j, :], b2g[:, :], start=True, stop=True)
            mm.then_inc(base_up, 1)
            eng.wait_ge(accb_ok, 4)
            for v in range(2):
                up_e(*expert_of(0, v, 0))
                down_e(*expert_of(0, v, 1))
            with eng.Fori(1, (E1 - 1) // 2) as it:
                for v in range(2):
                    up_e(*expert_of(it, v, 0))
                    down_e(*expert_of(it, v, 1))
            up_e(*expert_of(0, E1 - 1, 0))
            down_e(*expert_of(0, E1 - 1, 1))
            down_e(*expert_of(0, E1, 1))

        @block.vector
        def _(eng):
            seq = Chain(eng, dve_seq)

            def layer_norm(n, fetch):
                for b in range(5):
                    if b < 4:
                        fetch(b)
                        for j in range(4 * b, 4 * b + 4):
                            ins = eng.bn_stats(stats[:, j, :], x[:, j, :])
                        seq(ins)
                        for j in range(4 * b, 4 * b + 4):
                            ins = eng.bn_aggr(mv[:, j, :], stats[:, j, :])
                        seq(ins)
                        eng.tensor_scalar(var_eps[:, 4 * b:4 * b + 4], mv[:, 4 * b:4 * b + 4, 1], EPS_LN, None, ALU.add).then_inc(var_ok, 1)
                    if b >= 1:
                        js = slice(4 * b - 4, 4 * b)
                        eng.wait_ge(std_ok, 4 * (n - 1) + b)
                        seq(eng.reciprocal(rstd[:, js], std[:, js]))
                        eng.scalar_tensor_tensor(out=nmr[:, js], in0=mv[:, js, 0], scalar=-1.0, in1=rstd[:, js], op0=ALU.mult,
                                                 op1=ALU.mult).then_inc(nmr_ok, 1)
                        for j in range(4 * b - 4, 4 * b - 2):
                            eng.tensor_scalar(z[:, j, :], x[:, j, :], mv[:, j, 0:1], rstd[:, j:j + 1], ALU.subtract, ALU.mult).then_inc(zV_ok, 1)

            eng.wait_ge(cols_up, 1)
            eng.tensor_copy(cols[:, 0:2], ps[:, 0, 0:2]).then_inc(cols_ok, 1)
            eng.wait_ge(silu_ok, 1)
            eng.wait_ge(fill_ok, 1)
            for l in range(2):
                eng.tensor_scalar(silu_cb[:, l, :], ones[:, :], silu_c[:, l:l + 1], None, ALU.mult).then_inc(silub_ok, 1)
            layer_norm(1, lambda b: eng.wait_ge(ld_x[b // 2], 16))
            eng.wait_ge(mod_up, 1)
            mc = modc[:, :, :].rearrange("p l k -> p (l k)")
            seq(eng.tensor_copy(mc, ps[:, 1, 0:8]))
            seq(eng.tensor_scalar(mc[:, 1::2], mc[:, 1::2], 1.0, None, ALU.add))
            eng.tensor_scalar(sa128[:, :], modc[:, 0, 0:1], float(P), None, ALU.mult).then_inc(modc_ok, 1)
            eng.wait_ge(mod_up, 2)
            g4 = lambda t: t[:, :, :, :].rearrange("p l k c -> p (l k c)")
            seq(eng.tensor_scalar(g4(gsign), ps[:, 2, :], 0.0, 2.0, ALU.is_ge, ALU.mult))
            seq(eng.tensor_scalar(g4(gneg), ps[:, 2, :], -1.0, 0.25, ALU.mult, ALU.max))
            seq(eng.tensor_tensor(g4(gmag), ps[:, 2, :], g4(gneg), ALU.max))
            eng.scalar_tensor_tensor(out=g4(gate), in0=g4(gsign), scalar=-1.0, in1=g4(gmag), op0=ALU.add, op1=ALU.mult).then_inc(gate_ok, 1)
            eng.wait_ge(gate_ok, 1)
            eng.wait_ge(wT_up, 1)
            eng.tensor_tensor(wo1_g[:, :], ps[:, 4, 0:C], gate[:, 1, 0, :], ALU.mult).then_inc(wo1_ok, 1)
            eng.wait_ge(cols_up, 2)
            eng.tensor_copy(cols[:, 2:NROWS], ps[:, 5, 2:NROWS]).then_inc(cols_ok, 1)
            for b in range(1, 4, 2):
                eng.wait_ge(hT_up, b + 1)
                eng.tensor_scalar(hT[:, :, 4 * b:4 * b + 4], ps[:, b, :].rearrange("c (j m) -> c m j", m=P), modc[:, 0, 1:2],
                                  None, ALU.mult).then_inc(hT_ok, 1)
            eng.wait_ge(hT_ok, 4)
            eng.wait_ge(modc_ok, 1)
            eng.tensor_scalar(hTf[:, 0:J], hTf[:, 0:J], sa128[:, 0:1], None, ALU.add).then_inc(hT_all, 1)
            for b in range(4):
                eng.wait_ge(qk_up, 4 + b + 1)
                eng.tensor_copy(kT[:, 512 * b:512 * b + 512], ps[:, 4 + b, :]).then_inc(k_ok, 1)
            copy = lambda o, i: eng.tensor_copy(o, i)
            eng.wait_ge(prod_up, 1)
            for i in range(2, 4):
                for q in range(4):
                    take_prod(copy, i, q).then_inc(prod_ok, 1)
            eng.wait_ge(lagf_up, 1)
            eng.tensor_copy(lag_f[:, :], ps[0:NS, 0, 0:96]).then_inc(lagf_ok, 1)
            eng.wait_ge(lag_up, 1)
            eng.tensor_copy(lag[:, :], ps[:, 1, 0:J]).then_inc(lag_ok, 1)
            eng.wait_ge(lag_up, 2)
            seq(eng.tensor_copy(lagT[:, :], ps[0:J, 2, 0:P]))

            def largest(dst, src, w1, w2):
                seq(eng.max(dst[:, 0:8], src))
                seq(eng.match_replace(w1, dst[:, 0:8], src, NEG))
                seq(eng.max(dst[:, 8:16], w1))
                seq(eng.match_replace(w2, dst[:, 8:16], w1, NEG))
                seq(eng.max(dst[:, 16:24], w2))

            largest(cand, lagT[:, :], lagW[:, :], lagX[:, :])
            eng.tensor_tensor(cand_d[:, :, :], tb("blk16").rearrange("a (b c) -> a b c", c=24),
                              cand[:, None, :].to_broadcast([J, J, 24]), ALU.mult).then_inc(candd_ok, 1)
            eng.wait_ge(call_up, 1)
            seq(eng.tensor_copy(call[:, :], ps[:, 3, 0:J * 24]))
            largest(best, call[:, :], callW[:, :], callX[:, :])
            thr = best[:, TOPK - 1:TOPK]
            seq(eng.tensor_scalar(above[:, :], lag[:, :], thr, None, ALU.is_gt))
            seq(eng.tensor_scalar(equal[:, :], lag[:, :], thr, None, ALU.is_equal))
            seq(eng.tensor_reduce(n_above[:, :], above[:, :], AX.X, ALU.add))
            eng.tensor_tensor_scan(eq_run[:, :], ones[:, 0:J], equal[:, :], 0.0, ALU.mult, ALU.add).then_inc(cnt_ok, 1)
            eng.wait_ge(cnt_ok, 1)
            eng.wait_ge(cnt_up, 1)
            seq(eng.tensor_copy(n_before[:, :], ps[:, 0, 0:1]))
            seq(eng.tensor_scalar(keep[:, :], eq_run[:, :], n_before[:, 0:1], TOPK + 0.5, ALU.add, ALU.is_le))
            seq(eng.tensor_tensor(keep2[:, :], keep[:, :], equal[:, :], ALU.mult))
            seq(eng.tensor_tensor(keep3[:, :], keep2[:, :], above[:, :], ALU.add))
            eng.tensor_tensor(gx[:, J:2 * J], keep3[:, :], lag[:, :], ALU.mult).then_inc(g_ok, 1)
            eng.wait_ge(gprev_up, 1)
            eng.tensor_copy(gx[:, 0:J], ps[:, 1, 0:J]).then_inc(gx_ok, 1)
            eng.wait_ge(gh_up, 1)
            eng.tensor_copy(gh[:, :], ps[0:96, 2, 0:NS]).then_inc(gh_ok, 1)
            eng.wait_ge(toep_up, 1)
            eng.wait_ge(fill_ok, 3)
            for i in range(4):
                for q in range(2, 4):
                    take_toep(copy, i, q).then_inc(gb_ok, 1)
            for b in range(1, 4, 2):
                eng.wait_ge(aT_up, b + 1)
                eng.tensor_copy(aTf[:, 512 * b:512 * b + 512], ps[:, 4 + b, :]).then_inc(aT_ok, 1)
            for b in range(1, 4, 2):
                eng.wait_ge(oh_up, b + 1)
                eng.tensor_copy(oh[:, 4 * b:4 * b + 4, :], ps[:, b, :]).then_inc(oh_ok, 1)
            eng.wait_ge(xb_ok, 1)

            def add_attention(b):
                eng.wait_ge(attn_up, b + 1)
                eng.tensor_tensor(x[:, 4 * b:4 * b + 4, :], ps[:, 4 + b, :], x[:, 4 * b:4 * b + 4, :], ALU.add).then_inc(x_ok, 1)
                eng.wait_ge(x_ok, b + 1)

            layer_norm(2, add_attention)
            for b in range(1, 4, 2):
                eng.wait_ge(hT_up, 4 + b + 1)
                eng.tensor_scalar(h2T[:, 512 * b:512 * b + 512], ps[:, b, :], modc[:, 0, 3:4], modc[:, 0, 2:3], ALU.mult,
                                  ALU.add).then_inc(hT_ok, 1)
            eng.wait_ge(score_up, 1)
            seq(eng.tensor_tensor(score[:, :, :], ps[:, 4, 0:J * E0].rearrange("p (j e) -> p j e", e=E0),
                                  bg_b[:, None, :].to_broadcast([P, J, E0]), ALU.add))
            seq(eng.tensor_reduce(smax[:, :], score[:, :, :], AX.X, ALU.max))
            seq(eng.tensor_tensor(hit[:, :, :], score[:, :, :], smax[:, :, None].to_broadcast([P, J, E0]), ALU.is_equal))
            seq(eng.tensor_tensor(rank[:, :, :], hit[:, :, :], tb("last")[:, None, :].to_broadcast([P, J, E0]), ALU.mult))
            seq(eng.tensor_reduce(rmax[:, :], rank[:, :, :], AX.X, ALU.max))
            eng.tensor_tensor(choice[:, :, :].rearrange("p e j -> p j e"), rank[:, :, :],
                              rmax[:, :, None].to_broadcast([P, J, E0]), ALU.is_equal).then_inc(choice_ok, 1)
            eng.wait_ge(count_up, 1)
            seq(eng.tensor_copy(total[:, :], ps[:, 6, 0:P]))
            seq(eng.tensor_tensor_scan(run_in[:, :], ones[:, 0:E0 * J], total[:, :], 0.0, ALU.mult, ALU.add))
            seq(eng.tensor_tensor(run_ex[:, :], run_in[:, :], total[:, :], ALU.subtract))
            seq(eng.tensor_tensor(count[:, :], run_in[:, J - 1::J], run_ex[:, 0::J], ALU.subtract))
            seq(eng.tensor_tensor(over[:, :, :], count[:, :, None].to_broadcast([P, E0, J]),
                                  tb("steps")[:, None, :].to_broadcast([P, E0, J]), ALU.is_gt))
            seq(eng.tensor_reduce(nblk[:, :], over[:, :, :], AX.X, ALU.add))
            seq(eng.tensor_tensor_scan(bend[:, :], ones[:, 0:E0], nblk[:, :], 0.0, ALU.mult, ALU.add))
            seq(eng.tensor_tensor(bstart[:, :], bend[:, :], nblk[:, :], ALU.subtract))
            seq(eng.scalar_tensor_tensor(out=shift[:, :], in0=bstart[:, :], scalar=float(P), in1=run_ex[:, 0::J],
                                         op0=ALU.mult, op1=ALU.subtract))
            flat = lambda t: t[:, :, :].rearrange("p e j -> p (e j)")
            seq(eng.tensor_tensor(flat(place), ps[:, 5, 0:P], run_ex[:, :], ALU.add))
            seq(eng.tensor_tensor(place2[:, :, :], place[:, :, :], shift[:, :, None].to_broadcast([P, E0, J]), ALU.add))
            seq(eng.tensor_tensor(place3[:, :, :], place2[:, :, :], choice[:, :, :], ALU.mult))
            seq(eng.tensor_reduce(slot_f[:, :], place3[:, :, :].rearrange("p e j -> p j e"), AX.X, ALU.add))
            eng.tensor_copy(slot[:, :], slot_f[:, :]).then_inc(slot_ok, 1)
            seq(eng.tensor_scalar(past[:, :], bend[:, :], tb("pidx")[:, 0:1], None, ALU.is_le))
            seq(eng.tensor_reduce(bexp[:, :], past[:, :], AX.X, ALU.add))
            seq(eng.tensor_scalar(bexp_c[:, :], bexp[:, :], E0 - 1.0, None, ALU.min))
            eng.tensor_scalar(bhot[:, :], tb("eidx"), bexp_c[:, 0:1], None, ALU.is_equal).then_inc(bexp_ok, 1)
            eng.wait_ge(bexp_up, 1)
            eng.tensor_copy(bexpT[:, :], ps[0:1, 0, 0:P]).then_inc(bexp_ok, 1)
            eng.tensor_copy(bhotT[:, :], ps[0:E0, 1, 0:P]).then_inc(bhotT_ok, 1)
            eng.wait_ge(b1all_up, 1)
            eng.tensor_copy(b1all[:, :, :].rearrange("p b k -> p k b"), ps[:, 7, :].rearrange("p (k b) -> p k b", k=HC)).then_inc(b1all_ok, 1)

            phase = tb("phase")

            def angles(g):
                for k in range(T // (2 * C)):
                    cut = slice(k * 2 * C, (k + 1) * 2 * C)
                    ins = eng.tensor_scalar(ang[:, cut], pos[:, :], float(k * 2 * C), cols[:, ROW_TH + g:ROW_TH + g + 1], ALU.add, ALU.mult)
                seq(ins)
                seq(eng.tensor_scalar(part, ang, INV_2PI, phase[:, 1:2], ALU.mult, ALU.add))
                seq(eng.tensor_scalar(turns, part, ROUND, ROUND, ALU.add, ALU.subtract))
                for piece in TWO_PI:
                    seq(eng.scalar_tensor_tensor(out=ang, in0=turns, scalar=-piece, in1=ang, op0=ALU.mult, op1=ALU.add))
                seq(eng.tensor_scalar(ang, ang, phase[:, 0:1], PI_IN, ALU.add, ALU.min))
                eng.tensor_scalar(ang, ang, -PI_IN, None, ALU.max).then_inc(ang_ok, 1)

            eng.wait_ge(pos_ok, 1)
            angles(0)
            eng.wait_ge(trig_ok, 1)

            def scale_x(b, slot_, rnd):
                u = slot_ % 2
                wait_if(eng, xT_up, b + 1)
                wait_if(eng, h_up, b - 1)
                eng.tensor_scalar(xTb[:, u, :], ps[:, u, 0:P], modc[:, 0, 3:4], modc[:, 0, 2:3], ALU.mult, ALU.add).then_inc(xT_ok, 1)
                wait_if(eng, hA_ok, b - 1)
                wait_if(eng, hV_ok, b - 1)
                eng.tensor_copy(b1b[:, u, :], b1all[:, bass.ds(b, 1), :].rearrange("p b k -> p (b k)")).then_inc(b1_ok, 1)

            def relu_v(b, slot_, rnd):
                u = slot_ % 2
                wait_if(eng, h_up, b + 1)
                wait_if(eng, b1_ok, b + 1)
                wait_if(eng, y_up, b - 1)
                for k in range(2, HC):
                    r = eng.tensor_scalar(hb[:, u, k * P:k * P + P], ps[:, 6 + u, k * P:k * P + P], b1b[:, u, k:k + 1], 0.0, ALU.add, ALU.max)
                r.then_inc(hV_ok, 1)

            def gate_y(b, slot_, rnd):
                u = slot_ % 2
                wait_if(eng, y_up, b + 1)
                wait_if(eng, st_y[slot_], 16 * rnd)
                eng.tensor_tensor(yb[:, slot_, :], ps[:, 4 + u, 0:C], gate[:, 0, 1, :], ALU.mult).then_inc(y_ok, 1)

            eng.wait_ge(b1all_ok, 1)
            scale_x(*block_of(0, -3, 0))
            scale_x(*block_of(0, -2, 0))
            relu_v(*block_of(0, -2, 1))
            for v in (-1,):
                scale_x(*block_of(0, v, 0))
                relu_v(*block_of(0, v, 1))
                gate_y(*block_of(0, v, 2))
            for v in range(4):
                scale_x(*block_of(0, v, 0))
                relu_v(*block_of(0, v, 1))
                gate_y(*block_of(0, v, 2))
            with eng.Fori(1, (NB0 - 3) // 4) as it:
                for v in range(4):
                    scale_x(*block_of(it, v, 0))
                    relu_v(*block_of(it, v, 1))
                    gate_y(*block_of(it, v, 2))
            relu_v(*block_of(0, NB0 - 3, 1))
            gate_y(*block_of(0, NB0 - 3, 2))
            gate_y(*block_of(0, NB0 - 2, 2))
            angles(1)
            eng.wait_ge(decay_ok0, 1)
            seq(eng.tensor_scalar(decay_v[:, :, :], decay[:, :, None].to_broadcast([P, HEADS, HD]), -1.0, None, ALU.add))
            hm = tb("head")
            eng.tensor_tensor(decay_h[:, :, :], decay_v[:, :, :].rearrange("p (g h) d -> p g (h d)", g=2), hm[:, None, :].to_broadcast([P, 2, 64]),
                              ALU.mult).then_inc(decay_ok, 1)

            def add_experts(b):
                eng.wait_ge(got[b], 4 * 16)
                eng.tensor_tensor(x[:, 4 * b:4 * b + 4, :], x[:, 4 * b:4 * b + 4, :], yg[:, 4 * b:4 * b + 4, :], ALU.add).then_inc(x_ok, 1)
                eng.wait_ge(x_ok, 4 + b + 1)

            layer_norm(3, add_experts)
            for b in range(1, 4, 2):
                eng.wait_ge(hT_up, 8 + b + 1)
                eng.tensor_scalar(hT3[:, :, 4 * b:4 * b + 4], ps[:, b, :].rearrange("c (j p) -> c p j", p=P), modc[:, 1, 1:2],
                                  modc[:, 1, 0:1], ALU.mult, ALU.add).then_inc(hT_ok, 1)
            eng.wait_ge(trig_ok, 2)
            for n in range(16):
                w, g, b = 1 - n // 8, n // 4 % 2, n % 4
                if b < 3:
                    eng.wait_ge(act4_ok, n + 1)
                    eng.tensor_tensor(qk[:, w, g, 512 * b:512 * b + 512], act4[:, b, :], trig[:, g, 512 * b:512 * b + 512], ALU.mult).then_inc(qkV_ok, 1)
            eng.wait_ge(qkV_ok, 12)
            eng.wait_ge(qkP_ok, 4)
            for b in range(4):
                eng.wait_ge(v_up, b + 1)
                for odd in range(2):
                    pair = lambda t: t.rearrange("p (q a d) -> p q a d", q=4, a=2)[:, :, odd, :]
                    eng.tensor_tensor(vpad[:, 4 * b:4 * b + 4, :, 2 * odd, :],
                                      ps[:, 4 + b, :].rearrange("p (m q a d) -> p m q a d", m=4, q=4, a=2)[:, :, :, odd, :],
                                      pair(v_b[:, :])[:, None, :, :].to_broadcast([P, 4, 4, HD]), ALU.add).then_inc(v_ok, 1)
            for n in range(1, 8, 2):
                eng.wait_ge(kt_up, n + 1)
                eng.tensor_copy(kt[:, 2 * n:2 * n + 2, :, :], ps[:, n % 4, :]).then_inc(ktV_ok, 1)
            seq(eng.memset(run[:, 0, :, :], 0.0))
            for m in range(J):
                eng.wait_ge(st_up, m + 1)
                if m:
                    eng.wait_ge(run_ok, m)
                eng.tensor_tensor(run[:, m + 1, :, :].rearrange("p g (q a d) -> p (g q) a d", q=2, a=2),
                                  ps[:, 4 + m % 4, 0:192].rearrange("p (q a d) -> p q a d", q=4, a=3)[:, :, 0:3:2, :],
                                  run[:, m, :, :].rearrange("p g (q a d) -> p (g q) a d", q=2, a=2), ALU.add).then_inc(run_ok, 1)
            eng.wait_ge(run_ok, J)
            eng.tensor_tensor(total_s[:, :, :], run[:, J, :, :], hm[:, None, :].to_broadcast([P, 2, 64]), ALU.mult).then_inc(total_ok, 1)
            early = run[:, 0:J // 2, :, :].rearrange("p m g c -> p m (g c)")
            seq(eng.tensor_tensor(early, early, decay_h[:, :, :].rearrange("p g c -> p (g c)")[:, None, :].to_broadcast([P, J // 2, C]), ALU.mult))
            eng.wait_ge(total_ok, 1)
            eng.tensor_tensor(state[:, 0:J // 2, :, :].rearrange("p m g c -> p m (g c)"), early,
                              total_s[:, :, :].rearrange("p g c -> p (g c)")[:, None, :].to_broadcast([P, J // 2, C]), ALU.add).then_inc(state_ok, 1)

            def mask(m):
                eng.wait_ge(sc_up, m + 1)
                if m >= 2:
                    eng.wait_ge(o_up, m - 1)
                for g in range(2):
                    eng.tensor_tensor(sc[:, m % 2, g, :, :], ps[:, 2 * (m % 2) + g, :].rearrange("p (h n) -> p h n", h=4),
                                      cmask[:, 4 * g:4 * g + 4, :], ALU.mult).then_inc(sc_ok, 1)

            eng.wait_ge(cmask_ok, 1)
            for m in range(J + 3):
                if m < J:
                    mask(m)
                if m % 4 == 2 and m > 4:
                    b = m // 4 - 1
                    eng.wait_ge(oT_ok, b + 1)
                    eng.tensor_tensor(yT[:, 32 * b:32 * b + 32, :], oT[:, 512 * b:512 * b + 512], uT[:, 512 * b:512 * b + 512], ALU.mult).then_inc(yT_ok, 1)
            eng.wait_ge(ssq_up, 1)
            eng.tensor_scalar(msq[:, :], ps[:, 6, 0:J], 1.0 / C, EPS_RMS, ALU.mult, ALU.add).then_inc(msq_ok, 1)
            eng.wait_ge(rms_ok, 1)
            seq(eng.reciprocal(irms[:, :], rms[:, :]))
            eng.wait_ge(xb_ok, 2)

            def add_linear_attention(b):
                eng.wait_ge(attn_up, 4 + b + 1)
                for j in range(4 * b, 4 * b + 4):
                    r = eng.scalar_tensor_tensor(out=x[:, j, :], in0=ps[:, b, (j % 4) * P:(j % 4 + 1) * P], scalar=irms[:, j:j + 1], in1=x[:, j, :],
                                                 op0=ALU.mult, op1=ALU.add)
                r.then_inc(x_ok, 1)
                eng.wait_ge(x_ok, 8 + b + 1)

            layer_norm(4, add_linear_attention)
            for b in range(1, 4, 2):
                eng.wait_ge(hT_up, 12 + b + 1)
                eng.tensor_scalar(h4T[:, 512 * b:512 * b + 512], ps[:, b, :], modc[:, 1, 3:4], modc[:, 1, 2:3], ALU.mult, ALU.add).then_inc(hT_ok, 1)
            eng.wait_ge(logit_up, 1)
            seq(eng.memset(cw[:, :, E1:E1 + 1], 1.0))
            wide = [P, J, E1]
            seq(eng.tensor_tensor(logit[:, :, :], ps[:, 4, 0:J * E1].rearrange("p (j e) -> p j e", e=E1), rb_b[:, None, :].to_broadcast(wide), ALU.add))
            seq(eng.tensor_reduce(lmax[:, :], logit[:, :, :], AX.X, ALU.max))
            eng.tensor_tensor(ldiff[:, :, :], logit[:, :, :], lmax[:, :, None].to_broadcast(wide), ALU.subtract).then_inc(ldiff_ok, 1)
            eng.wait_ge(lexp_ok, 1)
            seq(eng.tensor_reduce(lsum[:, :], lexp[:, :, :], AX.X, ALU.add))
            seq(eng.reciprocal(lrec[:, :], lsum[:, :]))
            seq(eng.tensor_tensor(prob[:, :, :], lexp[:, :, :], lrec[:, :, None].to_broadcast(wide), ALU.mult))
            src = prob
            for n in range(TOP1):
                seq(eng.tensor_reduce(pmax[:, :], src[:, :, :], AX.X, ALU.max))
                seq(eng.tensor_tensor(phit[:, :, :], src[:, :, :], pmax[:, :, None].to_broadcast(wide), ALU.is_equal))
                seq(eng.tensor_tensor(prank[:, :, :], phit[:, :, :], tb("last1")[:, None, :].to_broadcast(wide), ALU.mult))
                seq(eng.tensor_reduce(prmax[:, :], prank[:, :, :], AX.X, ALU.max))
                seq(eng.tensor_tensor(pick[:, :, :], prank[:, :, :], prmax[:, :, None].to_broadcast(wide), ALU.is_equal))
                seq(eng.scalar_tensor_tensor(out=left[:, :, :], in0=pick[:, :, :], scalar=-2.0, in1=src[:, :, :], op0=ALU.mult, op1=ALU.add))
                src = left
            eng.scalar_tensor_tensor(out=cw[:, :, 0:E1], in0=left[:, :, :], scalar=0.0, in1=prob[:, :, :], op0=ALU.is_lt, op1=ALU.mult).then_inc(cw_ok, 1)
            eng.wait_ge(cwT_up, 1)
            for b in range(4):
                eng.tensor_copy(cwT[:, 4 * b:4 * b + 4, :], ps[0:E1 + 1, 4 + b, :].rearrange("e (j p) -> e j p", p=P)).then_inc(cwT_ok, 1)
            eng.wait_ge(base_up, 1)
            for b in range(4):
                eng.tensor_tensor(x[:, 4 * b:4 * b + 4, :], ps[:, 4 + b, :], x[:, 4 * b:4 * b + 4, :], ALU.add).then_inc(accb_ok, 1)

            def add_e(e, u, rnd):
                for b in range(4):
                    eng.wait_ge(edb_up, 4 * e + b + 1)
                    for j in range(4 * b, 4 * b + 4):
                        col = e if isinstance(e, int) else None
                        w = cw[:, j, e:e + 1] if isinstance(e, int) else cw[:, j, bass.ds(e, 1)]
                        r = eng.scalar_tensor_tensor(out=x[:, j, :], in0=ps[:, 4 + b, (j % 4) * P:(j % 4 + 1) * P], scalar=w, in1=x[:, j, :],
                                                     op0=ALU.mult, op1=ALU.add)
                    r.then_inc(accb_ok, 1)
                eng.wait_ge(accb_ok, 4 * e + 8)

            eng.wait_ge(accb_ok, 4)
            for v in range(2):
                add_e(*expert_of(0, v, 1))
            with eng.Fori(1, (E1 - 1) // 2) as it:
                for v in range(2):
                    add_e(*expert_of(it, v, 1))
            add_e(*expert_of(0, E1 - 1, 1))
            add_e(*expert_of(0, E1, 1))


OUT = (1, T, C)


def kernel(**inputs):
    import concourse.bacc as bacc
    from concourse.bass_utils import run_bass_kernel_spmd

    nc = bacc.Bacc("TRN2", target_bir_lowering=False, num_devices=1)
    arrays, aps = {}, {}
    for name, v in (*inputs.items(), ("table", TABLE)):
        v = np.ascontiguousarray(v)
        arrays[name] = v
        aps[name] = nc.dram_tensor(name, v.shape, mybir.dt.from_np(v.dtype), kind="ExternalInput").ap()
    out = nc.dram_tensor("out", OUT, F32, kind="ExternalOutput").ap()
    build(nc, aps, out)
    got = run_bass_kernel_spmd(nc, [arrays], core_ids=[0])
    return got.results[0]["out"]
```

```python
from contextlib import ExitStack

import numpy as np
import concourse.bass as bass
from concourse import mybir

F32 = mybir.dt.float32
I32 = mybir.dt.int32
F32R = mybir.dt.float32r
ALU = mybir.AluOpType
ACT = mybir.ActivationFunctionType
AX = mybir.AxisListType

P = 128
C = 128
T = 2048
J = T // P
NS = P // 2
NG = NS // 4
TOPK = int(3 * np.log(T))
EPS_LN = 1e-5
NEG = -3.0e38
E0, H0 = 8, 512
HC = H0 // P
NB0 = T // P + E0 - 1
HEADS, HD = 8, 16
E1, TOP1 = 15, 3
EPS_RMS = 1e-6
TWO_PI = [6.28125, float(np.float32(np.round((2 * np.pi - 6.28125) * 2**20) / 2**20))]
TWO_PI.append(float(np.float32(2 * np.pi - TWO_PI[0] - TWO_PI[1])))
INV_2PI = float(np.float32(0.5 / np.pi))
ROUND = 1.5 * 2.0**23
WHOLE3 = 2
HIGH = -4096
PI_IN = 3.1415925


class Chain:

    def __init__(self, eng, sem):
        self.eng, self.sem, self.n = eng, sem, 0

    def note(self, ins):
        self.n += 1
        ins.then_inc(self.sem, 1)
        return self.n

    def wait(self, n):
        self.eng.wait_ge(self.sem, n)

    def __call__(self, ins):
        self.wait(self.note(ins))


def shape_constants():
    p, b = np.arange(P), np.arange(NS)
    ang = 2 * np.pi * np.outer(p, b) / P
    nyq = np.cos(np.pi * p)
    dft = np.zeros((P, NS, 2))
    dft[:, :, 0], dft[:, :, 1] = np.cos(ang), -np.sin(ang)
    dft[:, 0, 1] = nyq
    idft = np.zeros((NS, 2, P))
    idft[:, 0], idft[:, 1] = 2 * np.cos(ang.T) / P, -2 * np.sin(ang.T) / P
    idft[0, 0], idft[0, 1] = 1 / P, nyq / P
    diag = np.zeros((4, 2, J, 2, 4, 3, 32))
    toep = np.zeros((3, 32, 2, 4, 4, 2, J))
    for a in range(J):
        for c in range(J):
            for r1, r2, kind, v in ((0, 0, 0, 1), (1, 1, 1, 1), (1, 0, 2, 1), (0, 1, 2, -1)):
                diag[c % 4, r1, a, r2, c // 4, kind, a - c + 16] = v
                toep[kind, a - c + 16, r2, c // 4, c % 4, r1, a] = 1 if kind < 2 else -v
    corr = np.zeros((NS, 2, 3, P))
    for half, d in ((0, p + 1), (1, p)):
        a2 = 2 * np.pi * np.outer(b, d) / P
        corr[:, half, 0] = corr[:, half, 1] = 2 * np.cos(a2)
        corr[:, half, 2] = -2 * np.sin(a2)
        corr[0, half, 0], corr[0, half, 1], corr[0, half, 2] = 1, np.cos(np.pi * d), 0
    corr /= P * C
    gdft = np.zeros((P, 3, NS))
    gdft[:, 0] = gdft[:, 1] = np.cos(ang)
    gdft[:, 2] = np.sin(ang)
    gdft[:, 1, 0] = nyq
    ident = np.eye(P)
    before = np.triu(np.ones((P, P)), 1)
    prev = np.roll(np.eye(P), 1, axis=1)
    blk16 = np.repeat(np.eye(J), 24, axis=1)
    causal = np.triu(np.ones((P, P)))
    head = np.repeat(np.repeat(np.eye(4), 32, axis=0), HD, axis=1)
    phase = np.tile(np.repeat([[np.pi / 2, 0.25], [0, 0]], HD, axis=0), (4, 1))
    last = np.tile(8.0 - np.arange(8), (P, 1))
    steps = np.tile(128.0 * np.arange(J), (P, 1))
    pidx = np.arange(P, dtype=float)[:, None]
    eidx = np.tile(np.arange(E0, dtype=float), (P, 1))
    parts = dict(ident=ident, dft=dft.reshape(P, P), idft=idft.reshape(P, P), corr=corr.reshape(NS, -1),
                 diag=diag.reshape(P, -1), before=before, prev=prev, blk16=blk16, gdft=gdft.reshape(P, -1),
                 toep=toep.reshape(96, -1), causal=causal, head=head, phase=phase,
                 last=last, steps=steps, pidx=pidx, eidx=eidx)
    first = ("ident", "dft")
    cols, at = {}, 0
    for n in (*first, *(k for k in parts if k not in first)):
        cols[n] = (at, parts[n].shape)
        at += parts[n].shape[1]
    table = np.zeros((P, at), np.float32)
    for n, (a, (r, w)) in cols.items():
        table[:r, a:a + w] = parts[n]
    return table, cols


TABLE, COLS = shape_constants()
NFIRST = COLS["dft"][0] + P

ROW_C0, ROW_C1, ROW_SB1, ROW_EB1 = 0, 1, 2, 3
ROW_QB = ROW_EB1 + E1
ROW_KB = ROW_QB + 2
ROW_TH = ROW_KB + 2
ROW_UB = ROW_TH + 2
NROWS = ROW_UB + 1


def build(nc, a, out):
    ctx = ExitStack()
    with ctx:
        def sb(name, shape, dt=F32):
            return ctx.enter_context(nc.sbuf_tensor(name, shape, dt))

        def sem(name):
            return ctx.enter_context(nc.semaphore(name))

        tab = sb("tab", [P, TABLE.shape[1]])

        def tb(name):
            at, (r, w) = COLS[name]
            return tab[0:r, at:at + w]

        ident, dft, idft, before, prev = (tb(n) for n in ("ident", "dft", "idft", "before", "prev"))
        rows = sb("rows", [NROWS, C])
        cols = sb("cols", [P, NROWS])
        wmod = sb("wmod", [P, 2, 6 * C])
        silu_c = sb("silu_c", [P, 2])
        silu_cb = sb("silu_cb", [P, 2, P])
        ones = sb("ones", [P, P])
        modc = sb("modc", [P, 2, 4])
        gate = sb("gate", [P, 2, 2, C])
        space_d = sb("space_d", [P, T])
        gsign, gneg, gmag = (space_d[:, 512 * k:512 * k + 512].rearrange("p (l k c) -> p l k c", l=2, k=2) for k in range(3))
        x = sb("x", [P, J, C])
        z_id = sb("z_id", [P, J * (C + 1)])
        by_token = lambda t: t.rearrange("p (j c) -> p j c", c=C + 1)
        z = by_token(z_id[:, :])[:, :, 0:C]
        stats = sb("stats", [P, J, 6])
        mv = sb("mv", [P, J, 2])
        var_eps = sb("var_eps", [P, J])
        std = sb("std", [P, J])
        rstd = sb("rstd", [P, J])
        nmr = sb("nmr", [P, J])
        hT = sb("hT", [P, P, J])
        hTf = hT[:, :, :].rearrange("c m j -> c (m j)")
        wqkvo = sb("wqkvo", [P, 4, C])
        brow = sb("brow", [1, 3, C])
        bo_b = sb("bo_b", [P, C])
        ind = sb("ind", [1, P])
        sa128 = sb("sa128", [P, 1])
        with nc.sbuf_tensor("space_a", [P, 4 * T], F32) as space_a:
            pass
        space_r = sb("space_r", [P, 4 * T], F32R)
        qT = space_a[:, 0:T]
        kT = space_a[:, T:2 * T]
        v0 = space_a[:, 2 * T:3 * T].rearrange("p (g c) -> p g c", c=C)
        prod = sb("prod", [P, 8, NS])
        lag_f = sb("lag_f", [NS, 96])
        lag = sb("lag", [P, J])
        lagT = sb("lagT", [J, P])
        lagW = sb("lagW", [J, P])
        lagX = sb("lagX", [J, P])
        cand = sb("cand", [J, 24])
        cand_d = sb("cand_d", [J, J, 24])
        with nc.sbuf_tensor("space_c", [P, 17 * 2 * C], F32) as space_c:
            pass
        space_cr = sb("space_cr", [P, 17 * 2 * C], F32R)
        call, callW, callX = (space_c[:, k * J * 24:(k + 1) * J * 24] for k in range(3))
        best = sb("best", [P, 24])
        above = sb("above", [P, J])
        equal = sb("equal", [P, J])
        n_above = sb("n_above", [P, 1])
        eq_run = sb("eq_run", [P, J])
        n_before = sb("n_before", [P, 1])
        keep = sb("keep", [P, J])
        keep2 = sb("keep2", [P, J])
        keep3 = sb("keep3", [P, J])
        gx = sb("gx", [P, 2 * J])
        gh = sb("gh", [96, NS])
        gb = space_a[:, 3 * T:4 * T].rearrange("p (g m) -> p g m", m=P)
        with nc.sbuf_tensor("space_b", [P, 2 * T], F32) as space_b:
            pass
        space_br = sb("space_br", [P, 2 * T], F32R)
        aT = space_b[:, 0:T].rearrange("p (m j) -> p m j", j=J)
        aTf = space_b[:, 0:T]
        wo_g = sb("wo_g", [P, C])
        bo_g = sb("bo_g", [P, C])
        oh = space_b[:, T:2 * T].rearrange("p (j c) -> p j c", c=C)


        h2T = hTf
        wg = sb("wg", [P, E0])
        bg_b = sb("bg_b", [P, E0])
        b1rows = sb("b1rows", [E0, H0])
        score = sb("score", [P, J, E0])
        smax = sb("smax", [P, J])
        hit = sb("hit", [P, J, E0])
        rank = sb("rank", [P, J, E0])
        rmax = sb("rmax", [P, J])
        choice = sb("choice", [P, E0, J])
        total = sb("total", [P, E0 * J])
        run_in = sb("run_in", [P, E0 * J])
        run_ex = sb("run_ex", [P, E0 * J])
        count = sb("count", [P, E0])
        over = sb("over", [P, E0, J])
        nblk = sb("nblk", [P, E0])
        bend = sb("bend", [P, E0])
        bstart = sb("bstart", [P, E0])
        shift = sb("shift", [P, E0])
        place = sb("place", [P, E0, J])
        place2 = sb("place2", [P, E0, J])
        place3 = sb("place3", [P, E0, J])
        slot_f = sb("slot_f", [P, J])
        slot = sb("slot", [P, J], I32)
        past = sb("past", [P, E0])
        bexp = sb("bexp", [P, 1])
        bexp_c = sb("bexp_c", [P, 1])
        bhot = sb("bhot", [P, E0])
        bhotT = sb("bhotT", [E0, P])
        bexpT = sb("bexpT", [1, P], I32)
        b1all = sb("b1all", [P, P, HC])
        w1b = space_c[:, 0:4 * H0].rearrange("p (s n) -> p s n", s=4)
        w2b = space_c[:, 4 * H0:8 * H0].rearrange("p (s k n) -> p s k n", s=4, k=HC)
        b2rows = sb("b2rows", [E0, C])
        bsel = sb("bsel", [E0, 2, P])
        xb = sb("xb", [P, 4, C + 1])
        ids = sb("ids", [P, NB0], I32)
        xTb = sb("xTb", [P, 2, P])
        b1b = sb("b1b", [P, 2, HC])
        hb = space_d[:, 0:2 * H0].rearrange("p (u n) -> p u n", u=2)
        yb = sb("yb", [P, 4, C])
        yg = z
        xsort = nc.dram_tensor("xsort", (NB0 * P, C + 1), F32).ap()
        ytok = nc.dram_tensor("ytok", (T + NB0 * P, C), F32).ap()

        def block_of(it, v, back):
            c = 3 + v - back
            return 4 * it + c, c % 4, it + c // 4

        def wait_if(eng, s, value):
            if not isinstance(value, int) or value > 0:
                eng.wait_ge(s, value)


        wrow = sb("wrow", [P, 5, C])
        wqe_vu = sb("wqe_vu", [P, 6 * C])
        wqe = wqe_vu[:, 0:4 * C].rearrange("c (w g h s d) -> c w g h s d", w=2, g=2, h=4, s=2)
        wvu = wqe_vu[:, 4 * C:6 * C]
        v_b = sb("v_b", [P, C])
        ob_b = sb("ob_b", [P, C])
        ob_g = sb("ob_g", [P, C])
        wo1_g = sb("wo1_g", [P, C])
        slope = sb("slope", [P, HEADS])
        decay = sb("decay", [P, HEADS])
        decay_v = sb("decay_v", [P, HEADS, HD])
        decay_h = sb("decay_h", [P, 2, C // 2])
        total_s = sb("total_s", [P, 2, C // 2])
        cmask = wmod[:, :, :].rearrange("p l n -> p (l n)")[:, 0:HEADS * P].rearrange("p (h n) -> p h n", h=HEADS)
        space_e = sb("space_e", [P, 2 * T])
        unused = space_e[:, 0:NB0 * (C + 1)]
        trig = space_e[:, :].rearrange("p (g t) -> p g t", g=2)
        qk = space_a[:, :].rearrange("p (w g t) -> p w g t", w=2, g=2)
        hT3 = hT
        act4 = space_d[:, :].rearrange("p (n c) -> p n c", n=4)
        vpad = space_e[:, 0:J * 4 * 3 * HD].rearrange("p (m q a d) -> p m q a d", m=J, q=4, a=3)
        kt = space_b[:, :].rearrange("p (m g c) -> p m g c", m=J, g=2)
        w3_hi, w3_lo = (space_cr[:, k * 6 * C:(k + 1) * 6 * C] for k in range(2))
        h3_hi, h3_lo = (space_br[:, k * T:(k + 1) * T].rearrange("c (p j) -> c p j", j=J) for k in range(2))
        w3_cut, h3_cut = space_c[:, T:T + 6 * C], space_c[:, T:2 * T].rearrange("c (p j) -> c p j", j=J)
        run = space_c[:, 0:(J + 1) * C].rearrange("p (m g c) -> p m g c", m=J + 1, g=2)
        state = sb("state", [P, J, 2, C // 2])
        space_q = sb("space_q", [P, T])
        qd = space_q[:, :].rearrange("p (u g h n) -> p u g h n", u=2, g=2, h=4)
        sc = space_d[:, :].rearrange("p (u g h n) -> p u g h n", u=2, g=2, h=4)
        msq = sb("msq", [P, J])
        rms = sb("rms", [P, J])
        irms = sb("irms", [P, J])
        ssr = space_c[0:1, 0:T]
        ssq = sb("ssq", [P, J])
        uT = z_id[:, 0:T]
        oT = hTf
        oT2 = space_b[:, 0:T]
        yT = space_b[:, T:2 * T].rearrange("c (p j) -> c p j", j=J)
        turns = state[:, :, :, :].rearrange("p m g c -> p (m g c)")
        part = space_q[:, :]
        pos = turns.bitcast(I32)

        h4T = hTf
        rw = sb("rw", [P, E1])
        rb_b = sb("rb_b", [P, E1])
        b2r = sb("b2r", [E1 + 1, C])
        b2g = sb("b2g", [E1 + 1, C])
        by_expert = lambda k: space_c[:, T + k * J * E1:T + (k + 1) * J * E1].rearrange("p (j e) -> p j e", e=E1)
        logit = by_expert(0)
        lmax = sb("lmax", [P, J])
        ldiff = by_expert(1)
        lexp = by_expert(2)
        lsum = sb("lsum", [P, J])
        lrec = sb("lrec", [P, J])
        prob = by_expert(3)
        pabove = by_expert(4)
        pequal = by_expert(5)
        prun = by_expert(6)
        pnth = by_expert(7)
        pkeep, pick = logit, ldiff
        pcount = sb("pcount", [P, J])
        top8 = space_c[:, T + 8 * J * E1:T + 8 * J * E1 + 8 * J].rearrange("p (j k) -> p j k", k=8)
        restart = sb("restart", [P, J, E1])
        cw = sb("cw", [P, J, E1 + 1])
        cwT = space_c[0:E1 + 1, 0:T].rearrange("e (j p) -> e j p", p=P)
        ew1 = sb("ew1", [P, 2, C])
        ew2 = sb("ew2", [P, 2, C])
        ew2g = sb("ew2g", [P, 2, C])
        ebs = sb("ebs", [P, 2])
        hid = space_b[:, :].rearrange("p (u t) -> p u t", u=2)
        h4_hi, h4_lo = (space_r[:, k * T:(k + 1) * T] for k in range(2))
        ew1_hi, ew1_lo = (space_r[:, 3 * T + 2 * k * C:3 * T + 2 * (k + 1) * C].rearrange("p (u c) -> p u c", u=2) for k in range(2))
        h4_cut, ew1_cut = space_q[:, :], wrow[:, 0:2, :]

        def nth_split(e):
            return e + 1 if isinstance(e, int) and e < 2 else e + 5

        def expert_of(it, v, back):
            c = 2 + v - back
            return 2 * it + c, c % 2, it + c // 2

        ps = ctx.enter_context(nc.psum_tensor("ps", [P, 8, 512], F32))

        (ld_x_0, ld_x_1, got_0, got_1, got_2, got_3, ld_tab, ld_tab2, ld_rows, ld_mod, ld_att, fill_ok, dve_seq, pool_seq, cols_up, cols_ok,
         silu_ok, mod_up, modc_ok, gate_ok, var_ok, std_ok, nmr_ok, zV_ok, zA_ok, hT_up, hT_ok, hT_all,
         q_ok, k_ok, prod_up, prod_ok, v0_up, v0_ok, lagf_up, lagf_ok, lag_up, lag_ok,
         candd_ok, call_up, cnt_ok, cnt_up, g_ok, gprev_up, gx_ok, gh_up, gh_ok, toep_up, gb_ok, aT_up, aT_ok,
         oh_up, oh_ok, attn_up, x_ok, wo_ok, xb_ok, st_out) = (sem(n) for n in """ld_x_0 ld_x_1 got_0 got_1 got_2 got_3 ld_tab ld_tab2 ld_rows
         ld_mod ld_att fill_ok dve_seq pool_seq cols_up cols_ok silu_ok mod_up modc_ok
         gate_ok var_ok std_ok nmr_ok zV_ok zA_ok hT_up hT_ok hT_all q_ok k_ok prod_up prod_ok v0_up v0_ok lagf_up
         lagf_ok lag_up lag_ok candd_ok call_up cnt_ok cnt_up g_ok gprev_up gx_ok gh_up gh_ok toep_up
         gb_ok aT_up aT_ok oh_up oh_ok attn_up x_ok wo_ok xb_ok st_out""".split())

        (ld_moe, pool_zero, score_up, choice_ok, count_up, slot_ok, bexp_ok, bexp_up,
         bhotT_ok, b1all_ok, zfill, id_ok, scattered, xT_up, xT_ok, b1_ok, h_up, hA_ok, hV_ok, y_up,
         y_ok, ld_w1_0, ld_w1_1, ld_w1_2, ld_w1_3, ld_w2_0, ld_w2_1, ld_w2_2, ld_w2_3, ld_xb_0, ld_xb_1, ld_xb_2, ld_xb_3,
         st_y_0, st_y_1, st_y_2, st_y_3) = (sem(n) for n in """
         ld_moe pool_zero score_up choice_ok count_up slot_ok bexp_ok bexp_up bhotT_ok
         b1all_ok zfill id_ok scattered xT_up xT_ok b1_ok h_up hA_ok hV_ok y_up y_ok
         ld_w1_0 ld_w1_1 ld_w1_2 ld_w1_3 ld_w2_0 ld_w2_1 ld_w2_2 ld_w2_3 ld_xb_0 ld_xb_1 ld_xb_2 ld_xb_3 st_y_0 st_y_1 st_y_2 st_y_3""".split())

        (ld_l1w, ld_l1b, ld_rows2, ld_r, wT_up, wT_ok, ang_ok, angP_ok, angV_ok, trig_ok, decay_ok0, decay_ok,
         qk_up, act4_ok, qkV_ok, qkP_ok, u_up, u_ok, v_up, v_ok, vz_ok, kt_up, ktA_ok,
         ktV_ok, st_up, run_ok, total_ok, state_ok, cmask_ok, qz_ok, qdA_ok, qdP_ok, sc_up, sc_ok,
         o_up, oT_ok, oT2_ok, ssr_up, ssr_ok, ssq_in, msq_ok, rms_ok, yT_ok, logit_up,
         ldiff_ok, lexp_ok, cw_ok, cwT_up, cwT_ok, b2g_ok, proj_ok, eu_up, hid_ok, edb_up, accb_ok, ew2g_ok, split_ok,
         ebs_ok, ld_e_0, ld_e_1, ld_e2_0, ld_e2_1) = (sem(n) for n in """
         ld_l1w ld_l1b ld_rows2 ld_r wT_up wT_ok ang_ok angP_ok angV_ok trig_ok decay_ok0 decay_ok
         qk_up act4_ok qkV_ok qkP_ok u_up u_ok v_up v_ok vz_ok kt_up ktA_ok ktV_ok st_up run_ok total_ok state_ok
         cmask_ok qz_ok qdA_ok qdP_ok sc_up sc_ok o_up oT_ok oT2_ok ssr_up ssr_ok ssq_in msq_ok rms_ok yT_ok
         logit_up ldiff_ok lexp_ok cw_ok cwT_up cwT_ok b2g_ok proj_ok eu_up hid_ok
         edb_up accb_ok ew2g_ok split_ok ebs_ok ld_e_0 ld_e_1 ld_e2_0 ld_e2_1""".split())

        block = ctx.enter_context(nc.Block())

        ld_x, got = (ld_x_0, ld_x_1), (got_0, got_1, got_2, got_3)
        ld_e, ld_e2 = (ld_e_0, ld_e_1), (ld_e2_0, ld_e2_1)
        ld_w1, ld_w2 = (ld_w1_0, ld_w1_1, ld_w1_2, ld_w1_3), (ld_w2_0, ld_w2_1, ld_w2_2, ld_w2_3)
        ld_xb, st_y = (ld_xb_0, ld_xb_1, ld_xb_2, ld_xb_3), (st_y_0, st_y_1, st_y_2, st_y_3)

        LN_V = (2, 2, 2, 3)

        def z_ready(eng, n, b):
            eng.wait_ge(zV_ok, sum(LN_V) * (n - 1) + sum(LN_V[:b + 1]))
            eng.wait_ge(zA_ok, (J - sum(LN_V)) * (n - 1) + 4 * (b + 1) - sum(LN_V[:b + 1]))

        phase = tb("phase")

        def whole_turns_off(eng, seq, g, fused):
            ang = trig[:, g, :]
            seq(eng.tensor_scalar(turns, part, ROUND, ROUND, ALU.add, ALU.subtract))
            for piece in TWO_PI:
                if fused:
                    ins = eng.scalar_tensor_tensor(out=ang, in0=turns, scalar=-piece, in1=ang, op0=ALU.mult, op1=ALU.add)
                else:
                    seq(eng.tensor_scalar(part, turns, piece, None, ALU.mult))
                    ins = eng.tensor_tensor(ang, ang, part, ALU.subtract)
                if piece != TWO_PI[-1]:
                    seq(ins)
            return ins

        psq = ps[:, 0:4, :].rearrange("p b (g m) -> p m (b g)", m=P)
        pst = ps[:, 3, :].rearrange("p (m b) -> p m b", m=8)

        def take_prod(copy, i, q):
            return copy(prod[32 * q:32 * q + 32, :, i::4], psq[32 * i:32 * i + 32, 32 * i + q:32 * i + 32:4, :])

        gbv = gb[:, :, :].rearrange("p g (i m q) -> p i q m g", i=4, q=4)

        def take_toep(copy, i, q):
            return copy(gbv[32 * i:32 * i + 32, i, q, :, :], pst[32 * q:32 * q + 32, :, i::4])

        @block.sync
        def _(eng):
            for b in range(2):
                eng.dma_start(x[:, 8 * b:8 * b + 8, :], a["L0_attn_hidden_states"][0].rearrange("(p j) c -> p j c", j=J)[:, 8 * b:8 * b + 8, :]).then_inc(ld_x[b], 16)
            for k, n in enumerate(("Wq", "Wk", "Wv", "Wo")):
                eng.dma_start(wqkvo[:, k, :], a["L0_attn_" + n]).then_inc(ld_att, 16)
            for k, n in enumerate(("bq", "bk", "bv")):
                eng.dma_start(brow[0:1, k, :], a["L0_attn_" + n].rearrange("(a c) -> a c", a=1)).then_inc(ld_att, 16)
            eng.dma_start(bo_b[:, :], a["L0_attn_bo"].partition_broadcast(P)).then_inc(ld_att, 16)
            eng.dma_start(tab[:, NFIRST:], a["table"][:, NFIRST:]).then_inc(ld_tab2, 16)
            eng.dma_start(wrow[:, 0:4, :], a["L1_attn_qkvu_w"].rearrange("(s p) c -> p s c", p=P)).then_inc(ld_l1w, 16)
            eng.dma_start(wrow[:, 4, :], a["L1_attn_out_w"]).then_inc(ld_l1w, 16)
            eng.dma_start(rows[ROW_SB1:ROW_SB1 + 1, :], a["L1_ffn_sb1"].rearrange("(a c) -> a c", a=1)).then_inc(ld_rows2, 16)
            eng.dma_start(rows[ROW_EB1:ROW_EB1 + E1, :], a["L1_ffn_eb1"]).then_inc(ld_rows2, 16)
            eng.dma_start(rows[ROW_UB:ROW_UB + 1, :], a["L1_attn_qkvu_b"][3 * C:4 * C].rearrange("(a c) -> a c", a=1)).then_inc(ld_rows2, 16)
            for at, src in ((ROW_QB, a["L1_attn_qkvu_b"][0:C]), (ROW_KB, a["L1_attn_qkvu_b"][C:2 * C]),
                            (ROW_TH, a["L1_attn_theta"].rearrange("h a d -> (h a d)"))):
                s3 = src.rearrange("(g h d) -> g h d", g=2, h=4)
                for half in range(2):
                    dst = rows[at:at + 2, :].rearrange("g (h s d) -> g h s d", h=4, s=2)[:, :, half, :]
                    eng.dma_start(dst, s3).then_inc(ld_rows2, 16)
            eng.dma_start(wg[:, :], a["L0_ffn_Wg"]).then_inc(ld_moe, 16)
            eng.dma_start(bg_b[:, :], a["L0_ffn_bg"].partition_broadcast(P)).then_inc(ld_moe, 16)
            eng.dma_start(b1rows[:, :], a["L0_ffn_b1"]).then_inc(ld_moe, 16)
            eng.dma_start(b2rows[:, :], a["L0_ffn_b2"]).then_inc(ld_moe, 16)
            eng.wait_ge(pool_zero, 3)
            eng.dma_start(xsort.rearrange("(b p) c -> p b c", p=P), by_token(unused)).then_inc(zfill, 16)
            eng.dma_start(v_b[:, :], a["L1_attn_qkvu_b"][2 * C:3 * C].partition_broadcast(P)).then_inc(ld_l1b, 16)
            eng.dma_start(ob_b[:, :], a["L1_attn_out_b"].partition_broadcast(P)).then_inc(ld_l1b, 16)
            eng.dma_start(slope[:, :], a["L1_attn_slope_rate"].rearrange("h a b -> (h a b)").partition_broadcast(P)).then_inc(ld_l1b, 16)
            eng.dma_start(rw[:, :], a["L1_ffn_router_W"]).then_inc(ld_r, 16)
            eng.dma_start(rb_b[:, :], a["L1_ffn_router_b"].partition_broadcast(P)).then_inc(ld_r, 16)
            eng.dma_start(b2r[1:E1 + 1, :], a["L1_ffn_eb2"]).then_inc(ld_r, 16)
            eng.dma_start(b2r[0:1, :], a["L1_ffn_sb2"].rearrange("(a c) -> a c", a=1)).then_inc(ld_r, 16)

            def expert_id(b):
                return eng.value_load(bexpT[0:1, bass.ds(b, 1)], min_val=0, max_val=E0 - 1)

            def load_w1(b, slot_, rnd):
                e = expert_id(b)
                wait_if(eng, h_up, b - 3)
                eng.dma_start(w1b[:, slot_, :], a["L0_ffn_W1"][bass.ds(e, 1)].rearrange("e p n -> (e p) n")).then_inc(ld_w1[slot_], 16)
                return e

            def load_w2(b, slot_, rnd, e):
                wait_if(eng, y_up, b - 3)
                eng.dma_start(w2b[:, slot_, :, :], a["L0_ffn_W2"][bass.ds(e, 1)].rearrange("e (k p) n -> p (e k) n", p=P)).then_inc(ld_w2[slot_], 16)

            def step(it, v, e, last=False):
                if e is None:
                    e = expert_id(block_of(it, v, -1)[0])
                e2 = None
                if not last or v < 2:
                    e2 = load_w1(*block_of(it, v, -2))
                if not last or v < 3:
                    load_w2(*block_of(it, v, -1), e)
                return e2

            def round_of(it, last=False):
                e = None
                for v in range(4):
                    e = step(it, v, e, last)

            eng.wait_ge(bexp_ok, 2)
            for b in range(4):
                e = load_w1(*block_of(0, b - 3, 0))
                load_w2(*block_of(0, b - 3, 0), e)
            load_w1(*block_of(0, 1, 0))
            round_of(0)
            with eng.Fori(1, (NB0 - 3) // 4 - 1) as it:
                round_of(it)
            round_of((NB0 - 3) // 4 - 1, last=True)
            for k in range(4):
                eng.wait_ge(st_y[k], 16 * ((NB0 - 1 - k) // 4 + 1))
            for b in range(4):
                eng.dma_start(yg[:, 4 * b:4 * b + 4, :], ytok[0:T].rearrange("(p j) c -> p j c", j=J)[:, 4 * b:4 * b + 4, :]).then_inc(got[b], 16)
            def load_e(e, u, rnd):
                shared = isinstance(e, int) and e == 0
                wait_if(eng, ew2g_ok, e - 1)
                eng.dma_start(ew2[:, u, :], a["L1_ffn_sW2"] if shared else
                              a["L1_ffn_eW2"][bass.ds(e - 1, 1)].rearrange("e p n -> (e p) n")).then_inc(ld_e2[u], 16)
                if not isinstance(e, int) or e >= 2:
                    eng.wait_ge(split_ok, 2 * nth_split(e - 2))
                eng.dma_start(ew1[:, u, :], a["L1_ffn_sW1"] if shared else
                              a["L1_ffn_eW1"][bass.ds(e - 1, 1)].rearrange("e p n -> (e p) n")).then_inc(ld_e[u], 16)

            for v in (-2, -1):
                load_e(*expert_of(0, v, 0))
            eng.wait_ge(ssr_ok, 4)
            eng.dma_start(ssq[:, :], ssr[0:1, :].rearrange("a (p j) -> a p j", j=J)).then_inc(ssq_in, 16)
            for v in range(2):
                load_e(*expert_of(0, v, 0))
            with eng.Fori(1, (E1 - 1) // 2) as it:
                for v in range(2):
                    load_e(*expert_of(it, v, 0))
            for b in range(4):
                eng.wait_ge(accb_ok, 4 * E1 + b + 1)
                eng.dma_start(out[0].rearrange("(p j) c -> p j c", j=J)[:, 4 * b:4 * b + 4, :], x[:, 4 * b:4 * b + 4, :]).then_inc(st_out, 16)
            eng.wait_ge(st_out, 4 * 16)

        @block.scalar
        def _(eng):
            eng.dma_start(tab[:, 0:NFIRST], a["table"][:, 0:NFIRST]).then_inc(ld_tab, 16)
            for at, src in ((ROW_C0, a["L0_c"]), (ROW_C1, a["L1_c"])):
                eng.dma_start(rows[at:at + 1, :], src).then_inc(ld_rows, 16)
            for l in range(2):
                eng.dma_start(wmod[:, l, :], a[f"L{l}_wmod"]).then_inc(ld_mod, 16)
            eng.wait_ge(cols_up, 1)
            eng.activation(silu_c[:, :], ps[:, 6, 0:2], ACT.Silu).then_inc(silu_ok, 1)
            eng.wait_ge(silu_ok, 1)
            eng.wait_ge(fill_ok, 1)
            for l in range(2):
                eng.activation(silu_cb[:, l, :], ones[:, :], ACT.Copy, scale=silu_c[:, l:l + 1]).then_inc(silu_ok, 1)

            def layer_norm(n, spread, lag=2):
                for b in range(4 + lag):
                    if b < 4:
                        eng.wait_ge(var_ok, 4 * (n - 1) + b + 1)
                        eng.activation(std[:, 4 * b:4 * b + 4], var_eps[:, 4 * b:4 * b + 4], ACT.Sqrt).then_inc(std_ok, 1)
                    if 1 <= b < 5:
                        eng.wait_ge(nmr_ok, 4 * (n - 1) + b)
                        for j in range(4 * b - 4 + LN_V[b - 1], 4 * b):
                            eng.activation(z[:, j, :], x[:, j, :], ACT.Identity, bias=nmr[:, j:j + 1], scale=rstd[:, j:j + 1]).then_inc(zA_ok, 1)
                    if b >= lag:
                        eng.wait_ge(hT_up, 4 * (n - 1) + b - lag + 1)
                        spread(b - lag).then_inc(hT_ok, 1)

            def scaled(b):
                eng.wait_ge(modc_ok, 1)
                return eng.activation(hT[:, :, 4 * b:4 * b + 4], ps[:, b, :].rearrange("c (j m) -> c m j", m=P), ACT.Copy, scale=modc[:, 0, 1:2])

            layer_norm(1, scaled, lag=4)
            eng.wait_ge(cols_up, 2)
            eng.activation(cols[:, 2:NROWS], ps[:, 6, 2:NROWS], ACT.Copy).then_inc(cols_ok, 1)
            for b in range(4):
                eng.wait_ge(qk_up, b + 1)
                eng.activation(qT[:, 512 * b:512 * b + 512], ps[:, b, :], ACT.Copy).then_inc(q_ok, 1)
            copy = lambda o, i: eng.activation(o, i, ACT.Copy)
            eng.wait_ge(prod_up, 1)
            for i in range(2):
                for q in range(4):
                    take_prod(copy, i, q).then_inc(prod_ok, 1)
            for b in range(4):
                eng.wait_ge(v0_up, b + 1)
                eng.activation(v0[:, 4 * b:4 * b + 4, :], ps[:, 4 + b, :], ACT.Copy).then_inc(v0_ok, 1)
            eng.wait_ge(wT_up, 1)
            for w in range(2):
                for half in range(2):
                    for g in range(2):
                        eng.activation(wqe[:, w, g, :, half, :], ps[:, 4, w * C + 64 * g:w * C + 64 * g + 64].rearrange("c (h d) -> c h d", h=4),
                                       ACT.Copy).then_inc(wT_ok, 1)
            eng.activation(wvu[:, :], ps[:, 4, 2 * C:4 * C], ACT.Copy).then_inc(wT_ok, 1)
            eng.activation(wo1_g[:, :], ps[:, 5, 0:C], ACT.Copy).then_inc(wT_ok, 1)
            eng.wait_ge(ld_tab2, 16)
            eng.wait_ge(fill_ok, 7)
            eng.wait_ge(cols_ok, 1)
            eng.wait_ge(zfill, 16)
            for g in range(2):
                eng.activation(trig[:, g, :], pos, ACT.Copy, scale=cols[:, ROW_TH + g:ROW_TH + g + 1]).then_inc(ang_ok, 1)
            eng.wait_ge(ang_ok, 2)
            eng.activation(part, trig[:, 1, :], ACT.Identity, bias=phase[:, 1:2], scale=INV_2PI).then_inc(ang_ok, 1)
            eng.wait_ge(toep_up, 1)
            eng.wait_ge(fill_ok, 3)
            for i in range(4):
                for q in range(2):
                    take_toep(copy, i, q).then_inc(gb_ok, 1)
            for b in range(0, 4, 2):
                eng.wait_ge(aT_up, b + 1)
                eng.activation(aTf[:, 512 * b:512 * b + 512], ps[:, 4 + b, :], ACT.Copy).then_inc(aT_ok, 1)
            for b in range(0, 4, 2):
                eng.wait_ge(oh_up, b + 1)
                eng.activation(oh[:, 4 * b:4 * b + 4, :], ps[:, b, :], ACT.Copy).then_inc(oh_ok, 1)
            layer_norm(2, lambda b: eng.activation(h2T[:, 512 * b:512 * b + 512], ps[:, b, :], ACT.Identity, bias=modc[:, 0, 2:3],
                                                   scale=modc[:, 0, 3:4]))
            eng.wait_ge(angP_ok, 1)
            eng.activation(trig[:, 1, :], trig[:, 1, :], ACT.Identity, bias=phase[:, 0:1]).then_inc(ang_ok, 1)
            for g in (1, 0):
                eng.wait_ge(angV_ok, 2 - g)
                eng.activation(trig[:, g, :], trig[:, g, :], ACT.Sin).then_inc(trig_ok, 1)

            def relu_a(b, slot_, rnd):
                u = slot_ % 2
                wait_if(eng, h_up, b + 1)
                wait_if(eng, b1_ok, b + 1)
                wait_if(eng, y_up, b - 1)
                for k in range(2):
                    r = eng.activation(hb[:, u, k * P:k * P + P], ps[:, 2 + u, k * P:k * P + P], ACT.Relu, bias=b1b[:, u, k:k + 1])
                r.then_inc(hA_ok, 1)

            def load_x(b, slot_, rnd):
                wait_if(eng, xT_up, b - 3)
                wait_if(eng, id_ok, b - 3)
                eng.dma_start(xb[:, slot_, :], xsort.rearrange("(b p) c -> b p c", p=P)[bass.ds(b, 1)].rearrange("b p c -> (b p) c")).then_inc(ld_xb[slot_], 16)

            eng.wait_ge(scattered, J * 16)
            for b in range(4):
                load_x(*block_of(0, b - 3, 0))
            for v in range(-2, 0):
                relu_a(*block_of(0, v, 1))
            load_x(*block_of(0, 1, 0))

            def round_of(it, last=False):
                for v in range(4):
                    if not last or v < 2:
                        load_x(*block_of(it, v, -2))
                    relu_a(*block_of(it, v, 1))

            round_of(0)
            with eng.Fori(1, (NB0 - 3) // 4 - 1) as it:
                round_of(it)
            round_of((NB0 - 3) // 4 - 1, last=True)
            relu_a(*block_of(0, NB0 - 3, 1))
            eng.wait_ge(ld_l1b, 48)
            eng.activation(decay[:, :], slope[:, :], ACT.Exp).then_inc(decay_ok0, 1)
            layer_norm(3, lambda b: eng.activation(hT3[:, :, 4 * b:4 * b + 4], ps[:, b, :].rearrange("c (j p) -> c p j", p=P), ACT.Identity,
                                                   bias=modc[:, 1, 0:1], scale=modc[:, 1, 1:2]))
            for n in range(16):
                w, g, b = 1 - n // 8, n // 4 % 2, n % 4
                col = (ROW_QB, ROW_KB)[w] + g
                eng.wait_ge(qk_up, 8 + n + 1)
                if n >= 4 and b < 3:
                    eng.wait_ge(qkV_ok, 3 * (n // 4 - 1) + b + 1)
                elif n >= 4:
                    eng.wait_ge(qkP_ok, n // 4)
                eng.activation(act4[:, b, :], ps[:, n % 8, :], ACT.Silu, bias=cols[:, col:col + 1]).then_inc(act4_ok, 1)
            for b in range(4):
                eng.wait_ge(u_up, b + 1)
                eng.activation(uT[:, 512 * b:512 * b + 512], ps[:, b, :], ACT.Identity, bias=cols[:, ROW_UB:ROW_UB + 1]).then_inc(u_ok, 1)
            for n in range(0, 8, 2):
                eng.wait_ge(kt_up, n + 1)
                eng.activation(kt[:, 2 * n:2 * n + 2, :, :], ps[:, n % 4, :], ACT.Copy).then_inc(ktA_ok, 1)
            eng.wait_ge(qz_ok, 1)
            eng.wait_ge(qkV_ok, 12)
            eng.wait_ge(qkP_ok, 4)
            def row_of(b):
                eng.wait_ge(state_ok, 2)
                eng.wait_ge(ssr_up, b + 1)
                eng.activation(ssr[0:1, 512 * b:512 * b + 512], ps[0:1, 6 + b % 2, :], ACT.Copy).then_inc(ssr_ok, 1)

            for m in range(J + 2):
                if m < J:
                    if m >= 2:
                        eng.wait_ge(sc_up, m - 1)
                    for h in range(2):
                        r = eng.activation(qd[32 * h:32 * h + 32, m % 2, :, h, :], qk[32 * h:32 * h + 32, 0, :, m * P:m * P + P], ACT.Copy)
                    r.then_inc(qdA_ok, 1)
                if m % 4 == 1 and m > 4:
                    b = m // 4 - 1
                    eng.wait_ge(o_up, 4 * b + 4)
                    eng.activation(oT[:, 512 * b:512 * b + 512], ps[:, 4 + b % 2, :], ACT.Copy).then_inc(oT_ok, 1)
                    eng.activation(oT2[:, 512 * b:512 * b + 512], ps[:, 4 + b % 2, :], ACT.Square).then_inc(oT2_ok, 1)
                if m % 4 == 0 and m >= 8:
                    row_of(m // 4 - 2)
            row_of(3)
            eng.wait_ge(msq_ok, 1)
            eng.activation(rms[:, :], msq[:, :], ACT.Sqrt).then_inc(rms_ok, 1)
            layer_norm(4, lambda b: eng.activation(h4T[:, 512 * b:512 * b + 512], ps[:, b, :], ACT.Identity, bias=modc[:, 1, 2:3],
                                                   scale=modc[:, 1, 3:4]))
            eng.wait_ge(ldiff_ok, 1)
            eng.activation(lexp[:, :, :], ldiff[:, :, :], ACT.Exp).then_inc(lexp_ok, 1)

            def relu_e(e, u, rnd):
                eng.activation(ebs[:, u:u + 1], cols[:, bass.ds(e + ROW_SB1, 1)], ACT.Copy).then_inc(ebs_ok, 1)
                eng.wait_ge(ebs_ok, e + 1)
                for b in range(4):
                    eng.wait_ge(eu_up, 4 * e + b + 1)
                    if b == 0:
                        wait_if(eng, edb_up, 4 * e - 4)
                    eng.activation(hid[:, u, 512 * b:512 * b + 512], ps[:, b, :], ACT.Relu, bias=ebs[:, u:u + 1]).then_inc(hid_ok, 1)

            for v in (-2, -1, 0, 1):
                relu_e(*expert_of(0, v, 0))
            with eng.Fori(1, (E1 - 1) // 2) as it:
                for v in range(2):
                    relu_e(*expert_of(it, v, 0))

        @block.gpsimd
        def _(eng):
            seq = Chain(eng, pool_seq)
            eng.memset(ones[:, :], 1.0).then_inc(fill_ok, 1)
            eng.memset(unused, 0.0).then_inc(pool_zero, 1)
            eng.memset(ind[:, :], 0.0).then_inc(fill_ok, 1)
            eng.memset(gb[:, :, :], 0.0).then_inc(fill_ok, 1)
            eng.wait_ge(fill_ok, 3)
            eng.memset(ind[:, 0:J], float(P)).then_inc(fill_ok, 1)
            eng.memset(restart[:, :, :], 1.0).then_inc(fill_ok, 1)
            eng.wait_ge(fill_ok, 5)
            eng.memset(restart[:, :, 0:1], 0.0).then_inc(fill_ok, 1)
            eng.iota(by_token(z_id[:, :].bitcast(I32))[:, :, C], pattern=[[1, J]], base=0, channel_multiplier=J).then_inc(pool_zero, 1)
            eng.wait_ge(pool_zero, 1)
            eng.iota(by_token(unused.bitcast(I32))[:, :, C], pattern=[[P, NB0]], base=T, channel_multiplier=1).then_inc(pool_zero, 1)
            eng.iota(pos, pattern=[[1, T]], base=0, channel_multiplier=0).then_inc(fill_ok, 1)
            eng.wait_ge(gate_ok, 1)
            eng.wait_ge(ld_att, 8 * 16)
            eng.tensor_tensor(wo_g[:, :], wqkvo[:, 3, :], gate[:, 0, 0, :], ALU.mult).then_inc(wo_ok, 1)
            seq(eng.tensor_tensor(bo_g[:, :], bo_b[:, :], gate[:, 0, 0, :], ALU.mult))
            z_ready(eng, 1, 3)
            eng.tensor_tensor(x[:, :, :], x[:, :, :], bo_g[:, None, :].to_broadcast([P, J, C]), ALU.add).then_inc(xb_ok, 1)
            eng.wait_ge(ang_ok, 3)
            whole_turns_off(eng, seq, 1, fused=False).then_inc(angP_ok, 1)
            eng.wait_ge(slot_ok, 1)
            eng.wait_ge(pool_zero, 3)
            eng.wait_ge(zfill, 16)
            for j in range(J):
                eng.indirect_dma_start(out=xsort, out_offset=bass.IndirectOffsetOnAxis(ap=slot[:, j:j + 1], axis=0),
                                       in_=by_token(z_id[:, :])[:, j, :], in_offset=None).then_inc(scattered, 16)
            eng.wait_ge(wT_ok, 10)
            eng.tensor_tensor(wo1_g[:, :], wo1_g[:, :], gate[:, 1, 0, :], ALU.mult).then_inc(wo_ok, 1)
            for b in range(NB0 + 3):
                if b < NB0:
                    eng.wait_ge(ld_xb[b % 4], 16 * (b // 4 + 1))
                    eng.tensor_copy(ids[:, b:b + 1], xb[:, b % 4, C:C + 1].bitcast(I32)).then_inc(id_ok, 1)
                if b >= 3:
                    c = b - 3
                    eng.wait_ge(y_ok, c + 1)
                    eng.wait_ge(id_ok, c + 1)
                    eng.indirect_dma_start(out=ytok, out_offset=bass.IndirectOffsetOnAxis(ap=ids[:, c:c + 1], axis=0),
                                           in_=yb[:, c % 4, :], in_offset=None).then_inc(st_y[c % 4], 16)
            seq(eng.tensor_tensor(ob_g[:, :], ob_b[:, :], gate[:, 1, 0, :], ALU.mult))
            eng.wait_ge(angV_ok, 2)
            eng.memset(qd[:, :, :, :, :], 0.0).then_inc(qz_ok, 1)
            eng.wait_ge(decay_ok, 1)
            eng.tensor_tensor(cmask[:, :, :], tb("causal")[:, None, :].to_broadcast([P, HEADS, P]),
                              decay_v[:, :, 0:1].to_broadcast([P, HEADS, P]), ALU.mult).then_inc(cmask_ok, 1)
            eng.wait_ge(trig_ok, 2)
            for n in range(3, 16, 4):
                w, g, b = 1 - n // 8, n // 4 % 2, n % 4
                eng.wait_ge(act4_ok, n + 1)
                eng.tensor_tensor(qk[:, w, g, 512 * b:512 * b + 512], act4[:, b, :], trig[:, g, 512 * b:512 * b + 512], ALU.mult).then_inc(qkP_ok, 1)
            eng.wait_ge(qkP_ok, 4)
            eng.wait_ge(qkV_ok, 12)
            eng.memset(vpad[:, :, :, 1, :], 0.0).then_inc(vz_ok, 1)

            def spread_q(m):
                if m >= 2:
                    eng.wait_ge(sc_up, m - 1)
                for h in range(2, 4):
                    eng.tensor_copy(qd[32 * h:32 * h + 32, m % 2, :, h, :], qk[32 * h:32 * h + 32, 0, :, m * P:m * P + P]).then_inc(qdP_ok, 1)
                    eng.wait_ge(qdP_ok, 2 * m + h - 1)

            eng.wait_ge(vz_ok, 1)
            for m in range(J):
                spread_q(m)
            z_ready(eng, 3, 3)
            eng.tensor_tensor(x[:, :, :], x[:, :, :], ob_g[:, None, :].to_broadcast([P, J, C]), ALU.add).then_inc(xb_ok, 1)
            eng.wait_ge(ld_r, 64)
            eng.tensor_tensor(b2g[:, :], b2r[:, :], gate[0:E1 + 1, 1, 1, :], ALU.mult).then_inc(b2g_ok, 1)

            def gate_w(e, u, rnd):
                wait_if(eng, ld_e2[u], 16 * (rnd + 1))
                wait_if(eng, edb_up, 4 * e - 4)
                eng.tensor_tensor(ew2g[:, u, :], ew2[:, u, :], gate[:, 1, 1, :], ALU.mult).then_inc(ew2g_ok, 1)

            for v in range(-2, E1 - 1):
                gate_w(*expert_of(0, v, 0))

        @block.tensor
        def _(eng):
            eng.wait_ge(ld_tab, 16)
            eng.wait_ge(ld_rows, 2 * 16)
            eng.transpose(ps[:, 6, 0:2], rows[0:2, :], ident[0:2, 0:2]).then_inc(cols_up, 1)
            eng.wait_ge(silu_ok, 1)
            eng.wait_ge(ld_mod, 32)
            for l in range(2):
                for k, part in enumerate((0, 1, 3, 4)):
                    mm = eng.matmul(ps[:, 4, 4 * l + k:4 * l + k + 1], wmod[:, l, part * C:part * C + C],
                                    silu_c[:, l:l + 1], start=True, stop=True)
            mm.then_inc(mod_up, 1)
            for j in range(J):
                z_ready(eng, 1, j // 4)
                mm = eng.matmul(ps[:, j // 4, (j % 4) * P:(j % 4 + 1) * P], z[:, j, :], dft, start=True, stop=True)
                if j % 4 == 3:
                    mm.then_inc(hT_up, 1)
            eng.wait_ge(silu_ok, 3)
            for l in range(2):
                for k, part in enumerate((2, 5)):
                    mm = eng.matmul(ps[:, 5, (2 * l + k) * C:(2 * l + k + 1) * C], silu_cb[:, l, :],
                                    wmod[:, l, part * C:part * C + C], start=True, stop=True)
            mm.then_inc(mod_up, 1)
            eng.wait_ge(ld_rows2, 9 * 16)
            eng.transpose(ps[:, 6, 0:NROWS], rows[:, :], ident[0:NROWS, 0:NROWS]).then_inc(cols_up, 1)
            eng.wait_ge(hT_all, 1)
            eng.wait_ge(ld_att, 8 * 16)
            eng.wait_ge(fill_ok, 4)
            for w, first in ((0, 0), (1, 4)):
                if w == 1:
                    eng.wait_ge(gate_ok, 1)
                    eng.wait_ge(cols_ok, 1)
                for b in range(4):
                    mm = eng.matmul(ps[:, first + b, :], wqkvo[:, w, :], hTf[:, 512 * b:512 * b + 512], start=True, stop=b > 0)
                    if b == 0:
                        mm = eng.matmul(ps[:, first, 0:J], brow[0:1, w, :], ind[0:1, 0:J], start=False, stop=True)
                    mm.then_inc(qk_up, 1)
            for g in range(NG):
                if g % 4 == 0:
                    eng.wait_ge(q_ok, g // 4 + 1)
                    eng.wait_ge(k_ok, g // 4 + 1)
                mm = eng.matmul(ps[:, g // 4, (g % 4) * P:(g % 4 + 1) * P], qT[:, g * P:g * P + P], kT[:, g * P:g * P + P],
                                start=True, stop=True)
            mm.then_inc(prod_up, 1)
            for g in range(NG):
                mm = eng.matmul(ps[:, 4 + g // 4, (g % 4) * P:(g % 4 + 1) * P], hTf[:, g * P:g * P + P], wqkvo[:, 2, :],
                                start=True, stop=g > 0)
                if g == 0:
                    eng.matmul(ps[:, 4, 0:C], ind[0:1, :], brow[0:1, 2, :], start=False, stop=True)
                if g % 4 == 3:
                    mm.then_inc(v0_up, 1)
            eng.wait_ge(ld_tab2, 16)
            eng.wait_ge(prod_ok, 16)
            diag = tb("diag")
            for n in range(8):
                mm = eng.matmul(ps[0:NS, 0, 0:96], prod[:, n, :], diag[:, 96 * n:96 * n + 96], start=n == 0, stop=n == 7)
            mm.then_inc(lagf_up, 1)
            eng.wait_ge(lagf_ok, 1)
            corr = tb("corr")
            for k in range(6):
                half, kind = divmod(k, 3)
                mm = eng.matmul(ps[:, 1, 0:J], corr[:, k * P:k * P + P], lag_f[:, 32 * kind + 16 * half:32 * kind + 16 * half + 16],
                                start=k == 0, stop=k == 5)
            mm.then_inc(lag_up, 1)
            eng.wait_ge(lag_ok, 1)
            eng.transpose(ps[0:J, 2, 0:P], lag[:, :], ident).then_inc(lag_up, 1)
            eng.wait_ge(ld_l1w, 32)
            eng.wait_ge(v0_ok, 4)
            for k in range(4):
                eng.transpose(ps[:, 4, k * C:k * C + C], wrow[:, k, :], ident)
            eng.transpose(ps[:, 5, 0:C], wrow[:, 4, :], ident).then_inc(wT_up, 1)
            eng.wait_ge(candd_ok, 1)
            eng.matmul(ps[:, 3, 0:J * 24], ones[0:J, :], cand_d[:, :, :].rearrange("a b c -> a (b c)"), start=True, stop=True).then_inc(call_up, 1)
            eng.wait_ge(cnt_ok, 1)
            eng.matmul(ps[:, 0, 0:1], ones[:, :], n_above[:, :], start=True, stop=False)
            eng.matmul(ps[:, 0, 0:1], before, eq_run[:, J - 1:J], start=False, stop=True).then_inc(cnt_up, 1)
            eng.wait_ge(g_ok, 1)
            eng.matmul(ps[:, 1, 0:J], prev, gx[:, J:2 * J], start=True, stop=True).then_inc(gprev_up, 1)
            eng.wait_ge(gx_ok, 1)
            gdft, toep = tb("gdft"), tb("toep")
            for k in range(3):
                mm = eng.matmul(ps[32 * k:32 * k + 32, 2, 0:NS], gx[:, :], gdft[:, NS * k:NS * k + NS], start=True, stop=True)
            mm.then_inc(gh_up, 1)
            eng.wait_ge(gh_ok, 1)
            for m in range(8):
                mm = eng.matmul(ps[:, 3, m * NS:m * NS + NS], toep[:, m * P:m * P + P], gh[:, :], start=True, stop=True)
            mm.then_inc(toep_up, 1)
            eng.wait_ge(gb_ok, 16)
            eng.wait_ge(wT_ok, 10)
            for g in range(NG):
                mm = eng.matmul(ps[:, 4 + g // 4, (g % 4) * P:(g % 4 + 1) * P], v0[:, g, :], gb[:, g, :], start=True, stop=True)
                if g % 4 == 3:
                    mm.then_inc(aT_up, 1)
            eng.wait_ge(aT_ok, 4)
            eng.wait_ge(wo_ok, 1)
            for j in range(J):
                mm = eng.matmul(ps[:, j // 4, (j % 4) * P:(j % 4 + 1) * P], aT[:, :, j], wo_g[:, :], start=True, stop=True)
                if j % 4 == 3:
                    mm.then_inc(oh_up, 1)
            eng.wait_ge(oh_ok, 4)
            for b in range(4):
                eng.matmul(ps[:, 4 + b, :], idft, oh[:, 4 * b:4 * b + 4, :], start=True, stop=True).then_inc(attn_up, 1)
            def normalised(n, b):
                z_ready(eng, n, b)
                for j in range(4 * b, 4 * b + 4):
                    mm = eng.transpose(ps[:, b, (j % 4) * P:(j % 4 + 1) * P], z[:, j, :], ident)
                mm.then_inc(hT_up, 1)

            eng.wait_ge(ld_moe, 4 * 16)
            eng.wait_ge(oh_ok, 4)
            for b in range(5):
                if b < 4:
                    normalised(2, b)
                if b >= 1:
                    eng.wait_ge(hT_ok, 4 + b)
                    eng.wait_ge(x_ok, 4)
                    for j in range(4 * b - 4, 4 * b):
                        mm = eng.matmul(ps[:, 4, j * E0:j * E0 + E0], h2T[:, j * P:j * P + P], wg[:, :], start=True, stop=True)
            mm.then_inc(score_up, 1)
            eng.wait_ge(choice_ok, 1)
            ch = choice[:, :, :].rearrange("p e j -> p (e j)")
            eng.matmul(ps[:, 5, 0:P], before, ch, start=True, stop=True)
            eng.matmul(ps[:, 6, 0:P], ones[:, :], ch, start=True, stop=True).then_inc(count_up, 1)
            eng.wait_ge(bexp_ok, 1)
            eng.transpose(ps[0:1, 0, 0:P], bexp_c[:, :], ident)
            eng.transpose(ps[0:E0, 1, 0:P], bhot[:, :], ident).then_inc(bexp_up, 1)
            eng.wait_ge(bhotT_ok, 1)
            for k in range(HC):
                mm = eng.matmul(ps[:, 7, k * P:k * P + P], b1rows[:, k * P:k * P + P], bhotT[:, :], start=True, stop=True)
            mm.then_inc(bexp_up, 1)

            def turn(b, slot_, rnd):
                u = slot_ % 2
                wait_if(eng, ld_xb[slot_], 16 * (rnd + 1))
                wait_if(eng, xT_ok, b - 1)
                eng.transpose(ps[:, u, 0:P], xb[:, slot_, 0:C], ident).then_inc(xT_up, 1)

            def up(b, slot_, rnd):
                u = slot_ % 2
                wait_if(eng, xT_ok, b + 1)
                wait_if(eng, hA_ok, b - 1)
                wait_if(eng, hV_ok, b - 1)
                wait_if(eng, ld_w1[slot_], 16 * (rnd + 1))
                for k in range(HC):
                    mm = eng.matmul(ps[:, (2 if k < 2 else 6) + u, k * P:k * P + P], w1b[:, slot_, k * P:k * P + P], xTb[:, u, :], start=True, stop=True)
                mm.then_inc(h_up, 1)

            def down(b, slot_, rnd):
                u = slot_ % 2
                wait_if(eng, hA_ok, b + 1)
                wait_if(eng, hV_ok, b + 1)
                wait_if(eng, y_ok, b - 1)
                wait_if(eng, ld_w2[slot_], 16 * (rnd + 1))
                for k in range(HC):
                    eng.matmul(ps[:, 4 + u, 0:C], hb[:, u, k * P:k * P + P], w2b[:, slot_, k, :], start=k == 0, stop=False)
                eng.matmul(ps[:, 4 + u, 0:C], bsel[:, u, :], b2rows[:, :], start=False, stop=True).then_inc(y_up, 1)

            eng.wait_ge(b1all_ok, 1)
            turn(*block_of(0, -3, 0))
            turn(*block_of(0, -2, 0))
            up(*block_of(0, -2, 1))
            for v in (-1,):
                turn(*block_of(0, v, 0))
                up(*block_of(0, v, 1))
                down(*block_of(0, v, 2))
            for v in range(4):
                turn(*block_of(0, v, 0))
                up(*block_of(0, v, 1))
                down(*block_of(0, v, 2))
            with eng.Fori(1, (NB0 - 3) // 4) as it:
                for v in range(4):
                    turn(*block_of(it, v, 0))
                    up(*block_of(it, v, 1))
                    down(*block_of(it, v, 2))
            up(*block_of(0, NB0 - 3, 1))
            down(*block_of(0, NB0 - 3, 2))
            down(*block_of(0, NB0 - 2, 2))
            eng.wait_ge(y_ok, NB0)
            for b in range(4):
                normalised(3, b)
            eng.wait_ge(hT_ok, 12)

            def products(o, of):
                for k, (i, j) in enumerate(((0, 0), (0, 1), (1, 0))):
                    mm = eng.matmul(o, of(0, i), of(1, j), start=k == 0, stop=k == 2)
                return mm

            w3 = lambda i, at, width: (w3_hi, w3_lo)[i][:, at:at + width]
            h3 = lambda i, at, width: (h3_hi, h3_lo)[i].rearrange("c p j -> c (p j)")[:, at:at + width]
            for n in range(16):
                w, g, b = 1 - n // 8, n // 4 % 2, n % 4
                if n >= 8:
                    eng.wait_ge(act4_ok, n - 7)
                if n < WHOLE3:
                    mm = eng.matmul(ps[:, n % 8, :], wqe_vu[:, (2 * w + g) * C:(2 * w + g + 1) * C], hTf[:, 512 * b:512 * b + 512],
                                    start=True, stop=True)
                else:
                    if n == WHOLE3:
                        eng.wait_ge(proj_ok, 2 * 5)
                    mm = products(ps[:, n % 8, :], lambda o, i: h3(i, 512 * b, 512) if o else w3(i, (2 * w + g) * C, C))
                mm.then_inc(qk_up, 1)
            for b in range(4):
                eng.wait_ge(act4_ok, 9 + b)
                products(ps[:, b, :], lambda o, i: h3(i, 512 * b, 512) if o else w3(i, 5 * C, C)).then_inc(u_up, 1)
            for b in range(4):
                eng.wait_ge(act4_ok, 13 + b)
                for m in range(4 * b, 4 * b + 4):
                    mm = eng.matmul(ps[:, 4 + b, (m % 4) * C:(m % 4) * C + C], hTf[:, m * P:m * P + P], wvu[:, 0:C], start=True, stop=True)
                mm.then_inc(v_up, 1)
            eng.wait_ge(qkV_ok, 6)
            eng.wait_ge(qkP_ok, 2)
            for n in range(8):
                if n < 4:
                    eng.wait_ge(u_ok, n + 1)
                else:
                    eng.wait_ge((ktA_ok, ktV_ok)[n % 2], (n - 4) // 2 + 1)
                for i in range(4):
                    m, g = 2 * n + i // 2, i % 2
                    mm = eng.transpose(ps[:, n % 4, i * P:i * P + P], qk[:, 1, g, m * P:m * P + P], ident)
                mm.then_inc(kt_up, 1)
            eng.wait_ge(vz_ok, 1)
            for m in range(J):
                n = m // 2
                eng.wait_ge((ktA_ok, ktV_ok)[n % 2], n // 2 + 1)
                eng.wait_ge(v_ok, 8)
                if m >= 4:
                    eng.wait_ge(run_ok, m - 3)
                for g in range(2):
                    mm = eng.matmul(ps[:, 4 + m % 4, 96 * g:96 * g + 96], kt[:, m, g, :],
                                    vpad[:, m, 2 * g:2 * g + 2, :, :].rearrange("p q a d -> p (q a d)"), start=True, stop=True)
                mm.then_inc(st_up, 1)

            def scores(m):
                eng.wait_ge(qdA_ok, m + 1)
                eng.wait_ge(qdP_ok, 2 * m + 2)
                if m >= 2:
                    eng.wait_ge(sc_ok, 2 * m - 2)
                for g in range(2):
                    mm = eng.matmul(ps[:, 2 * (m % 2) + g, :], qk[:, 1, g, m * P:m * P + P], qd[:, m % 2, g, :, :].rearrange("p h n -> p (h n)"),
                                    start=True, stop=True)
                mm.then_inc(sc_up, 1)

            def outputs(m):
                eng.wait_ge(state_ok, 1 if m < J // 2 else 2)
                if m >= 8 and m % 4 == 0:
                    eng.wait_ge(oT2_ok, m // 4 - 1)
                o = ps[:, 4 + m // 4 % 2, (m % 4) * P:(m % 4 + 1) * P]
                for g in range(2):
                    eng.matmul(o[64 * g:64 * g + 64, :], state[:, m, g, :], qk[:, 0, g, m * P:m * P + P], start=True, stop=False,
                               skip_group_check=True)
                for g in range(2):
                    eng.wait_ge(sc_ok, 2 * m + g + 1)
                    for h in range(4):
                        q = 2 * g + h // 2
                        if h % 2 == 0:
                            mm = eng.matmul(o[32 * q:32 * q + HD, :], vpad[:, m, q, 0, :], sc[:, m % 2, g, h, :], start=False, stop=False,
                                            skip_group_check=True)
                        else:
                            mm = eng.matmul(o[32 * q:32 * q + 2 * HD, :], vpad[:, m, q, 1:3, :].rearrange("p a d -> p (a d)"),
                                            sc[:, m % 2, g, h, :], start=False, stop=True, skip_group_check=True)
                mm.then_inc(o_up, 1)

            def squares(b):
                eng.wait_ge(oT2_ok, b + 1)
                if b >= 2:
                    eng.wait_ge(ssr_ok, b - 1)
                eng.matmul(ps[0:1, 6 + b % 2, :], ones[:, 0:1], oT2[:, 512 * b:512 * b + 512], start=True, stop=True).then_inc(ssr_up, 1)

            eng.wait_ge(ktV_ok, 4)
            eng.wait_ge(ktA_ok, 4)
            for m in range(J + 1):
                if m < J:
                    scores(m)
                if m == 1:
                    eng.wait_ge(run_ok, J)
                if m >= 1:
                    outputs(m - 1)
                if m % 4 == 3 and m > 4:
                    squares(m // 4 - 1)
            squares(3)
            eng.wait_ge(yT_ok, 4)
            eng.wait_ge(sc_ok, 2 * J)
            eng.wait_ge(wo_ok, 2)
            for j in range(J):
                mm = eng.matmul(ps[:, j // 4, (j % 4) * P:(j % 4 + 1) * P], yT[:, :, j], wo1_g[:, :], start=True, stop=True)
                if j % 4 == 3:
                    mm.then_inc(attn_up, 1)

            eng.wait_ge(ld_r, 64)
            for b in range(5):
                if b < 4:
                    eng.wait_ge(x_ok, 8 + b + 1)
                    normalised(4, b)
                if b >= 1:
                    eng.wait_ge(hT_ok, 12 + b)
                    for j in range(4 * b - 4, 4 * b):
                        mm = eng.matmul(ps[:, 4, j * E1:j * E1 + E1], h4T[:, j * P:j * P + P], rw[:, :], start=True, stop=True)
            mm.then_inc(logit_up, 1)

            def up_e(e, u, rnd):
                if not isinstance(e, int) or e >= 2:
                    eng.wait_ge(split_ok, 2 * nth_split(e))
                for b in range(4):
                    if isinstance(e, int) and e == 0:
                        eng.wait_ge(split_ok, 2 * (3 + b))
                    wait_if(eng, hid_ok, 4 * e - 3 + b)
                    group = slice(512 * b, 512 * b + 512)
                    for k, (w, h) in enumerate(((ew1_hi, h4_hi), (ew1_hi, h4_lo), (ew1_lo, h4_hi))):
                        mm = eng.matmul(ps[:, b, :], w[:, u, :], h[:, group], start=k == 0, stop=k == 2)
                    mm.then_inc(eu_up, 1)

            def down_e(e, u, rnd):
                eng.wait_ge(ew2g_ok, e + 1)
                for b in range(4):
                    eng.wait_ge(hid_ok, 4 * e + b + 1)
                    wait_if(eng, accb_ok, 4 * e - 3 + b)
                    for j in range(4 * b, 4 * b + 4):
                        mm = eng.matmul(ps[:, 4 + b, (j % 4) * P:(j % 4 + 1) * P], hid[:, u, j * P:j * P + P], ew2g[:, u, :], start=True, stop=True)
                    mm.then_inc(edb_up, 1)

            up_e(*expert_of(0, -2, 0))
            up_e(*expert_of(0, -1, 0))
            eng.wait_ge(cw_ok, 1)
            eng.wait_ge(hid_ok, 8)
            for j in range(J):
                mm = eng.transpose(ps[0:E1 + 1, j // 4, (j % 4) * P:(j % 4 + 1) * P], cw[:, j, :], ident)
                if j % 4 == 3:
                    mm.then_inc(cwT_up, 1)
            eng.wait_ge(ew2g_ok, 1)
            eng.wait_ge(b2g_ok, 1)
            for j in range(J):
                if j % 4 == 0:
                    eng.wait_ge(cwT_ok, j // 4 + 1)
                o = ps[:, 4 + j // 4, (j % 4) * P:(j % 4 + 1) * P]
                eng.matmul(o, hid[:, 0, j * P:j * P + P], ew2g[:, 0, :], start=True, stop=False)
                mm = eng.matmul(o, cwT[:, j, :], b2g[:, :], start=False, stop=True)
                if j % 4 == 3:
                    mm.then_inc(edb_up, 1)
            for v in range(2):
                up_e(*expert_of(0, v, 0))
                down_e(*expert_of(0, v, 1))
            with eng.Fori(1, (E1 - 1) // 2) as it:
                for v in range(2):
                    up_e(*expert_of(it, v, 0))
                    down_e(*expert_of(it, v, 1))
            down_e(*expert_of(0, E1 - 2, 0))

        @block.vector
        def _(eng):
            seq = Chain(eng, dve_seq)

            def split(done, n, hi, lo, cut, full):
                eng.tensor_scalar(cut.bitcast(I32), full.bitcast(I32), HIGH, None, ALU.bitwise_and).then_inc(done, 1)
                eng.wait_ge(done, 2 * n - 1)
                eng.tensor_copy(hi, cut)
                eng.tensor_tensor(lo, full, cut, ALU.subtract).then_inc(done, 1)

            def layer_norm(n, fetch):
                for b in range(5):
                    js, before_ = slice(4 * b, 4 * b + 4), slice(4 * b - 4, 4 * b)
                    if b < 4:
                        arrived, value = fetch(b)
                    if b >= 1:
                        eng.wait_ge(std_ok, 4 * (n - 1) + b)
                        inverted = seq.note(eng.reciprocal(rstd[:, before_], std[:, before_]))
                    if b < 4:
                        eng.wait_ge(arrived, value)
                        for j in range(4 * b, 4 * b + 4):
                            ins = eng.bn_stats(stats[:, j, :], x[:, j, :])
                        stats_done = seq.note(ins)
                    if b >= 1:
                        seq.wait(inverted)
                        eng.scalar_tensor_tensor(out=nmr[:, before_], in0=mv[:, before_, 0], scalar=-1.0, in1=rstd[:, before_], op0=ALU.mult,
                                                 op1=ALU.mult).then_inc(nmr_ok, 1)
                    if b < 4:
                        seq.wait(stats_done)
                        for j in range(4 * b, 4 * b + 4):
                            ins = eng.bn_aggr(mv[:, j, :], stats[:, j, :])
                        mv_done = seq.note(ins)
                    if b >= 1:
                        for j in range(4 * b - 4, 4 * b - 4 + LN_V[b - 1]):
                            eng.tensor_scalar(z[:, j, :], x[:, j, :], mv[:, j, 0:1], rstd[:, j:j + 1], ALU.subtract, ALU.mult).then_inc(zV_ok, 1)
                    if b < 4:
                        seq.wait(mv_done)
                        eng.tensor_scalar(var_eps[:, js], mv[:, js, 1], EPS_LN, None, ALU.add).then_inc(var_ok, 1)

            layer_norm(1, lambda b: (ld_x[b // 2], 16))
            eng.wait_ge(mod_up, 1)
            mc = modc[:, :, :].rearrange("p l k -> p (l k)")
            seq(eng.tensor_copy(mc, ps[:, 4, 0:8]))
            seq(eng.tensor_scalar(mc[:, 1::2], mc[:, 1::2], 1.0, None, ALU.add))
            eng.tensor_scalar(sa128[:, :], modc[:, 0, 0:1], float(P), None, ALU.mult).then_inc(modc_ok, 1)
            eng.wait_ge(hT_ok, 4)
            eng.wait_ge(modc_ok, 1)
            eng.tensor_scalar(hTf[:, 0:J], hTf[:, 0:J], sa128[:, 0:1], None, ALU.add).then_inc(hT_all, 1)
            eng.wait_ge(mod_up, 2)
            g4 = lambda t: t[:, :, :, :].rearrange("p l k c -> p (l k c)")
            seq(eng.tensor_scalar(g4(gsign), ps[:, 5, :], 0.0, 2.0, ALU.is_ge, ALU.mult))
            seq(eng.tensor_scalar(g4(gneg), ps[:, 5, :], -1.0, 0.25, ALU.mult, ALU.max))
            seq(eng.tensor_tensor(g4(gmag), ps[:, 5, :], g4(gneg), ALU.max))
            eng.scalar_tensor_tensor(out=g4(gate), in0=g4(gsign), scalar=-1.0, in1=g4(gmag), op0=ALU.add, op1=ALU.mult).then_inc(gate_ok, 1)
            for b in range(4):
                eng.wait_ge(qk_up, 4 + b + 1)
                eng.tensor_copy(kT[:, 512 * b:512 * b + 512], ps[:, 4 + b, :]).then_inc(k_ok, 1)
            copy = lambda o, i: eng.tensor_copy(o, i)
            eng.wait_ge(prod_up, 1)
            for i in range(2, 4):
                for q in range(4):
                    take_prod(copy, i, q).then_inc(prod_ok, 1)
            eng.wait_ge(lagf_up, 1)
            eng.tensor_copy(lag_f[:, :], ps[0:NS, 0, 0:96]).then_inc(lagf_ok, 1)
            eng.wait_ge(lag_up, 1)
            eng.tensor_copy(lag[:, :], ps[:, 1, 0:J]).then_inc(lag_ok, 1)
            eng.wait_ge(lag_up, 2)
            seq(eng.tensor_copy(lagT[:, :], ps[0:J, 2, 0:P]))

            def largest(dst, src, w1, w2):
                seq(eng.max(dst[:, 0:8], src))
                seq(eng.match_replace(w1, dst[:, 0:8], src, NEG))
                seq(eng.max(dst[:, 8:16], w1))
                seq(eng.match_replace(w2, dst[:, 8:16], w1, NEG))
                seq(eng.max(dst[:, 16:24], w2))

            largest(cand, lagT[:, :], lagW[:, :], lagX[:, :])
            eng.tensor_tensor(cand_d[:, :, :], tb("blk16").rearrange("a (b c) -> a b c", c=24),
                              cand[:, None, :].to_broadcast([J, J, 24]), ALU.mult).then_inc(candd_ok, 1)
            eng.wait_ge(call_up, 1)
            seq(eng.tensor_copy(call[:, :], ps[:, 3, 0:J * 24]))
            largest(best, call[:, :], callW[:, :], callX[:, :])
            thr = best[:, TOPK - 1:TOPK]
            seq(eng.tensor_scalar(above[:, :], lag[:, :], thr, None, ALU.is_gt))
            seq(eng.tensor_scalar(equal[:, :], lag[:, :], thr, None, ALU.is_equal))
            seq(eng.tensor_reduce(n_above[:, :], above[:, :], AX.X, ALU.add))
            eng.tensor_tensor_scan(eq_run[:, :], ones[:, 0:J], equal[:, :], 0.0, ALU.mult, ALU.add).then_inc(cnt_ok, 1)
            eng.wait_ge(cnt_ok, 1)
            eng.wait_ge(cnt_up, 1)
            seq(eng.tensor_copy(n_before[:, :], ps[:, 0, 0:1]))
            seq(eng.tensor_scalar(keep[:, :], eq_run[:, :], n_before[:, 0:1], TOPK + 0.5, ALU.add, ALU.is_le))
            seq(eng.tensor_tensor(keep2[:, :], keep[:, :], equal[:, :], ALU.mult))
            seq(eng.tensor_tensor(keep3[:, :], keep2[:, :], above[:, :], ALU.add))
            eng.tensor_tensor(gx[:, J:2 * J], keep3[:, :], lag[:, :], ALU.mult).then_inc(g_ok, 1)
            eng.wait_ge(gprev_up, 1)
            eng.tensor_copy(gx[:, 0:J], ps[:, 1, 0:J]).then_inc(gx_ok, 1)
            eng.wait_ge(gh_up, 1)
            eng.tensor_copy(gh[:, :], ps[0:96, 2, 0:NS]).then_inc(gh_ok, 1)
            eng.wait_ge(toep_up, 1)
            eng.wait_ge(fill_ok, 3)
            for i in range(4):
                for q in range(2, 4):
                    take_toep(copy, i, q).then_inc(gb_ok, 1)
            for b in range(1, 4, 2):
                eng.wait_ge(aT_up, b + 1)
                eng.tensor_copy(aTf[:, 512 * b:512 * b + 512], ps[:, 4 + b, :]).then_inc(aT_ok, 1)
            for b in range(1, 4, 2):
                eng.wait_ge(oh_up, b + 1)
                eng.tensor_copy(oh[:, 4 * b:4 * b + 4, :], ps[:, b, :]).then_inc(oh_ok, 1)
            eng.wait_ge(xb_ok, 1)

            def add_attention(b):
                eng.wait_ge(attn_up, b + 1)
                eng.tensor_tensor(x[:, 4 * b:4 * b + 4, :], ps[:, 4 + b, :], x[:, 4 * b:4 * b + 4, :], ALU.add).then_inc(x_ok, 1)
                return x_ok, b + 1

            layer_norm(2, add_attention)
            eng.wait_ge(score_up, 1)
            seq(eng.tensor_tensor(score[:, :, :], ps[:, 4, 0:J * E0].rearrange("p (j e) -> p j e", e=E0),
                                  bg_b[:, None, :].to_broadcast([P, J, E0]), ALU.add))
            seq(eng.tensor_reduce(smax[:, :], score[:, :, :], AX.X, ALU.max))
            seq(eng.tensor_tensor(hit[:, :, :], score[:, :, :], smax[:, :, None].to_broadcast([P, J, E0]), ALU.is_equal))
            seq(eng.tensor_tensor(rank[:, :, :], hit[:, :, :], tb("last")[:, None, :].to_broadcast([P, J, E0]), ALU.mult))
            seq(eng.tensor_reduce(rmax[:, :], rank[:, :, :], AX.X, ALU.max))
            eng.tensor_tensor(choice[:, :, :].rearrange("p e j -> p j e"), rank[:, :, :],
                              rmax[:, :, None].to_broadcast([P, J, E0]), ALU.is_equal).then_inc(choice_ok, 1)
            eng.wait_ge(count_up, 1)
            seq(eng.tensor_copy(total[:, :], ps[:, 6, 0:P]))
            seq(eng.tensor_tensor_scan(run_in[:, :], ones[:, 0:E0 * J], total[:, :], 0.0, ALU.mult, ALU.add))
            seq(eng.tensor_tensor(run_ex[:, :], run_in[:, :], total[:, :], ALU.subtract))
            seq(eng.tensor_tensor(count[:, :], run_in[:, J - 1::J], run_ex[:, 0::J], ALU.subtract))
            seq(eng.tensor_tensor(over[:, :, :], count[:, :, None].to_broadcast([P, E0, J]),
                                  tb("steps")[:, None, :].to_broadcast([P, E0, J]), ALU.is_gt))
            seq(eng.tensor_reduce(nblk[:, :], over[:, :, :], AX.X, ALU.add))
            seq(eng.tensor_tensor_scan(bend[:, :], ones[:, 0:E0], nblk[:, :], 0.0, ALU.mult, ALU.add))
            seq(eng.tensor_tensor(bstart[:, :], bend[:, :], nblk[:, :], ALU.subtract))
            seq(eng.scalar_tensor_tensor(out=shift[:, :], in0=bstart[:, :], scalar=float(P), in1=run_ex[:, 0::J],
                                         op0=ALU.mult, op1=ALU.subtract))
            flat = lambda t: t[:, :, :].rearrange("p e j -> p (e j)")
            seq(eng.tensor_tensor(flat(place), ps[:, 5, 0:P], run_ex[:, :], ALU.add))
            seq(eng.tensor_tensor(place2[:, :, :], place[:, :, :], shift[:, :, None].to_broadcast([P, E0, J]), ALU.add))
            seq(eng.tensor_tensor(place3[:, :, :], place2[:, :, :], choice[:, :, :], ALU.mult))
            seq(eng.tensor_reduce(slot_f[:, :], place3[:, :, :].rearrange("p e j -> p j e"), AX.X, ALU.add))
            eng.tensor_copy(slot[:, :], slot_f[:, :]).then_inc(slot_ok, 1)
            seq(eng.tensor_scalar(past[:, :], bend[:, :], tb("pidx")[:, 0:1], None, ALU.is_le))
            seq(eng.tensor_reduce(bexp[:, :], past[:, :], AX.X, ALU.add))
            seq(eng.tensor_scalar(bexp_c[:, :], bexp[:, :], E0 - 1.0, None, ALU.min))
            eng.tensor_scalar(bhot[:, :], tb("eidx"), bexp_c[:, 0:1], None, ALU.is_equal).then_inc(bexp_ok, 1)
            eng.wait_ge(bexp_up, 1)
            eng.tensor_copy(bexpT[:, :], ps[0:1, 0, 0:P]).then_inc(bexp_ok, 1)
            eng.tensor_copy(bhotT[:, :], ps[0:E0, 1, 0:P]).then_inc(bhotT_ok, 1)
            eng.wait_ge(bexp_up, 2)
            eng.tensor_copy(b1all[:, :, :].rearrange("p b k -> p k b"), ps[:, 7, :].rearrange("p (k b) -> p k b", k=HC)).then_inc(b1all_ok, 1)

            eng.wait_ge(ang_ok, 4)
            eng.tensor_scalar(trig[:, 1, :], trig[:, 1, :], PI_IN, -PI_IN, ALU.min, ALU.max).then_inc(angV_ok, 1)
            seq(eng.tensor_scalar(part, trig[:, 0, :], INV_2PI, phase[:, 1:2], ALU.mult, ALU.add))
            seq(whole_turns_off(eng, seq, 0, fused=True))
            seq(eng.tensor_scalar(trig[:, 0, :], trig[:, 0, :], phase[:, 0:1], PI_IN, ALU.add, ALU.min))
            eng.tensor_scalar(trig[:, 0, :], trig[:, 0, :], -PI_IN, None, ALU.max).then_inc(angV_ok, 1)

            def scale_x(b, slot_, rnd):
                u = slot_ % 2
                wait_if(eng, xT_up, b + 1)
                wait_if(eng, h_up, b - 1)
                eng.tensor_scalar(xTb[:, u, :], ps[:, u, 0:P], modc[:, 0, 3:4], modc[:, 0, 2:3], ALU.mult, ALU.add).then_inc(xT_ok, 1)
                wait_if(eng, hA_ok, b - 1)
                wait_if(eng, hV_ok, b - 1)
                eng.tensor_copy(b1b[:, u, :], b1all[:, bass.ds(b, 1), :].rearrange("p b k -> p (b k)")).then_inc(b1_ok, 1)

            def relu_v(b, slot_, rnd):
                u = slot_ % 2
                wait_if(eng, y_up, b - 1)
                eng.tensor_copy(bsel[:, u, :], bhotT[:, bass.ds(b, 1)].to_broadcast([E0, P]))
                wait_if(eng, h_up, b + 1)
                wait_if(eng, b1_ok, b + 1)
                for k in range(2, HC):
                    r = eng.tensor_scalar(hb[:, u, k * P:k * P + P], ps[:, 6 + u, k * P:k * P + P], b1b[:, u, k:k + 1], 0.0, ALU.add, ALU.max)
                r.then_inc(hV_ok, 1)

            def gate_y(b, slot_, rnd):
                u = slot_ % 2
                wait_if(eng, y_up, b + 1)
                wait_if(eng, st_y[slot_], 16 * rnd)
                eng.tensor_tensor(yb[:, slot_, :], ps[:, 4 + u, 0:C], gate[:, 0, 1, :], ALU.mult).then_inc(y_ok, 1)

            eng.wait_ge(b1all_ok, 1)
            scale_x(*block_of(0, -3, 0))
            scale_x(*block_of(0, -2, 0))
            relu_v(*block_of(0, -2, 1))
            for v in (-1,):
                scale_x(*block_of(0, v, 0))
                relu_v(*block_of(0, v, 1))
                gate_y(*block_of(0, v, 2))
            for v in range(4):
                scale_x(*block_of(0, v, 0))
                relu_v(*block_of(0, v, 1))
                gate_y(*block_of(0, v, 2))
            with eng.Fori(1, (NB0 - 3) // 4) as it:
                for v in range(4):
                    scale_x(*block_of(it, v, 0))
                    relu_v(*block_of(it, v, 1))
                    gate_y(*block_of(it, v, 2))
            relu_v(*block_of(0, NB0 - 3, 1))
            gate_y(*block_of(0, NB0 - 3, 2))
            gate_y(*block_of(0, NB0 - 2, 2))
            eng.wait_ge(decay_ok0, 1)
            seq(eng.tensor_scalar(decay_v[:, :, :], decay[:, :, None].to_broadcast([P, HEADS, HD]), -1.0, None, ALU.add))
            hm = tb("head")
            eng.tensor_tensor(decay_h[:, :, :], decay_v[:, :, :].rearrange("p (g h) d -> p g (h d)", g=2), hm[:, None, :].to_broadcast([P, 2, 64]),
                              ALU.mult).then_inc(decay_ok, 1)

            def add_experts(b):
                eng.wait_ge(got[b], 16)
                eng.tensor_tensor(x[:, 4 * b:4 * b + 4, :], x[:, 4 * b:4 * b + 4, :], yg[:, 4 * b:4 * b + 4, :], ALU.add).then_inc(x_ok, 1)
                return x_ok, 4 + b + 1

            eng.wait_ge(wT_ok, 10)
            eng.wait_ge(y_up, NB0)
            split(proj_ok, 1, w3_hi, w3_lo, w3_cut, wqe_vu[:, :])
            layer_norm(3, add_experts)
            for b in range(4):
                eng.wait_ge(hT_ok, 8 + b + 1)
                part_of = lambda t: t[:, :, 4 * b:4 * b + 4]
                split(proj_ok, 2 + b, part_of(h3_hi), part_of(h3_lo), part_of(h3_cut), part_of(hT3))
            eng.wait_ge(trig_ok, 2)
            for n in range(16):
                w, g, b = 1 - n // 8, n // 4 % 2, n % 4
                if b < 3:
                    eng.wait_ge(act4_ok, n + 1)
                    eng.tensor_tensor(qk[:, w, g, 512 * b:512 * b + 512], act4[:, b, :], trig[:, g, 512 * b:512 * b + 512], ALU.mult).then_inc(qkV_ok, 1)
            eng.wait_ge(qkV_ok, 12)
            eng.wait_ge(qkP_ok, 4)
            for b in range(4):
                eng.wait_ge(v_up, b + 1)
                for odd in range(2):
                    pair = lambda t: t.rearrange("p (q a d) -> p q a d", q=4, a=2)[:, :, odd, :]
                    eng.tensor_tensor(vpad[:, 4 * b:4 * b + 4, :, 2 * odd, :],
                                      ps[:, 4 + b, :].rearrange("p (m q a d) -> p m q a d", m=4, q=4, a=2)[:, :, :, odd, :],
                                      pair(v_b[:, :])[:, None, :, :].to_broadcast([P, 4, 4, HD]), ALU.add).then_inc(v_ok, 1)
            for n in range(1, 8, 2):
                eng.wait_ge(kt_up, n + 1)
                eng.tensor_copy(kt[:, 2 * n:2 * n + 2, :, :], ps[:, n % 4, :]).then_inc(ktV_ok, 1)
            seq(eng.memset(run[:, 0, :, :], 0.0))
            for m in range(J):
                eng.wait_ge(st_up, m + 1)
                if m:
                    eng.wait_ge(run_ok, m)
                eng.tensor_tensor(run[:, m + 1, :, :].rearrange("p g (q a d) -> p (g q) a d", q=2, a=2),
                                  ps[:, 4 + m % 4, 0:192].rearrange("p (q a d) -> p q a d", q=4, a=3)[:, :, 0:3:2, :],
                                  run[:, m, :, :].rearrange("p g (q a d) -> p (g q) a d", q=2, a=2), ALU.add).then_inc(run_ok, 1)
            eng.wait_ge(run_ok, J)
            eng.tensor_tensor(total_s[:, :, :], run[:, J, :, :], hm[:, None, :].to_broadcast([P, 2, 64]), ALU.mult).then_inc(total_ok, 1)
            early = run[:, 0:J // 2, :, :].rearrange("p m g c -> p m (g c)")
            seq(eng.tensor_tensor(early, early, decay_h[:, :, :].rearrange("p g c -> p (g c)")[:, None, :].to_broadcast([P, J // 2, C]), ALU.mult))
            eng.wait_ge(total_ok, 1)
            eng.tensor_tensor(state[:, 0:J // 2, :, :].rearrange("p m g c -> p m (g c)"), early,
                              total_s[:, :, :].rearrange("p g c -> p (g c)")[:, None, :].to_broadcast([P, J // 2, C]), ALU.add).then_inc(state_ok, 1)

            late = run[:, J // 2:J, :, :].rearrange("p m g c -> p m (g c)")

            def mask(m):
                eng.wait_ge(sc_up, m + 1)
                if m >= 2:
                    eng.wait_ge(o_up, m - 1)
                for g in range(2):
                    eng.tensor_tensor(sc[:, m % 2, g, :, :], ps[:, 2 * (m % 2) + g, :].rearrange("p (h n) -> p h n", h=4),
                                      cmask[:, 4 * g:4 * g + 4, :], ALU.mult).then_inc(sc_ok, 1)

            eng.wait_ge(cmask_ok, 1)
            for m in range(J + 3):
                if m < J:
                    mask(m)
                if m == 1:
                    late_done = seq.note(eng.tensor_tensor(late, late, decay_h[:, :, :].rearrange("p g c -> p (g c)")[:, None, :]
                                                           .to_broadcast([P, J // 2, C]), ALU.mult))
                if m == 2:
                    seq.wait(late_done)
                    eng.tensor_tensor(state[:, J // 2:J, :, :].rearrange("p m g c -> p m (g c)"), late,
                                      total_s[:, :, :].rearrange("p g c -> p (g c)")[:, None, :].to_broadcast([P, J // 2, C]), ALU.add).then_inc(state_ok, 1)
                if m % 4 == 2 and m > 4:
                    b = m // 4 - 1
                    eng.wait_ge(oT_ok, b + 1)
                    eng.tensor_tensor(yT[:, 32 * b:32 * b + 32, :], oT[:, 512 * b:512 * b + 512], uT[:, 512 * b:512 * b + 512], ALU.mult).then_inc(yT_ok, 1)

            def split_w(e, u, rnd):
                eng.wait_ge(ld_e[u], 16 * (rnd + 1))
                wait_if(eng, eu_up, 4 * e - 4)
                split(split_ok, nth_split(e), ew1_hi[:, u, :], ew1_lo[:, u, :], ew1_cut[:, u, :], ew1[:, u, :])

            eng.wait_ge(o_up, J)
            for v in (-2, -1):
                split_w(*expert_of(0, v, 0))
            eng.wait_ge(ssq_in, 16)
            eng.tensor_scalar(msq[:, :], ssq[:, :], 1.0 / C, EPS_RMS, ALU.mult, ALU.add).then_inc(msq_ok, 1)
            eng.wait_ge(rms_ok, 1)
            seq(eng.reciprocal(irms[:, :], rms[:, :]))
            eng.wait_ge(xb_ok, 2)

            def add_linear_attention(b):
                eng.wait_ge(attn_up, 4 + b + 1)
                for j in range(4 * b, 4 * b + 4):
                    r = eng.scalar_tensor_tensor(out=x[:, j, :], in0=ps[:, b, (j % 4) * P:(j % 4 + 1) * P], scalar=irms[:, j:j + 1], in1=x[:, j, :],
                                                 op0=ALU.mult, op1=ALU.add)
                r.then_inc(x_ok, 1)
                return x_ok, 8 + b + 1

            layer_norm(4, add_linear_attention)
            for b in range(4):
                eng.wait_ge(hT_ok, 12 + b + 1)
                group = slice(512 * b, 512 * b + 512)
                split(split_ok, 3 + b, h4_hi[:, group], h4_lo[:, group], h4_cut[:, group], h4T[:, group])
            eng.wait_ge(logit_up, 1)
            seq(eng.memset(cw[:, :, 0:1], 1.0))
            wide = [P, J, E1]
            seq(eng.tensor_tensor(logit[:, :, :], ps[:, 4, 0:J * E1].rearrange("p (j e) -> p j e", e=E1), rb_b[:, None, :].to_broadcast(wide), ALU.add))
            seq(eng.tensor_reduce(lmax[:, :], logit[:, :, :], AX.X, ALU.max))
            eng.tensor_tensor(ldiff[:, :, :], logit[:, :, :], lmax[:, :, None].to_broadcast(wide), ALU.subtract).then_inc(ldiff_ok, 1)
            eng.wait_ge(lexp_ok, 1)
            seq(eng.tensor_reduce(lsum[:, :], lexp[:, :, :], AX.X, ALU.add))
            seq(eng.reciprocal(lrec[:, :], lsum[:, :]))
            seq(eng.tensor_tensor(prob[:, :, :], lexp[:, :, :], lrec[:, :, None].to_broadcast(wide), ALU.mult))
            for j in range(J):
                ins = eng.max(top8[:, j, :], prob[:, j, :])
            seq(ins)
            third = top8[:, :, TOP1 - 1:TOP1].to_broadcast(wide)
            eng.tensor_tensor(pabove[:, :, :], prob[:, :, :], third, ALU.is_gt)
            seq(eng.tensor_tensor(pequal[:, :, :], prob[:, :, :], third, ALU.is_equal))
            eng.wait_ge(fill_ok, 6)
            by_row = lambda t: t[:, :, :].rearrange("p j e -> p (j e)")
            eng.tensor_tensor_scan(by_row(prun), by_row(restart), by_row(pequal), 0.0, ALU.mult, ALU.add)
            seq(eng.tensor_reduce(pcount[:, :], pabove[:, :, :], AX.X, ALU.add))
            seq(eng.tensor_tensor(pnth[:, :, :], prun[:, :, :], pcount[:, :, None].to_broadcast(wide), ALU.add))
            seq(eng.scalar_tensor_tensor(out=pkeep[:, :, :], in0=pnth[:, :, :], scalar=TOP1 + 0.5, in1=pequal[:, :, :], op0=ALU.is_le, op1=ALU.mult))
            seq(eng.tensor_tensor(pick[:, :, :], pkeep[:, :, :], pabove[:, :, :], ALU.add))
            eng.tensor_tensor(cw[:, :, 1:E1 + 1], pick[:, :, :], prob[:, :, :], ALU.mult).then_inc(cw_ok, 1)
            split_w(*expert_of(0, 0, 0))
            for b in range(4):
                eng.wait_ge(cwT_up, b + 1)
                eng.tensor_copy(cwT[:, 4 * b:4 * b + 4, :], ps[0:E1 + 1, b, :].rearrange("e (j p) -> e j p", p=P)).then_inc(cwT_ok, 1)
            for b in range(4):
                eng.wait_ge(edb_up, b + 1)
                eng.tensor_tensor(x[:, 4 * b:4 * b + 4, :], ps[:, 4 + b, :], x[:, 4 * b:4 * b + 4, :], ALU.add).then_inc(accb_ok, 1)
            eng.wait_ge(accb_ok, 4)

            def add_e(e, u, rnd):
                for b in range(4):
                    eng.wait_ge(edb_up, 4 * e + b + 1)
                    for j in range(4 * b, 4 * b + 4):
                        w = cw[:, j, e:e + 1] if isinstance(e, int) else cw[:, j, bass.ds(e, 1)]
                        r = eng.scalar_tensor_tensor(out=x[:, j, :], in0=ps[:, 4 + b, (j % 4) * P:(j % 4 + 1) * P], scalar=w, in1=x[:, j, :],
                                                     op0=ALU.mult, op1=ALU.add)
                    r.then_inc(accb_ok, 1)
                eng.wait_ge(accb_ok, 4 * e + 4)

            split_w(*expert_of(0, 1, 0))
            add_e(*expert_of(0, 0, 1))
            split_w(*expert_of(1, 0, 0))
            add_e(*expert_of(0, 1, 1))
            with eng.Fori(1, (E1 - 1) // 2 - 1) as it:
                split_w(*expert_of(it, 1, 0))
                add_e(*expert_of(it, 0, 1))
                split_w(*expert_of(it + 1, 0, 0))
                add_e(*expert_of(it, 1, 1))
            last = (E1 - 1) // 2 - 1
            split_w(*expert_of(last, 1, 0))
            for v in range(2):
                add_e(*expert_of(last, v, 1))
            add_e(*expert_of(0, E1 - 2, 0))


OUT = (1, T, C)


def kernel(**inputs):
    import concourse.bacc as bacc
    from concourse.bass_utils import run_bass_kernel_spmd

    nc = bacc.Bacc("TRN2", target_bir_lowering=False, num_devices=1)
    arrays, aps = {}, {}
    for name, v in (*inputs.items(), ("table", TABLE)):
        v = np.ascontiguousarray(v)
        arrays[name] = v
        aps[name] = nc.dram_tensor(name, v.shape, mybir.dt.from_np(v.dtype), kind="ExternalInput").ap()
    out = nc.dram_tensor("out", OUT, F32, kind="ExternalOutput").ap()
    build(nc, aps, out)
    got = run_bass_kernel_spmd(nc, [arrays], core_ids=[0])
    return got.results[0]["out"]
```
